# Optimizing a Trainium2 kernel written in Bass

```python
import numpy as np
import jax
import jax.numpy as jnp

def _softmax(x, axis=-1):
    return jax.nn.softmax(x, axis=axis)

def _gelu(x):
    return jax.nn.gelu(x, approximate=True)

def _silu(x):
    return jax.nn.silu(x)

def _sigmoid(x):
    return jax.nn.sigmoid(x)

def _layernorm(x, axis=-1, eps=1e-05):
    m = jnp.mean(x, axis=axis, keepdims=True)
    v = jnp.var(x, axis=axis, keepdims=True)
    return (x - m) / jnp.sqrt(v + eps)

def _scatter_add(tgt, idx, src, axis=0):
    return tgt.at[idx].add(src)

def _segment_sum(src, seg, n):
    return jax.ops.segment_sum(src, seg, n)
kernel_name = 'mk_decoder_postln_d1_seqx_r4_445c36'

def setup_inputs(seed: int=0):
    np.random.seed(seed)
    _w = jnp.asarray

    def _rec_inputs():
        import jax
        import jax.numpy as jnp
        _rk = jax.random.key(seed)
        x = 7.22e-05 + 1 * jax.random.normal(jax.random.fold_in(_rk, 1), (4, 512, 512), jnp.float32)
        _lenS = 512 - jax.random.randint(jax.random.fold_in(_rk, 7), (4,), 0, max(1, 512 // 4) + 1, jnp.int32)
        _lenS2 = 512 - jax.random.randint(jax.random.fold_in(_rk, 8), (4,), 0, max(1, 512 // 4) + 1, jnp.int32)
        _ctx_1024P = jax.random.normal(jax.random.fold_in(_rk, 11), (4, 16, 256), jnp.float32)
        _ctx_1024c = jax.random.dirichlet(jax.random.fold_in(_rk, 511), 0.3 * jnp.ones((16,), jnp.float32), (4, 512))
        _ctx_1024t = jnp.einsum('bsk,bkd->bsd', _ctx_1024c, _ctx_1024P)
        _ctx_1024t = _ctx_1024t * jax.lax.rsqrt(jnp.mean(jnp.square(_ctx_1024t)) + 1e-12) * 0.953939
        ctx_1024 = 2.81802e-05 + 1.00001 * (_ctx_1024t + 0.3 * jax.random.normal(jax.random.fold_in(_rk, 611), (4, 512, 256), jnp.float32))
        return (x, ctx_1024)
    x, ctx_1024 = _rec_inputs()

    def _L0_attn_setup():
        import jax, jax.numpy as jnp
        import numpy as np
        EPS = 1e-05
        CHUNK = 128

        def lightning_attn(q, k, v, ld, chunk=CHUNK):
            b, n, h, d = q.shape
            nc = n // chunk
            idx = jnp.arange(chunk)
            diff = idx[:, None] - idx[None, :]
            mask = diff >= 0
            D = jnp.exp(ld[:, None, None] * jnp.where(mask, diff, 0)) * mask
            q_decay = jnp.exp(ld[None, :] * (idx + 1)[:, None])
            k_decay = jnp.exp(ld[None, :] * (chunk - 1 - idx)[:, None])
            chunk_decay = jnp.exp(ld * chunk)
            qc = jnp.moveaxis(q.reshape(b, nc, chunk, h, d), 1, 0)
            kc = jnp.moveaxis(k.reshape(b, nc, chunk, h, d), 1, 0)
            vc = jnp.moveaxis(v.reshape(b, nc, chunk, h, d), 1, 0)

            def step(S, inp):
                qb, kb, vb = inp
                scores = jnp.einsum('bchd,bshd->bhcs', qb, kb) * D[None]
                o_intra = jnp.einsum('bhcs,bshd->bchd', scores, vb)
                o_inter = jnp.einsum('bchd,bhde->bche', qb, S) * q_decay[None, :, :, None]
                S_new = chunk_decay[None, :, None, None] * S + jnp.einsum('bshd,bshe->bhde', kb * k_decay[None, :, :, None], vb)
                return (S_new, o_intra + o_inter)
            S0 = jnp.zeros((b, h, d, d), dtype=q.dtype)
            S_final, oc = jax.lax.scan(step, S0, (qc, kc, vc))
            out = jnp.moveaxis(oc, 0, 1).reshape(b, n, h, d)
            return (out, S_final)

        def group_rmsnorm_fused_gate(o, gate, w, num_heads):
            b, n, d = o.shape
            hd = d // num_heads
            o = o * jax.nn.sigmoid(gate)
            og = o.reshape(b, n, num_heads, hd)
            og = og * jax.lax.rsqrt(jnp.mean(og * og, axis=-1, keepdims=True) + EPS)
            return og.reshape(b, n, d) * w
        key = jax.random.key(seed)
        ks = jax.random.split(key, 10)
        B, N, D, H = (2, 1024, 512, 16)
        HD = D // H
        s = 1.0 / np.sqrt(D)
        x = jax.random.normal(ks[0], (B, N, D), dtype=jnp.float32)
        log_decay = -jax.random.uniform(ks[1], (H,), dtype=jnp.float32, minval=0.01, maxval=1.0)
        Wq = jax.random.normal(ks[2], (D, D), dtype=jnp.float32) * s
        Wk = jax.random.normal(ks[3], (D, D), dtype=jnp.float32) * s
        Wv = jax.random.normal(ks[4], (D, D), dtype=jnp.float32) * s
        Wo = jax.random.normal(ks[5], (D, D), dtype=jnp.float32) * s
        Wg1 = jax.random.normal(ks[6], (D, HD), dtype=jnp.float32) * s
        Wg2 = jax.random.normal(ks[7], (HD, D), dtype=jnp.float32) / np.sqrt(HD)
        norm_w = jnp.ones((D,), dtype=jnp.float32)
        return {'x': x, 'log_decay': log_decay, 'Wq': Wq, 'Wk': Wk, 'Wv': Wv, 'Wo': Wo, 'Wg1': Wg1, 'Wg2': Wg2, 'norm_w': norm_w}
    _L0_attn_all = _L0_attn_setup()
    _L0_attn_in = {k: v for k, v in _L0_attn_all.items() if k in ('log_decay', 'Wq', 'Wk', 'Wv', 'Wo', 'Wg1', 'Wg2', 'norm_w')}
    del _L0_attn_all

    def _L0_xattn_setup():
        import jax, jax.numpy as jnp
        import numpy as np
        key = jax.random.key(seed)
        ks = jax.random.split(key, 6)
        B, L, N, C, D = (8, 128, 512, 256, 128)
        return {'teacher_logits': jax.random.normal(ks[0], (B, L, N), dtype=jnp.float32), 'teacher_features': jax.random.normal(ks[1], (B, N, C), dtype=jnp.float32), 'Wq': jax.random.normal(ks[2], (D, C), dtype=jnp.float32) * (1.0 / np.sqrt(C)), 'bq': jnp.zeros((D,), dtype=jnp.float32), 'Wk': jax.random.normal(ks[3], (D, C), dtype=jnp.float32) * (1.0 / np.sqrt(C)), 'bk': jnp.zeros((D,), dtype=jnp.float32)}
    _L0_xattn_all = _L0_xattn_setup()
    _L0_xattn_in = {k: v for k, v in _L0_xattn_all.items() if k in ('Wq', 'bq', 'Wk', 'bk')}
    del _L0_xattn_all

    def _L0_ffn_setup():
        import jax, jax.numpy as jnp
        import numpy as np
        B, S, H, I = (1, 64, 512, 1536)

        def _quantized_matmul(x, w, scale):
            wq = w.astype(jnp.float8_e4m3fn).astype(x.dtype)
            y = jnp.einsum('bsi,io->bso', x, wq)
            return y * scale
        key = jax.random.key(seed)
        ks = jax.random.split(key, 7)
        return {'x': jax.random.normal(ks[0], (B, S, H), dtype=jnp.float32), 'gate_w': jax.random.normal(ks[1], (H, I), dtype=jnp.float32) * 0.02, 'up_w': jax.random.normal(ks[2], (H, I), dtype=jnp.float32) * 0.02, 'down_w': jax.random.normal(ks[3], (I, H), dtype=jnp.float32) * 0.02, 'gate_scale': jax.random.uniform(ks[4], (I,), dtype=jnp.float32, minval=0.5, maxval=1.5), 'up_scale': jax.random.uniform(ks[5], (I,), dtype=jnp.float32, minval=0.5, maxval=1.5), 'down_scale': jax.random.uniform(ks[6], (H,), dtype=jnp.float32, minval=0.5, maxval=1.5)}
    _L0_ffn_all = _L0_ffn_setup()
    _L0_ffn_in = {k: v for k, v in _L0_ffn_all.items() if k in ('gate_w', 'up_w', 'down_w', 'gate_scale', 'up_scale', 'down_scale')}
    del _L0_ffn_all
    return {'x': x, 'ctx_1024': ctx_1024, 'L0_attn_log_decay': _L0_attn_in['log_decay'], 'L0_attn_Wq': _L0_attn_in['Wq'], 'L0_attn_Wk': _L0_attn_in['Wk'], 'L0_attn_Wv': _L0_attn_in['Wv'], 'L0_attn_Wo': _L0_attn_in['Wo'], 'L0_attn_Wg1': _L0_attn_in['Wg1'], 'L0_attn_Wg2': _L0_attn_in['Wg2'], 'L0_attn_norm_w': _L0_attn_in['norm_w'], 'L0_xattn_Wq': _L0_xattn_in['Wq'], 'L0_xattn_bq': _L0_xattn_in['bq'], 'L0_xattn_Wk': _L0_xattn_in['Wk'], 'L0_xattn_bk': _L0_xattn_in['bk'], 'L0_ffn_gate_w': _L0_ffn_in['gate_w'], 'L0_ffn_up_w': _L0_ffn_in['up_w'], 'L0_ffn_down_w': _L0_ffn_in['down_w'], 'L0_ffn_gate_scale': _L0_ffn_in['gate_scale'], 'L0_ffn_up_scale': _L0_ffn_in['up_scale'], 'L0_ffn_down_scale': _L0_ffn_in['down_scale']}

def reference(x, ctx_1024, L0_attn_log_decay, L0_attn_Wq, L0_attn_Wk, L0_attn_Wv, L0_attn_Wo, L0_attn_Wg1, L0_attn_Wg2, L0_attn_norm_w, L0_xattn_Wq, L0_xattn_bq, L0_xattn_Wk, L0_xattn_bk, L0_ffn_gate_w, L0_ffn_up_w, L0_ffn_down_w, L0_ffn_gate_scale, L0_ffn_up_scale, L0_ffn_down_scale):
    import jax
    import jax.numpy as jnp

    def _L0_attn_ref(x, log_decay, Wq, Wk, Wv, Wo, Wg1, Wg2, norm_w):
        import jax, jax.numpy as jnp
        import numpy as np
        EPS = 1e-05
        CHUNK = 128

        def lightning_attn(q, k, v, ld, chunk=CHUNK):
            b, n, h, d = q.shape
            nc = n // chunk
            idx = jnp.arange(chunk)
            diff = idx[:, None] - idx[None, :]
            mask = diff >= 0
            D = jnp.exp(ld[:, None, None] * jnp.where(mask, diff, 0)) * mask
            q_decay = jnp.exp(ld[None, :] * (idx + 1)[:, None])
            k_decay = jnp.exp(ld[None, :] * (chunk - 1 - idx)[:, None])
            chunk_decay = jnp.exp(ld * chunk)
            qc = jnp.moveaxis(q.reshape(b, nc, chunk, h, d), 1, 0)
            kc = jnp.moveaxis(k.reshape(b, nc, chunk, h, d), 1, 0)
            vc = jnp.moveaxis(v.reshape(b, nc, chunk, h, d), 1, 0)

            def step(S, inp):
                qb, kb, vb = inp
                scores = jnp.einsum('bchd,bshd->bhcs', qb, kb) * D[None]
                o_intra = jnp.einsum('bhcs,bshd->bchd', scores, vb)
                o_inter = jnp.einsum('bchd,bhde->bche', qb, S) * q_decay[None, :, :, None]
                S_new = chunk_decay[None, :, None, None] * S + jnp.einsum('bshd,bshe->bhde', kb * k_decay[None, :, :, None], vb)
                return (S_new, o_intra + o_inter)
            S0 = jnp.zeros((b, h, d, d), dtype=q.dtype)
            S_final, oc = jax.lax.scan(step, S0, (qc, kc, vc))
            out = jnp.moveaxis(oc, 0, 1).reshape(b, n, h, d)
            return (out, S_final)

        def group_rmsnorm_fused_gate(o, gate, w, num_heads):
            b, n, d = o.shape
            hd = d // num_heads
            o = o * jax.nn.sigmoid(gate)
            og = o.reshape(b, n, num_heads, hd)
            og = og * jax.lax.rsqrt(jnp.mean(og * og, axis=-1, keepdims=True) + EPS)
            return og.reshape(b, n, d) * w
        b, n, d = x.shape
        H = log_decay.shape[0]
        hd = d // H
        q = jax.nn.silu(jnp.einsum('bnd,de->bne', x, Wq).reshape(b, n, H, hd))
        k = jax.nn.silu(jnp.einsum('bnd,de->bne', x, Wk).reshape(b, n, H, hd))
        v = jax.nn.silu(jnp.einsum('bnd,de->bne', x, Wv).reshape(b, n, H, hd))
        o, _ = lightning_attn(q, k, v, log_decay)
        o = o.reshape(b, n, d)
        gate = jnp.einsum('bnk,kd->bnd', jnp.einsum('bnd,dk->bnk', x, Wg1), Wg2)
        o = group_rmsnorm_fused_gate(o, gate, norm_w, H)
        return jnp.einsum('bnd,de->bne', o, Wo)

    def _L0_xattn_ref(teacher_logits, teacher_features, Wq, bq, Wk, bk):
        import jax, jax.numpy as jnp
        import numpy as np
        query = jnp.einsum('bnc,dc->bnd', teacher_features, Wq) + bq
        key = jnp.einsum('bnc,dc->bnd', teacher_features, Wk) + bk
        energy = jnp.einsum('bnd,bmd->bnm', query, key)
        attention = jax.nn.softmax(energy, axis=-1)
        x_m = jnp.einsum('bln,bmn->blm', teacher_logits, attention)
        return x_m

    def _L0_ffn_ref(x, gate_w, up_w, down_w, gate_scale, up_scale, down_scale):
        import jax, jax.numpy as jnp
        import numpy as np
        B, S, H, I = (1, 64, 512, 1536)

        def _quantized_matmul(x, w, scale):
            wq = w.astype(jnp.float8_e4m3fn).astype(x.dtype)
            y = jnp.einsum('bsi,io->bso', x, wq)
            return y * scale
        gate = jax.nn.silu(_quantized_matmul(x, gate_w, gate_scale))
        up = _quantized_matmul(x, up_w, up_scale)
        fuse = gate * up
        return _quantized_matmul(fuse, down_w, down_scale)
    x = _layernorm(x + _L0_attn_ref(x, L0_attn_log_decay, L0_attn_Wq, L0_attn_Wk, L0_attn_Wv, L0_attn_Wo, L0_attn_Wg1, L0_attn_Wg2, L0_attn_norm_w), axis=-1)
    x = _layernorm(x + _L0_xattn_ref(x, ctx_1024, L0_xattn_Wq, L0_xattn_bq, L0_xattn_Wk, L0_xattn_bk), axis=-1)
    x = _layernorm(x + _L0_ffn_ref(x, L0_ffn_gate_w, L0_ffn_up_w, L0_ffn_down_w, L0_ffn_gate_scale, L0_ffn_up_scale, L0_ffn_down_scale), axis=-1)
    return x

_drawn_inputs = setup_inputs


def setup_inputs(seed=0):
    import zlib

    import numpy as np

    out = dict(_drawn_inputs(seed))
    spreads = {'L0_attn_norm_w': (1.0, 0.2), 'L0_xattn_bq': (0.0, 0.1), 'L0_xattn_bk': (0.0, 0.1)}
    factors = {}
    for name, (base, spread) in spreads.items():
        noise = np.random.default_rng([zlib.crc32(name.encode()), seed]).standard_normal(out[name].shape)
        drawn = base * np.exp(spread * noise) if base else spread * noise
        out[name] = jnp.asarray(drawn.astype(out[name].dtype))
    for name, factor in factors.items():
        out[name] = (out[name] * factor).astype(out[name].dtype)
    return out
```

```python
from contextlib import ExitStack

import concourse.bass as bass
from concourse import mybir

F32 = mybir.dt.float32
F32R = mybir.dt.float32r
F16 = mybir.dt.float16
BF16 = mybir.dt.bfloat16
U32 = mybir.dt.uint32
I32 = mybir.dt.int32
ALU = mybir.AluOpType
ACT = mybir.ActivationFunctionType
AX_X = mybir.AxisListType.X

P = 128
B, N, D = 4, 512, 512
H, HD = 16, 32
C = N // P
K = D // P
G = K
J = P // HD
CTX = 256
KC = CTX // P
FF = 1536
FT = FF // P
EPS = 1e-5

X2_SCALE = 1024.0
FUSE_TOP = 2.0 ** 15

GROUP_SCALE = HD * 256.0

PA_USES = 20
B5_USES = 7
XP_USES = 24
PREP = 9


def f32v(ap):
    return ap.bitcast(F32)


def build(nc, x, ctx_in, ld, wq, wk, wv, wo, wg1, wg2, nw, xwq, xbq, xwk, xbk,
          gate_w, up_w, down_w, gate_s, up_s, down_s, out):
    x_t = x.rearrange("b (t p) d -> (b t) p d", p=P)
    out_t = out.rearrange("b (t p) d -> (b t) p d", p=P)
    x1_dram = nc.dram_tensor("x1_scratch", (B * C, P, D), F32, kind="Internal").ap()
    ctx_t = ctx_in.rearrange("b (t p) d -> b p t d", p=P)
    gate_t = gate_w.rearrange("(k p) f -> k p f", p=P)
    up_t = up_w.rearrange("(k p) f -> k p f", p=P)
    down_t = down_w.rearrange("(k p) f -> k p f", p=P)

    with ExitStack() as top:
        def sem(name):
            return top.enter_context(nc.semaphore(name))

        def sb(name, shape, dt=F32, stack=top):
            return stack.enter_context(nc.sbuf_tensor(name, shape, dt))

        bank = [top.enter_context(nc.psum_tensor(f"bank{i}", [P, 512], F32)) for i in range(8)]

        ident = sb("ident", [P, P])
        wgu = sb("wgu", [P, 2, K, FF], F16)
        wdn = sb("wdn", [P, FT, D], BF16)
        neg_half = sb("neg_half", [P, H])
        eps_tile = sb("eps_tile", [P, 1])
        phase1_done = sem("phase1_done")
        setup_done = sem("setup_done")

        with ExitStack() as ph:
            def s1(name, shape, dt=F32):
                return sb(name, shape, dt, ph)

            w_hi = {w: s1(f"{w}_hi", [P, K, D], F32R) for w in ("wq", "wk", "wv", "wo")}
            w_lo = {w: s1(f"{w}_lo", [P, K, D], F32R) for w in ("wq", "wk", "wv", "wo")}
            wg1_hi = s1("wg1_hi", [P, K, P], F32R)
            wg1_lo = s1("wg1_lo", [P, K, P], F32R)
            wg2_st = s1("wg2_st", [P, D], F32R)
            decay = s1("decay", [P, J, G, P])
            qdec = s1("qdec", [P, G, P])
            kdec = s1("kdec", [P, G, P])
            cdec = s1("cdec", [P, G, HD])
            xin = s1("xin", [P, 2, D])
            xres = s1("xres", [P, 2, D])
            xt_hi = s1("xt_hi", [P, K, N], F32R)
            xt_lo = s1("xt_lo", [P, K, N], F32R)
            qt = s1("qt", [P, G, N])
            kt = s1("kt", [P, G, N])
            v = s1("v", [P, C, D])
            g1_st = s1("g1_st", [P, N], F32R)
            qtd = s1("qtd", [P, G, P])
            ktd = s1("ktd", [P, G, P])
            kn = s1("kn", [P, D])
            probs = s1("probs", [P, J, G * P])
            gt = s1("gt", [P, D])
            og = s1("og", [P, 2, D])
            osq = s1("osq", [P, D])
            ot_hi = s1("ot_hi", [P, K, P], F32R)
            ot_lo = s1("ot_lo", [P, K, P], F32R)
            y = s1("y", [P, 2, D])
            state = s1("state", [P, G * HD])
            state_d = s1("state_d", [P, G * HD])
            state_bd = s1("state_bd", [P, G, P])
            blocks_of_4 = s1("blocks_of_4", [P, J, HD])
            ss = s1("ss", [P, H])
            ss_e = s1("ss_e", [P, H])
            eps_group = s1("eps_group", [P, H])
            rs = s1("rs", [P, H])
            bst = s1("bst", [P, 6])
            mv = s1("mv", [P, 2])
            var_e = s1("var_e", [P, 1])
            rstd = s1("rstd", [P, 1])
            raw = s1("raw", [P, 512])
            magic = s1("magic", [P, 512])
            ldb = s1("ldb", [P, H])
            ldp = s1("ldp", [P, G])
            ldn = s1("ldn", [P, G])
            ld127 = s1("ld127", [P, G])
            nw_p = s1("nw_p", [P, K])
            wraw = [t[:] for t in (qt, kt, v, probs)]
            g1raw = og[:, 0, :].rearrange("p (k m) -> p k m", k=K)
            g2raw = y[:, 0, :]
            diff_i = gt[:, 0 * P:1 * P].bitcast(I32)
            diff = gt[:, 1 * P:2 * P]
            ramp_i = gt[:, 2 * P:3 * P].bitcast(I32)
            ramp = gt[:, 3 * P:4 * P]

            w_loaded = [sem(f"w{i}_loaded") for i in range(4)]
            small_loaded = sem("small_loaded")
            g1raw_loaded, g2raw_loaded, ld_loaded = sem("g1raw_loaded"), sem("g2raw_loaded"), sem("ld_loaded")
            const_done, tables_done, masks_exp = sem("const_done"), sem("tables_done"), sem("masks_exp")
            masks_done, ramps_done, wo_scaled, whi_done = sem("masks_done"), sem("ramps_done"), sem("wo_scaled"), sem("whi_done")
            wlo_done = sem("wlo_done")
            ident_zero, blocks_step = sem("ident_zero"), sem("blocks_step")
            ldn_done = sem("ldn_done")

            xin_loaded = [sem(f"xin{i}_loaded") for i in range(2)]
            xres_loaded = [sem(f"xres{i}_loaded") for i in range(2)]
            x1_stored = [sem(f"x1_{i}_stored") for i in range(2)]
            raw_loaded, magic_exp, magic_ready, raw_added, prep_done = (
                sem("raw_loaded"), sem("magic_exp"), sem("magic_ready"), sem("raw_added"), sem("prep_done"))
            pa_ps, pa_done, xth_done, tanh_done, g1h_done = (
                sem("pa_ps"), sem("pa_done"), sem("xth_done"), sem("tanh_done"), sem("g1h_done"))
            ktd_ready, qtd_ready = sem("ktd_ready"), sem("qtd_ready")
            b5_ps, b5_done = sem("b5_ps"), sem("b5_done")
            sc_ps, probs_done, pv_done, og_done = sem("sc_ps"), sem("probs_done"), sem("pv_done"), sem("og_done")
            state_new = sem("state_new")
            state_decayed, sq_ready, ss_ready = sem("state_decayed"), sem("sq_ready"), sem("ss_ready")
            ss_scaled, rs_ready, ogn_ready = sem("ss_scaled"), sem("rs_ready"), sem("ogn_ready")
            ot_ps, oth_done, ot_done, wo_ps, y_done = (
                sem("ot_ps"), sem("oth_done"), sem("ot_done"), sem("wo_ps"), sem("y_done"))
            mv_ready, var_ready, rstd_ready, x1_ready = (
                sem("mv_ready"), sem("var_ready"), sem("rstd_ready"), sem("x1_ready"))

            def pa_result(b, n):
                return PA_USES * (b + 1) + n + 1

            def pa_read(b, n):
                return 2 + PA_USES * b + n + 1

            def prob_slot(g):
                return probs[:, g, :]

            STEPS = C + 4

            with nc.Block() as block:

                @block.sync
                def _(sp):
                    for i, w in enumerate((wq, wk, wv, wo)):
                        sp.dma_start(wraw[i], w.rearrange("(k p) n -> p k n", p=P)).then_inc(w_loaded[i], 16)
                    with sp.Fori(0, B) as b:
                        for t in range(C):
                            if t < 2:
                                sp.wait_ge(pa_ps, PA_USES * b + t + 3)
                            else:
                                sp.wait_ge(pa_ps, pa_result(b, t - 2))
                            sp.dma_start(xin[:, t % 2, :], x_t[b * C + t]).then_inc(xin_loaded[t % 2], 16)

                        def load_raw(r):
                            sp.wait_ge(prep_done, b * PREP + r + 1)
                            if r < 6:
                                src = (gate_t, up_t)[r // 3][b, :, (r % 3) * 512:(r % 3 + 1) * 512]
                            else:
                                src = down_t[b * 3 + (r - 6)]
                            sp.dma_start(raw[:], src).then_inc(raw_loaded, 16)

                        def load_xres(c):
                            sp.wait_ge(y_done, b * C + c + 1)
                            sp.dma_start(xres[:, c % 2, :], x_t[b * C + c]).then_inc(xres_loaded[c % 2], 16)

                        def store_x1(c):
                            sp.wait_ge(x1_ready, b * C + c + 1)
                            sp.dma_start(x1_dram[b * C + c], y[:, c % 2, :]).then_inc(x1_stored[c % 2], 16)

                        for r in range(7):
                            load_raw(r)
                        load_xres(0)
                        load_xres(1)
                        load_raw(7)
                        load_raw(8)
                        for c in range(2, C):
                            load_xres(c)
                            store_x1(c - 2)
                        store_x1(2)
                        store_x1(3)
                    for s in x1_stored:
                        sp.wait_ge(s, 16 + 16 * B * C // 2)
                    sp.sem_inc(phase1_done, 1)

                @block.gpsimd
                def _(pool):
                    pool.sem_inc(prep_done, 1)
                    pool.dma_start(ldb[:], ld.rearrange("(a h) -> a h", a=1).to_broadcast([P, H])
                                   ).then_inc(ld_loaded, 16)
                    for j in range(J):
                        pool.dma_start(ldp[j * HD:(j + 1) * HD, :],
                                       ld.rearrange("(g j) -> j g", j=J)[j:j + 1, :].to_broadcast([HD, G]),
                                       allow_slow_non_contiguous=True).then_inc(ld_loaded, 16)
                    for r in range(4):
                        pool.dma_start(g1raw[:, :, r * HD:(r + 1) * HD], wg1.rearrange("(k p) c -> p k c", p=P)
                                       ).then_inc(g1raw_loaded, 16)
                        pool.dma_start(g2raw[r * HD:(r + 1) * HD, :], wg2).then_inc(g2raw_loaded, 16)
                    pool.dma_start(nw_p[:], nw.rearrange("(k p) -> p k", p=P), allow_slow_non_contiguous=True).then_inc(small_loaded, 16)
                    nc.gpsimd.memset(ident[:], 0.0).then_inc(ident_zero, 1)
                    nc.gpsimd.memset(neg_half[:], -0.5)
                    nc.gpsimd.memset(eps_tile[:], EPS)
                    nc.gpsimd.memset(eps_group[:], EPS * GROUP_SCALE)
                    pool.wait_ge(ident_zero, 1)
                    nc.gpsimd.affine_select(out=ident[:], in_=ident[:], compare_op=ALU.not_equal, fill=1.0,
                                            base=0, pattern=[[-1, P]], channel_multiplier=1).then_inc(const_done, 1)
                    nc.gpsimd.memset(blocks_of_4[:], 1.0).then_inc(blocks_step, 1)
                    pool.wait_ge(blocks_step, 1)
                    nc.gpsimd.affine_select(out=blocks_of_4[:], in_=blocks_of_4[:], compare_op=ALU.is_ge, fill=0.0,
                                            base=0, pattern=[[-HD, J], [0, HD]], channel_multiplier=1
                                            ).then_inc(blocks_step, 1)
                    pool.wait_ge(blocks_step, 2)
                    nc.gpsimd.affine_select(out=blocks_of_4[:], in_=blocks_of_4[:], compare_op=ALU.is_ge, fill=0.0,
                                            base=HD - 1, pattern=[[HD, J], [0, HD]], channel_multiplier=-1
                                            ).then_inc(blocks_step, 1)
                    nc.gpsimd.iota(diff_i, pattern=[[1, P]], base=0, channel_multiplier=-1).then_inc(const_done, 1)
                    nc.gpsimd.iota(ramp_i, pattern=[[1, P]], base=0, channel_multiplier=0).then_inc(const_done, 1)
                    for h in range(H):
                        pool.wait_ge(masks_exp, h + 1)
                        dh = decay[:, h % J, h // J, :]
                        nc.gpsimd.affine_select(out=dh, in_=dh, compare_op=ALU.is_ge,
                                                fill=0.0, base=0, pattern=[[1, P]], channel_multiplier=-1
                                                ).then_inc(masks_done, 1)
                    for i, w in enumerate(("wq", "wk", "wv", "wo")):
                        for k in range(K):
                            pool.wait_ge(whi_done, i * K + k + 1)
                            nc.gpsimd.tensor_tensor(w_lo[w][:, k, :], wraw[i][:, k, :], f32v(w_hi[w][:, k, :]),
                                                    ALU.subtract).then_inc(wlo_done, 1)
                    pool.wait_ge(wlo_done, 4 * K)
                    pool.sem_inc(setup_done, 1)

                    pool.wait_ge(setup_done, 3)
                    with pool.Fori(0, B) as b:
                        def prep(r):
                            pool.wait_ge(magic_ready, b * PREP + r + 1)
                            nc.gpsimd.tensor_tensor(raw[:], raw[:], magic[:], ALU.add).then_inc(raw_added, 1)
                            pool.wait_ge(raw_added, b * PREP + r + 1)
                            if r < 6:
                                dst = wgu[:, r // 3, b, (r % 3) * 512:(r % 3 + 1) * 512]
                            else:
                                dst = wdn[:, b * 3 + (r - 6), :]
                            nc.gpsimd.tensor_tensor(dst, raw[:], magic[:], ALU.subtract).then_inc(prep_done, 1)

                        for r in range(6):
                            prep(r)
                        for s in range(STEPS):
                            c = s
                            if s == 0:
                                pool.wait_ge(pa_done, pa_read(b, 11))
                            if c <= 2:
                                if c >= 1:
                                    pool.wait_ge(b5_ps, b * B5_USES + 2 * (c - 1) + 1)
                                nc.gpsimd.tensor_tensor(ktd[:], kt[:, :, c * P:(c + 1) * P], kdec[:], ALU.mult
                                                        ).then_inc(ktd_ready, 1)
                            if 1 <= c <= 3:
                                if c >= 2:
                                    pool.wait_ge(pv_done, b * 16 + 4 * c)
                                nc.gpsimd.tensor_tensor(qtd[:], qt[:, :, c * P:(c + 1) * P], qdec[:], ALU.mult
                                                        ).then_inc(qtd_ready, 1)
                            c = s - 1
                            if 0 <= c < C:
                                n = b * C + c + 1
                                pool.wait_ge(og_done, 1 + n)
                                nc.gpsimd.tensor_tensor(osq[:], og[:, c % 2, :], og[:, c % 2, :], ALU.mult
                                                        ).then_inc(sq_ready, 1)
                                pool.wait_ge(ss_ready, n)
                                nc.gpsimd.tensor_tensor(ss_e[:], ss[:], eps_group[:], ALU.add).then_inc(ss_scaled, 1)
                                pool.wait_ge(ss_scaled, n)
                                nc.gpsimd.tensor_tensor(rs[:], ss_e[:], neg_half[:], ALU.pow).then_inc(rs_ready, 1)
                                pool.wait_ge(rs_ready, n)
                                o3 = og[:, c % 2, :].rearrange("p (h d) -> p h d", d=HD)
                                nc.gpsimd.tensor_tensor(o3, o3, rs[:].unsqueeze(2).to_broadcast([P, H, HD]),
                                                        ALU.mult).then_inc(ogn_ready, 1)
                            c = s - 3
                            if 0 <= c < C:
                                n = b * C + c + 1
                                pool.wait_ge(mv_ready, n)
                                nc.gpsimd.tensor_tensor(var_e[:], mv[:, 1:2], eps_tile[:], ALU.add
                                                        ).then_inc(var_ready, 1)
                                pool.wait_ge(var_ready, n)
                                nc.gpsimd.tensor_tensor(rstd[:], var_e[:], neg_half[:, 0:1], ALU.pow
                                                        ).then_inc(rstd_ready, 1)
                            if 1 <= s <= 3:
                                prep(5 + s)
                    pool.wait_ge(prep_done, 1 + B * PREP)
                    pool.wait_ge(rstd_ready, B * C)
                    pool.sem_inc(phase1_done, 1)

                @block.scalar
                def _(act):
                    act.sem_inc(b5_done, 1)
                    act.wait_ge(ramps_done, 2)
                    act.wait_ge(ld_loaded, 16 * (1 + J))
                    for h in range(H):
                        nc.scalar.activation(decay[:, h % J, h // J, :], diff, ACT.Exp, scale=ldb[:, h:h + 1]
                                             ).then_inc(masks_exp, 1)
                    act.wait_ge(ldn_done, 2)
                    for g in range(G):
                        nc.scalar.activation(qdec[:, g, :], ramp, ACT.Exp, scale=ldp[:, g:g + 1],
                                             bias=ldp[:, g:g + 1])
                        nc.scalar.activation(kdec[:, g, :], ramp, ACT.Exp, scale=ldn[:, g:g + 1],
                                             bias=ld127[:, g:g + 1])
                    for i, w in enumerate(("wq", "wk", "wv", "wo")):
                        if w == "wo":
                            act.wait_ge(wo_scaled, K)
                        else:
                            act.wait_ge(w_loaded[i], 16)
                        for k in range(K):
                            nc.scalar.activation(w_hi[w][:, k, :], wraw[i][:, k, :], ACT.Copy).then_inc(whi_done, 1)
                    act.wait_ge(g1raw_loaded, 64)
                    nc.scalar.activation(wg1_hi[:], g1raw, ACT.Copy).then_inc(tables_done, 1)
                    act.wait_ge(g2raw_loaded, 64)
                    nc.scalar.activation(wg2_st[:], g2raw, ACT.Copy).then_inc(tables_done, 1)
                    act.wait_ge(tables_done, 2)
                    act.sem_inc(setup_done, 1)

                    act.wait_ge(setup_done, 3)
                    with act.Fori(0, B) as b:
                        for t in range(C):
                            act.wait_ge(pa_ps, pa_result(b, t))
                            nc.scalar.activation(xt_hi[:, :, t * P:(t + 1) * P],
                                                 bank[t % 2][:].rearrange("p (k c) -> p k c", k=K), ACT.Copy
                                                 ).then_inc(xth_done, 1)
                        for n in range(4, 16):
                            act.wait_ge(pa_ps, pa_result(b, n))
                            if n >= 6:
                                act.wait_ge(pa_done, pa_read(b, n - 2))
                            nc.scalar.activation(prob_slot(n % 2), bank[n % 2][:], ACT.Tanh, scale=0.5
                                                 ).then_inc(tanh_done, 1)
                        act.wait_ge(pa_ps, pa_result(b, 16))
                        nc.scalar.activation(g1_st[:], bank[0][:], ACT.Copy).then_inc(g1h_done, 1)
                        for s in range(STEPS):
                            c = s - 1
                            if 0 <= c < C:
                                use = 2 * c + 1 if c < 3 else 6
                                act.wait_ge(b5_ps, b * B5_USES + use + 1)
                                act.wait_ge(og_done, b * C + c + 1)
                                nc.scalar.activation(gt[:], bank[5][:], ACT.Tanh, scale=0.5).then_inc(b5_done, 1)
                            c = s
                            if c <= 2:
                                act.wait_ge(b5_ps, b * B5_USES + 2 * c + 1)
                                nc.scalar.activation(kn[:], bank[5][:], ACT.Copy).then_inc(b5_done, 1)
                            c = s - 2
                            if 0 <= c < C:
                                act.wait_ge(ot_ps, b * C + c + 1)
                                nc.scalar.activation(ot_hi[:], bank[6][:].rearrange("p (k c) -> p k c", k=K), ACT.Copy
                                                     ).then_inc(oth_done, 1)
                    act.wait_ge(oth_done, B * C)
                    act.sem_inc(phase1_done, 1)

                @block.tensor
                def _(pe):
                    pe.sem_inc(pa_ps, PA_USES)
                    pe.wait_ge(setup_done, 3)
                    with pe.Fori(0, B) as b:
                        for t in range(C):
                            pe.wait_ge(xin_loaded[t % 2], 32 * b + 16 * (t // 2 + 1))
                            pe.wait_ge(pa_done, PA_USES * b + t + 1)
                            for k in range(K):
                                mm = nc.tensor.transpose(bank[t % 2][:, k * P:(k + 1) * P],
                                                         xin[:, t % 2, k * P:(k + 1) * P], ident[:])
                            mm.then_inc(pa_ps, 1)
                        pe.wait_ge(pa_done, pa_read(b, 3))
                        for g in range(G):
                            for i, w in enumerate(("wq", "wk")):
                                n = 4 + 2 * g + i
                                pe.wait_ge(pa_done, PA_USES * b + n + 1)
                                for k in range(K):
                                    for q, (wt, xt) in enumerate(((w_hi, xt_hi), (w_hi, xt_lo), (w_lo, xt_hi))):
                                        mm = nc.tensor.matmul(bank[n % 2][:], wt[w][:, k, g * P:(g + 1) * P],
                                                              xt[:, k, :], start=(k + q == 0), stop=(k == K - 1 and q == 2))
                                mm.then_inc(pa_ps, 1)
                        for t in range(C):
                            n = 12 + t
                            pe.wait_ge(pa_done, PA_USES * b + n + 1)
                            for k in range(K):
                                for q, (xt, wt) in enumerate(((xt_hi, w_hi), (xt_hi, w_lo), (xt_lo, w_hi))):
                                    mm = nc.tensor.matmul(bank[n % 2][:], xt[:, k, t * P:(t + 1) * P], wt["wv"][:, k, :],
                                                          start=(k + q == 0), stop=(k == K - 1 and q == 2))
                            mm.then_inc(pa_ps, 1)
                        pe.wait_ge(pa_done, PA_USES * b + 16 + 1)
                        for k in range(K):
                            for q, (wt, xt) in enumerate(((wg1_hi, xt_hi), (wg1_hi, xt_lo), (wg1_lo, xt_hi))):
                                mm = nc.tensor.matmul(bank[0][:], wt[:, k, :], xt[:, k, :],
                                                      start=(k + q == 0), stop=(k == K - 1 and q == 2))
                        mm.then_inc(pa_ps, 1)

                        def scores(c, j):
                            pe.wait_ge(probs_done, b * 16 + c * 4 + j + 1)
                            r = slice(j * HD, (j + 1) * HD)
                            for g in range(G):
                                mm = nc.tensor.matmul(bank[2 + j % 2][:, g * P:(g + 1) * P],
                                                      kt[r, g, c * P:(c + 1) * P], qt[r, g, c * P:(c + 1) * P],
                                                      start=True, stop=True)
                            mm.then_inc(sc_ps, 1)

                        def values(c, j):
                            if j == 0:
                                pe.wait_ge(og_done, b * C + c + 1)
                                if c >= 1:
                                    pe.wait_ge(qtd_ready, b * 3 + c)
                                    pe.wait_ge(pa_done, pa_read(b, 17 + c - 1))
                                    for g in range(G):
                                        nc.tensor.matmul(bank[4][:, g * P:(g + 1) * P], qtd[:, g, :], state_bd[:, g, :],
                                                         start=(g == 0), stop=False, skip_group_check=True)
                            pe.wait_ge(probs_done, 2 + b * 16 + c * 4 + j + 1)
                            for g in range(G):
                                cols = slice((g * J + j) * HD, (g * J + j + 1) * HD)
                                mm = nc.tensor.matmul(bank[4][:, cols], probs[:, j, g * P:(g + 1) * P], v[:, c, cols],
                                                      start=(c == 0 and j + g == 0), stop=(j == J - 1 and g == G - 1),
                                                      skip_group_check=True)
                            mm.then_inc(pv_done, 1)

                        for s in range(STEPS):
                            c = s - 1
                            if 0 <= c < C:
                                if c == 0:
                                    pe.wait_ge(pa_done, pa_read(b, 16))
                                use = 2 * c + 1 if c < 3 else 6
                                pe.wait_ge(b5_done, b * B5_USES + use + 1)
                                nc.tensor.matmul(bank[5][:], g1_st[:, c * P:(c + 1) * P], wg2_st[:],
                                                 start=True, stop=True).then_inc(b5_ps, 1)
                            if s == 0:
                                pe.wait_ge(pa_done, pa_read(b, 15))
                            for j in range(J):
                                if s < C:
                                    scores(s, j)
                                if 0 <= s - 1 < C:
                                    values(s - 1, j)
                            c = s - 1
                            if 0 <= c <= 2:
                                n = 17 + c
                                pe.wait_ge(b5_done, 1 + b * B5_USES + 2 * c + 1)
                                pe.wait_ge(pa_done, PA_USES * b + n + 1)
                                for h in range(H):
                                    g, j = h // J, h % J
                                    cols = slice(h * HD, (h + 1) * HD)
                                    mm = nc.tensor.matmul(bank[n % 2][j * HD:(j + 1) * HD, g * HD:(g + 1) * HD],
                                                          kn[:, cols], v[:, c, cols], start=True, stop=True)
                                mm.then_inc(pa_ps, 1)
                            c = s
                            if c <= 2:
                                pe.wait_ge(ktd_ready, b * 3 + c + 1)
                                pe.wait_ge(b5_done, b * B5_USES + 2 * c + 1)
                                for g in range(G):
                                    mm = nc.tensor.transpose(bank[5][:, g * P:(g + 1) * P], ktd[:, g, :], ident[:])
                                mm.then_inc(b5_ps, 1)
                            c = s - 3
                            if 0 <= c < C:
                                pe.wait_ge(ot_done, 1 + b * C + c + 1)
                                pe.wait_ge(y_done, b * C + c + 2)
                                for k in range(K):
                                    for q, (ot, wt) in enumerate(((ot_hi, w_hi), (ot_hi, w_lo), (ot_lo, w_hi))):
                                        mm = nc.tensor.matmul(bank[7][:], ot[:, k, :], wt["wo"][:, k, :],
                                                              start=(k + q == 0), stop=(k == K - 1 and q == 2))
                                mm.then_inc(wo_ps, 1)
                            c = s - 2
                            if 0 <= c < C:
                                pe.wait_ge(ogn_ready, b * C + c + 1)
                                pe.wait_ge(ot_done, b * C + c + 1)
                                for k in range(K):
                                    mm = nc.tensor.transpose(bank[6][:, k * P:(k + 1) * P],
                                                             og[:, c % 2, k * P:(k + 1) * P], ident[:])
                                mm.then_inc(ot_ps, 1)
                    pe.wait_ge(wo_ps, B * C)
                    pe.sem_inc(phase1_done, 1)

                @block.vector
                def _(dve):
                    dve.sem_inc(pa_done, 2)
                    dve.sem_inc(probs_done, 2)
                    dve.sem_inc(og_done, 1)
                    dve.sem_inc(ot_done, 1)
                    dve.sem_inc(y_done, 2)
                    dve.sem_inc(x1_stored[0], 16)
                    dve.sem_inc(x1_stored[1], 16)
                    dve.wait_ge(const_done, 3)
                    nc.vector.tensor_scalar(diff, diff_i, 0.0, None, ALU.max).then_inc(ramps_done, 1)
                    nc.vector.tensor_copy(ramp, ramp_i).then_inc(ramps_done, 1)
                    dve.wait_ge(ld_loaded, 16 * (1 + J))
                    nc.vector.tensor_scalar(ldn[:], ldp[:], -1.0, None, ALU.mult).then_inc(ldn_done, 1)
                    nc.vector.tensor_scalar(ld127[:], ldp[:], float(P - 1), None, ALU.mult).then_inc(ldn_done, 1)
                    dve.wait_ge(small_loaded, 16)
                    dve.wait_ge(w_loaded[3], 16)
                    for k in range(K):
                        nc.vector.tensor_scalar(wraw[3][:, k, :], wraw[3][:, k, :], nw_p[:, k:k + 1], GROUP_SCALE ** 0.5 / 16,
                                                ALU.mult, ALU.mult).then_inc(wo_scaled, 1)
                    dve.wait_ge(whi_done, 1)
                    nc.vector.tensor_copy(cdec[:], qdec[:, :, P - 1:P].to_broadcast([P, G, HD]))
                    dve.wait_ge(tables_done, 2)
                    nc.vector.tensor_tensor(wg1_lo[:], g1raw, f32v(wg1_hi[:]), ALU.subtract)
                    for r in (2, 3):
                        q = slice(r * HD, (r + 1) * HD)
                        nc.vector.tensor_tensor(wg2_st[q, :], g2raw[q, :], f32v(wg2_st[q, :]), ALU.subtract)
                    dve.wait_ge(masks_done, H)
                    dve.drain().then_inc(setup_done, 1)

                    dve.wait_ge(setup_done, 3)
                    with dve.Fori(0, B) as b:
                        def prep(r):
                            dve.wait_ge(raw_loaded, 16 * (b * PREP + r + 1))
                            nc.vector.tensor_scalar(magic[:].bitcast(U32), raw[:].bitcast(U32), 0x7F800000, None,
                                                    ALU.bitwise_and).then_inc(magic_exp, 1)
                            dve.wait_ge(magic_exp, b * PREP + r + 1)
                            nc.vector.tensor_scalar(magic[:], magic[:], 2.0 ** -6, 1.5 * 2.0 ** 20, ALU.max, ALU.mult
                                                    ).then_inc(magic_ready, 1)

                        for t in range(C):
                            dve.wait_ge(xth_done, b * C + t + 1)
                            sl = (slice(None), slice(None), slice(t * P, (t + 1) * P))
                            nc.vector.tensor_tensor(xt_lo[sl], bank[t % 2][:].rearrange("p (k c) -> p k c", k=K),
                                                    f32v(xt_hi[sl]), ALU.subtract).then_inc(pa_done, 1)
                        for n in range(4, 16):
                            dve.wait_ge(tanh_done, b * 12 + n - 4 + 1)
                            if n < 12:
                                dst = (qt, kt)[n % 2][:, (n - 4) // 2, :]
                            else:
                                dst = v[:, n - 12, :]
                            nc.vector.scalar_tensor_tensor(out=dst, in0=prob_slot(n % 2), scalar=1.0,
                                                           in1=bank[n % 2][:], op0=ALU.add, op1=ALU.mult
                                                           ).then_inc(pa_done, 1)
                            if n % 2 == 1:
                                prep((n - 5) // 2)
                        dve.wait_ge(g1h_done, b + 1)
                        q = slice(HD, 2 * HD)
                        nc.vector.tensor_tensor(g1_st[q, :], bank[0][q, :], f32v(g1_st[q, :]), ALU.subtract)
                        q = slice(3 * HD, 4 * HD)
                        nc.vector.tensor_tensor(g1_st[q, :], bank[0][q, :], f32v(g1_st[q, :]), ALU.subtract
                                                ).then_inc(pa_done, 1)
                        for s in range(STEPS):
                            for j in range(J):
                                if s < C:
                                    dve.wait_ge(sc_ps, b * 16 + s * 4 + j + 1)
                                    if s >= 1:
                                        dve.wait_ge(pv_done, b * 16 + (s - 1) * 4 + j + 1)
                                    nc.vector.tensor_tensor(prob_slot(j), bank[2 + j % 2][:],
                                                            decay[:, j, :, :].rearrange("p g c -> p (g c)"),
                                                            ALU.mult).then_inc(probs_done, 1)
                            c = s - 1
                            if 0 <= c <= 2:
                                n = 17 + c
                                dve.wait_ge(pa_ps, pa_result(b, n))
                                if c == 0:
                                    nc.vector.tensor_copy(state[:], bank[n % 2][:, 0:G * HD]).then_inc(state_new, 1)
                                else:
                                    nc.vector.tensor_tensor(state_d[:], state[:], cdec[:].rearrange("p g e -> p (g e)"),
                                                            ALU.mult).then_inc(state_decayed, 1)
                                    dve.wait_ge(state_decayed, b * 2 + c)
                                    nc.vector.tensor_tensor(state[:], bank[n % 2][:, 0:G * HD], state_d[:], ALU.add
                                                            ).then_inc(state_new, 1)
                                dve.wait_ge(state_new, b * 3 + c + 1)
                                nc.vector.tensor_tensor(
                                    state_bd[:].rearrange("p g (j e) -> p g j e", j=J),
                                    state[:].rearrange("p (g e) -> p g e", g=G).unsqueeze(2).to_broadcast([P, G, J, HD]),
                                    blocks_of_4[:].unsqueeze(1).to_broadcast([P, G, J, HD]), ALU.mult
                                    ).then_inc(pa_done, 1)
                            if 0 <= c < C:
                                use = 2 * c + 1 if c < 3 else 6
                                dve.wait_ge(b5_done, 1 + b * B5_USES + use + 1)
                                dve.wait_ge(pv_done, b * 16 + 4 * c + 4)
                                if c >= 2:
                                    dve.wait_ge(ot_ps, b * C + c - 1)
                                nc.vector.scalar_tensor_tensor(out=og[:, c % 2, :], in0=gt[:], scalar=1.0,
                                                               in1=bank[4][:], op0=ALU.add, op1=ALU.mult
                                                               ).then_inc(og_done, 1)
                                dve.wait_ge(sq_ready, b * C + c + 1)
                                nc.vector.tensor_reduce(ss[:], osq[:].rearrange("p (h d) -> p h d", d=HD), AX_X,
                                                        ALU.add).then_inc(ss_ready, 1)
                            c = s - 2
                            if 0 <= c < C:
                                dve.wait_ge(oth_done, b * C + c + 1)
                                nc.vector.tensor_tensor(ot_lo[:], bank[6][:].rearrange("p (k c) -> p k c", k=K),
                                                        f32v(ot_hi[:]), ALU.subtract).then_inc(ot_done, 1)
                            c = s - 4
                            if 0 <= c < C:
                                dve.wait_ge(rstd_ready, b * C + c + 1)
                                nc.vector.tensor_scalar(y[:, c % 2, :], y[:, c % 2, :], mv[:, 0:1], rstd[:],
                                                        ALU.subtract, ALU.mult).then_inc(x1_ready, 1)
                            c = s - 3
                            if 0 <= c < C:
                                n = b * C + c + 1
                                dve.wait_ge(wo_ps, n)
                                dve.wait_ge(xres_loaded[c % 2], 32 * b + 16 * (c // 2 + 1))
                                dve.wait_ge(x1_stored[c % 2], 32 * b + 16 * (c // 2 + 1))
                                nc.vector.tensor_tensor(y[:, c % 2, :], bank[7][:], xres[:, c % 2, :], ALU.add
                                                        ).then_inc(y_done, 1)
                                dve.wait_ge(y_done, 2 + n)
                                nc.vector.bn_stats(bst[:], y[:, c % 2, :])
                                dve.drain()
                                nc.vector.bn_aggr(mv[:], bst[:]).then_inc(mv_ready, 1)
                            if 1 <= s <= 3:
                                prep(5 + s)
                    dve.wait_ge(x1_ready, B * C)
                    dve.sem_inc(phase1_done, 1)

        phase2(nc, sem, sb, bank, ident, wgu, wdn, neg_half, eps_tile, phase1_done, x1_dram, ctx_t, out_t,
               xwq, xbq, xwk, xbk, gate_s, up_s, down_s)


def phase2(nc, sem, sb, bank, ident, wgu, wdn, neg_half, eps_tile, phase1_done, x1_dram, ctx_t, out_t,
           xwq, xbq, xwk, xbk, gate_s, up_s, down_s):
    with ExitStack() as ph:
        def s2(name, shape, dt=F32):
            return sb(name, shape, dt, ph)

        xw_raw = s2("xw_raw", [P, 2, CTX])
        xw_hi = s2("xw_hi", [P, 2, KC, P], F32R)
        xw_lo = s2("xw_lo", [P, 2, KC, P], F32R)
        xb = s2("xb", [P, 2])
        gs, us = s2("gs", [P, FT]), s2("us", [P, FT])
        tanh_scale, fuse_scale, back = s2("tanh_scale", [P, FT]), s2("fuse_scale", [P, FT]), s2("back", [P, FT])
        sc = s2("sc", [P, 6, FT])
        norms = s2("norms", [P, 2 * FT])
        half = s2("half", [P, FT])
        ones = s2("ones", [P, 1], BF16)
        one = s2("one", [P, 1])
        sq = s2("sq", [P, 2, 512], BF16)
        down_b = s2("down_b", [P, D])

        cn = s2("cn", [P, C, CTX])
        ct_hi, ct_lo = s2("ct_hi", [P, KC, N], F32R), s2("ct_lo", [P, KC, N], F32R)
        qk_hi, qk_lo = s2("qk_hi", [P, 2, N], F32R), s2("qk_lo", [P, 2, N], F32R)
        x1n = s2("x1n", [P, C, D])
        x1t_hi, x1t_lo = s2("x1t_hi", [P, K, N], F32R), s2("x1t_lo", [P, K, N], F32R)
        att = s2("att", [P, C, N])
        att_hi, att_lo = s2("att_hi", [P, K, N], F32R), s2("att_lo", [P, K, N], F32R)
        nmax, esum, einv = s2("nmax", [P, C]), s2("esum", [P, C]), s2("einv", [P, C])
        x2n, x2k = s2("x2n", [P, C, D]), s2("x2k", [P, C, D])
        x2t_hi, x2t_lo = s2("x2t_hi", [P, K, N], F16), s2("x2t_lo", [P, K, N], F16)
        th, tu, fu = s2("th", [P, 2, N]), s2("tu", [P, 2, N]), s2("fu", [P, 2, N])
        fu_hi, fu_lo = s2("fu_hi", [P, FT, N], F16), s2("fu_lo", [P, FT, N], F16)
        y3 = s2("y3", [P, C, D])
        bst2, bst3 = s2("bst2", [P, 6]), s2("bst3", [P, 6])
        mv2, mv3 = s2("mv2", [P, C, 2]), s2("mv3", [P, C, 2])
        ve2, ve3 = s2("ve2", [P, C]), s2("ve3", [P, C])
        rstd2, rstd3 = s2("rstd2", [P, C]), s2("rstd3", [P, C])

        xw_loaded, sc_loaded, cn_loaded = sem("xw_loaded"), sem("sc_loaded"), sem("cn_loaded")
        x1_loaded = [sem(f"x1n{t}_loaded") for t in range(C)]
        out_stored = [sem(f"out{t}_stored") for t in range(C)]
        xw_ps, xwh_done, xw_done = sem("xw_ps"), sem("xwh_done"), sem("xw_done")
        const2, sq_done, sq_used = sem("const2"), sem("sq_done"), sem("sq_used")
        sc_step, sqrt_done, scales_done, wdn_done = sem("sc_step"), sem("sqrt_done"), sem("scales_done"), sem("wdn_done")
        xp_ps, xp_done, xhi_done, exp_done = sem("xp_ps"), sem("xp_done"), sem("xhi_done"), sem("exp_done")
        nmax_ready, einv_ready = sem("nmax_ready"), sem("einv_ready")
        mv2_ready, ve2_ready, rstd2_ready = sem("mv2_ready"), sem("ve2_ready"), sem("rstd2_ready")
        x2_ready, x2k_ready = sem("x2_ready"), sem("x2k_ready")
        g_ps, u_ps, th_done, tu_done, gu_done = sem("g_ps"), sem("u_ps"), sem("th_done"), sem("tu_done"), sem("gu_done")
        fhi_done, flo_done, dn_ps, dn_done = sem("fhi_done"), sem("flo_done"), sem("dn_ps"), sem("dn_done")
        y3_ready, mv3_ready, ve3_ready = sem("y3_ready"), sem("mv3_ready"), sem("ve3_ready")
        rstd3_ready, out_ready = sem("rstd3_ready"), sem("out_ready")

        CT, QK, X1T, EN, AT, XM, X2T = 0, KC, KC + 2, KC + 6, KC + 10, KC + 14, KC + 18
        XHI = 2 + 2 + 3 * 4

        def xp(n):
            return bank[6 + n % 2]

        def xp_result(b, n):
            return XP_USES * b + n + 1

        def xp_free(b, n):
            return XP_USES * b + n + 1

        def xp_read(b, n):
            return 2 + XP_USES * b + n + 1

        def hi_index(n):
            if n < EN:
                return n
            return n - 4 if n < XM else n - 8

        def xhi(b, n):
            return XHI * b + hi_index(n) + 1

        X_STAGES = [("ctx",), ("qk",), ("x1t", 0, 1), ("x1t", 2, 3), ("en", 0, 1), ("en", 2, 3),
                    ("at", 0, 1), ("at", 2, 3), ("xm", 0), ("xm", 1), ("xm", 2), ("xm", 3),
                    ("x2t", 0, 1), ("x2t", 2, 3)]

        def schedule(x_stage, inner_tile, down_tile, fi, xb_):
            for f in range(FT + C):
                if fi is not None:
                    if f < FT:
                        inner_tile(fi, f)
                    else:
                        down_tile(fi, f - FT)
                if xb_ is not None and f < len(X_STAGES):
                    x_stage(xb_, X_STAGES[f])

        def pipeline(eng, x_stage, inner_tile, down_tile):
            schedule(x_stage, inner_tile, down_tile, None, 0)
            with eng.Fori(0, B - 1) as i:
                schedule(x_stage, inner_tile, down_tile, i, i + 1)
            schedule(x_stage, inner_tile, down_tile, B - 1, None)

        with nc.Block() as block:

            @block.sync
            def _(sp):
                sp.wait_ge(phase1_done, 5)
                sp.dma_start(cn[:], ctx_t[0]).then_inc(cn_loaded, 16)
                for t in range(C):
                    sp.dma_start(x1n[:, t, :], x1_dram[t]).then_inc(x1_loaded[t], 16)
                sp.dma_start(xw_raw[:, 0, :], xwq).then_inc(xw_loaded, 16)
                sp.dma_start(xw_raw[:, 1, :], xwk).then_inc(xw_loaded, 16)
                sp.dma_start(xb[:, 0:1], xbq.rearrange("(p a) -> p a", a=1)).then_inc(xw_loaded, 16)
                sp.dma_start(xb[:, 1:2], xbk.rearrange("(p a) -> p a", a=1)).then_inc(xw_loaded, 16)
                sp.dma_start(gs[:], gate_s.rearrange("(f p) -> p f", p=P), allow_slow_non_contiguous=True).then_inc(sc_loaded, 16)
                sp.dma_start(us[:], up_s.rearrange("(f p) -> p f", p=P), allow_slow_non_contiguous=True).then_inc(sc_loaded, 16)
                sp.dma_start(down_b[:], down_s.rearrange("(a n) -> a n", a=1).to_broadcast([P, D])
                             ).then_inc(sc_loaded, 16)

                def store(i, t):
                    sp.wait_ge(out_ready, i * C + t + 1)
                    sp.dma_start(out_t[i * C + t], y3[:, t, :]).then_inc(out_stored[t], 16)

                with sp.Fori(0, B - 1) as i:
                    sp.wait_ge(xp_ps, xp_result(i, CT + KC - 1))
                    sp.dma_start(cn[:], ctx_t[i + 1]).then_inc(cn_loaded, 16)
                    for t in range(C):
                        sp.wait_ge(xp_done, xp_read(i, XM + t))
                        sp.dma_start(x1n[:, t, :], x1_dram[(i + 1) * C + t]).then_inc(x1_loaded[t], 16)
                    for t in range(C):
                        store(i, t)
                for t in range(C):
                    store(B - 1, t)
                for t in range(C):
                    sp.wait_ge(out_stored[t], 16 * (B + 1))

            @block.gpsimd
            def _(pool):
                pool.wait_ge(phase1_done, 5)
                pool.sem_inc(flo_done, 2)
                nc.gpsimd.memset(ones[:], 1.0).then_inc(const2, 1)
                nc.gpsimd.memset(half[:], 0.5).then_inc(const2, 1)
                nc.gpsimd.memset(one[:], 1.0).then_inc(const2, 1)
                pool.wait_ge(const2, 3)
                n = 0
                for i in range(2):
                    for f4 in range(3):
                        for k in range(K):
                            if n >= 2:
                                pool.wait_ge(sq_used, n - 1)
                            w = wgu[:, i, k, f4 * 512:(f4 + 1) * 512]
                            nc.gpsimd.tensor_tensor(sq[:, n % 2, :], w, w, ALU.mult).then_inc(sq_done, 1)
                            n += 1

                def rstd_op(mv, ve, rstd, t, mv_sem, ve_sem, rstd_sem, n):
                    pool.wait_ge(mv_sem, n)
                    nc.gpsimd.tensor_tensor(ve[:, t:t + 1], mv[:, t, 1:2], eps_tile[:], ALU.add
                                            ).then_inc(ve_sem, 1)
                    pool.wait_ge(ve_sem, n)
                    nc.gpsimd.tensor_tensor(rstd[:, t:t + 1], ve[:, t:t + 1], neg_half[:, 0:1], ALU.pow
                                            ).then_inc(rstd_sem, 1)

                def x_stage(b, st):
                    if st[0] == "xm":
                        rstd_op(mv2, ve2, rstd2, st[1], mv2_ready, ve2_ready, rstd2_ready, b * C + st[1] + 1)
                        if isinstance(b, int) and st[1] == C - 1:
                            pool.wait_ge(sc_step, 6)
                            nc.gpsimd.tensor_tensor(sc[:, 2, :], sc[:, 1, :], half[:], ALU.pow).then_inc(sqrt_done, 1)

                def inner_tile(i, f):
                    if f == 0:
                        for t in range(C):
                            pool.wait_ge(x2_ready, i * C + t + 1)
                            nc.gpsimd.tensor_tensor(x2k[:, t, :], x2n[:, t, :], one[:].to_broadcast([P, D]), ALU.mult
                                                    ).then_inc(x2k_ready, 1)
                    pool.wait_ge(fhi_done, i * FT + f + 1)
                    nc.gpsimd.tensor_tensor(fu_lo[:, f, :], fu[:, f % 2, :], fu_hi[:, f, :], ALU.subtract
                                            ).then_inc(flo_done, 1)

                def down_tile(i, t):
                    n = i * C + t + 1
                    pool.wait_ge(dn_done, 2 + n)
                    nc.gpsimd.tensor_tensor(y3[:, t, :], y3[:, t, :], x2k[:, t, :], ALU.add).then_inc(y3_ready, 1)
                    rstd_op(mv3, ve3, rstd3, t, mv3_ready, ve3_ready, rstd3_ready, n)

                pipeline(pool, x_stage, inner_tile, down_tile)

            @block.scalar
            def _(act):
                act.wait_ge(phase1_done, 5)
                act.wait_ge(xw_ps, 1)
                for i in range(2):
                    nc.scalar.activation(xw_hi[:, i, :, :],
                                         bank[5][:, i * CTX:(i + 1) * CTX].rearrange("p (k c) -> p k c", k=KC),
                                         ACT.Copy, scale=(-1.0, 1.0)[i]).then_inc(xwh_done, 1)

                def high(b, n, dst, src, **kw):
                    act.wait_ge(xp_ps, xp_result(b, n))
                    nc.scalar.activation(dst, src, **kw).then_inc(xhi_done, 1)

                def blocks(n):
                    return xp(n)[:].rearrange("p (k c) -> p k c", k=K)

                def x_stage(b, st):
                    if st[0] == "ctx":
                        for k in range(KC):
                            high(b, CT + k, ct_hi[:, k, :], xp(CT + k)[:], func=ACT.Copy)
                    elif st[0] == "qk":
                        for i in range(2):
                            high(b, QK + i, qk_hi[:, i, :], xp(QK + i)[:], func=ACT.Identity, bias=xb[:, i:i + 1])
                    elif st[0] == "x1t":
                        for t in st[1:]:
                            high(b, X1T + t, x1t_hi[:, :, t * P:(t + 1) * P], blocks(X1T + t), func=ACT.Copy)
                    elif st[0] == "en":
                        for m in st[1:]:
                            act.wait_ge(nmax_ready, b * C + m + 1)
                            nc.scalar.activation(att[:, m, :], xp(EN + m)[:], ACT.Exp, scale=-1.0,
                                                 bias=nmax[:, m:m + 1], accum_out=esum[:, m:m + 1]
                                                 ).then_inc(exp_done, 1)
                    elif st[0] == "at":
                        for m in st[1:]:
                            high(b, AT + m, att_hi[:, :, m * P:(m + 1) * P], blocks(AT + m), func=ACT.Copy)
                    elif st[0] == "x2t":
                        for t in st[1:]:
                            high(b, X2T + t, x2t_hi[:, :, t * P:(t + 1) * P], blocks(X2T + t), func=ACT.Copy,
                                 scale=X2_SCALE)

                def fuse_high(i, f):
                    act.wait_ge(gu_done, 2 + i * FT + f + 1)
                    nc.scalar.activation(fu_hi[:, f, :], fu[:, f % 2, :], ACT.Copy).then_inc(fhi_done, 1)

                def inner_tile(i, f):
                    if f == 0:
                        act.wait_ge(scales_done, 2)
                    act.wait_ge(g_ps, i * FT + f + 1)
                    nc.scalar.activation(th[:, f % 2, :], bank[f % 2][:], ACT.Tanh, scale=tanh_scale[:, f:f + 1]
                                         ).then_inc(th_done, 1)
                    if f >= 1:
                        fuse_high(i, f - 1)
                    if f == FT - 1:
                        fuse_high(i, f)

                def down_tile(i, t):
                    pass

                pipeline(act, x_stage, inner_tile, down_tile)

            @block.tensor
            def _(pe):
                pe.wait_ge(phase1_done, 5)
                pe.wait_ge(xw_loaded, 64)
                for i in range(2):
                    for k in range(KC):
                        mm = nc.tensor.transpose(bank[5][:, (i * KC + k) * P:(i * KC + k + 1) * P],
                                                 xw_raw[:, i, k * P:(k + 1) * P], ident[:])
                mm.then_inc(xw_ps, 1)

                def column_norms():
                    pe.wait_ge(const2, 2)
                    for n in range(2 * 3 * K):
                        pe.wait_ge(sq_done, n + 1)
                        i, f4, k = n // (3 * K), n // K % 3, n % K
                        for f in range(4):
                            col = (k * 2 + i) * FT + f4 * 4 + f
                            mm = nc.tensor.matmul(bank[4][:, col:col + 1], sq[:, n % 2, f * P:(f + 1) * P],
                                                  ones[:], start=True, stop=True)
                        mm.then_inc(sq_used, 1)

                def three(out_, a_hi, a_lo, b_hi, b_lo, ks):
                    for k in ks:
                        for q, (a, bb) in enumerate(((a_hi, b_hi), (a_hi, b_lo), (a_lo, b_hi))):
                            mm = nc.tensor.matmul(out_, a(k), bb(k), start=(k == 0 and q == 0),
                                                  stop=(k == len(ks) - 1 and q == 2))
                            del bb
                    return mm

                def turn(b, n, src, ks):
                    pe.wait_ge(xp_done, xp_free(b, n))
                    for k in ks:
                        mm = nc.tensor.transpose(xp(n)[:, k * P:(k + 1) * P], src(k), ident[:])
                    mm.then_inc(xp_ps, 1)

                def x_stage(b, st):
                    if st[0] == "ctx":
                        pe.wait_ge(cn_loaded, 16 * (b + 1))
                        for k in range(KC):
                            turn(b, CT + k, lambda t: cn[:, t, k * P:(k + 1) * P], range(C))
                    elif st[0] == "qk":
                        if isinstance(b, int):
                            pe.wait_ge(xw_done, 2)
                        pe.wait_ge(xp_done, xp_read(b, CT + KC - 1))
                        for i in range(2):
                            pe.wait_ge(xp_done, xp_free(b, QK + i))
                            three(xp(QK + i)[:], lambda k: xw_hi[:, i, k, :], lambda k: xw_lo[:, i, k, :],
                                  lambda k: ct_hi[:, k, :], lambda k: ct_lo[:, k, :], range(KC)).then_inc(xp_ps, 1)
                    elif st[0] == "x1t":
                        for t in st[1:]:
                            pe.wait_ge(x1_loaded[t], 16 * (b + 1))
                            turn(b, X1T + t, lambda k: x1n[:, t, k * P:(k + 1) * P], range(K))
                    elif st[0] == "en":
                        if st[1] == 0:
                            pe.wait_ge(xp_done, xp_read(b, QK + 1))
                        for m in st[1:]:
                            pe.wait_ge(xp_done, xp_free(b, EN + m))
                            mc = slice(m * P, (m + 1) * P)
                            three(xp(EN + m)[:], lambda k: qk_hi[:, 0, mc], lambda k: qk_lo[:, 0, mc],
                                  lambda k: qk_hi[:, 1, :], lambda k: qk_lo[:, 1, :], range(1)).then_inc(xp_ps, 1)
                    elif st[0] == "at":
                        for m in st[1:]:
                            pe.wait_ge(xp_done, xp_read(b, EN + m))
                            turn(b, AT + m, lambda k: att[:, m, k * P:(k + 1) * P], range(K))
                    elif st[0] == "xm":
                        t = st[1]
                        if t == 0:
                            pe.wait_ge(xp_done, xp_read(b, AT + C - 1))
                        pe.wait_ge(xp_done, xp_free(b, XM + t))
                        tc = slice(t * P, (t + 1) * P)
                        three(xp(XM + t)[:], lambda k: x1t_hi[:, k, tc], lambda k: x1t_lo[:, k, tc],
                              lambda k: att_hi[:, k, :], lambda k: att_lo[:, k, :], range(K)).then_inc(xp_ps, 1)
                        if isinstance(b, int) and t == 0:
                            column_norms()
                    elif st[0] == "x2t":
                        for t in st[1:]:
                            pe.wait_ge(x2_ready, b * C + t + 1)
                            turn(b, X2T + t, lambda k: x2n[:, t, k * P:(k + 1) * P], range(K))

                def inner_tile(i, f):
                    if f == 0:
                        pe.wait_ge(xp_done, xp_read(i, X2T + C - 1))
                    pe.wait_ge(gu_done, i * FT + f + 1)
                    for w, (first_bank, ready) in enumerate(((0, g_ps), (2, u_ps))):
                        for k in range(K):
                            for q, xt in enumerate((x2t_hi, x2t_lo)):
                                mm = nc.tensor.matmul(bank[first_bank + f % 2][:], wgu[:, w, k, f * P:(f + 1) * P],
                                                      xt[:, k, :], start=(k + q == 0), stop=(k == K - 1 and q == 1))
                        mm.then_inc(ready, 1)

                def down_tile(i, t):
                    if t == 0:
                        pe.wait_ge(flo_done, 2 + i * FT + FT)
                        pe.wait_ge(wdn_done, FT)
                    pe.wait_ge(dn_done, i * C + t + 1)
                    for f in range(FT):
                        for q, fa in enumerate((fu_hi, fu_lo)):
                            mm = nc.tensor.matmul(bank[4 + t % 2][:], fa[:, f, t * P:(t + 1) * P], wdn[:, f, :],
                                                  start=(f + q == 0), stop=(f == FT - 1 and q == 1))
                    mm.then_inc(dn_ps, 1)

                pipeline(pe, x_stage, inner_tile, down_tile)

            @block.vector
            def _(dve):
                dve.wait_ge(phase1_done, 5)
                dve.sem_inc(xp_done, 2)
                dve.sem_inc(gu_done, 2)
                dve.sem_inc(dn_done, 2)
                for t in range(C):
                    dve.sem_inc(out_stored[t], 16)
                dve.wait_ge(xwh_done, 2)
                for i in range(2):
                    src = bank[5][:, i * CTX:(i + 1) * CTX].rearrange("p (k c) -> p k c", k=KC)
                    nc.vector.scalar_tensor_tensor(out=xw_lo[:, i, :, :], in0=src, scalar=(-1.0, 1.0)[i],
                                                   in1=f32v(xw_hi[:, i, :, :]), op0=ALU.mult, op1=ALU.subtract)
                dve.wait_ge(xw_loaded, 64)
                nc.vector.tensor_scalar(xb[:, 0:1], xb[:, 0:1], -1.0, None, ALU.mult)
                dve.drain().then_inc(xw_done, 2)

                step = [0]

                def small(ins):
                    step[0] += 1
                    ins.then_inc(sc_step, 1)
                    dve.wait_ge(sc_step, step[0])

                def finish_scales():
                    dve.wait_ge(sc_loaded, 48)
                    dve.wait_ge(sq_used, 2 * 3 * K)
                    n4 = bank[4][:, 0:K * 2 * FT].rearrange("p (k i) -> p i k", k=K)
                    small(nc.vector.tensor_reduce(norms[:], n4, AX_X, ALU.add))
                    small(nc.vector.tensor_tensor(sc[:, 3, :], gs[:], us[:], ALU.mult))
                    small(nc.vector.tensor_tensor(sc[:, 0, :], norms[:, 0:FT], norms[:, FT:2 * FT], ALU.mult))
                    small(nc.vector.tensor_tensor(sc[:, 5, :], sc[:, 3, :], sc[:, 3, :], ALU.mult))
                    small(nc.vector.tensor_tensor(sc[:, 0, :], sc[:, 0, :], sc[:, 5, :], ALU.mult))
                    small(nc.vector.tensor_scalar(sc[:, 1, :], sc[:, 0, :], 2.0 ** -100, None, ALU.max))
                    dve.wait_ge(sqrt_done, 1)
                    small(nc.vector.tensor_scalar(sc[:, 4, :], sc[:, 2, :], D * 1.1, None, ALU.mult))
                    small(nc.vector.tensor_scalar(sc[:, 5, :].bitcast(U32), sc[:, 4, :].bitcast(U32), 0x7F800000, None,
                                                  ALU.bitwise_and))
                    small(nc.vector.tensor_scalar(back[:], sc[:, 5, :], 2.0 / FUSE_TOP, None, ALU.mult))
                    small(nc.vector.reciprocal(sc[:, 0, :], back[:]))
                    small(nc.vector.tensor_scalar(sc[:, 1, :], sc[:, 3, :], 0.5 / X2_SCALE ** 2, None, ALU.mult))
                    nc.vector.tensor_scalar(tanh_scale[:], gs[:], 0.5 / X2_SCALE, None, ALU.mult
                                            ).then_inc(scales_done, 1)
                    nc.vector.tensor_tensor(fuse_scale[:], sc[:, 0, :], sc[:, 1, :], ALU.mult).then_inc(scales_done, 1)
                    dve.wait_ge(scales_done, 2)
                    for f in range(FT):
                        nc.vector.tensor_scalar(wdn[:, f, :], wdn[:, f, :], back[:, f:f + 1], None, ALU.mult
                                                ).then_inc(wdn_done, 1)

                def low(b, n, dst, hi, src, scale=None, bias=None):
                    dve.wait_ge(xhi_done, xhi(b, n))
                    if scale is None and bias is None:
                        ins = nc.vector.tensor_tensor(dst, src, hi, ALU.subtract)
                    elif bias is None:
                        ins = nc.vector.scalar_tensor_tensor(out=dst, in0=src, scalar=scale, in1=hi, op0=ALU.mult,
                                                             op1=ALU.subtract)
                    else:
                        ins = nc.vector.scalar_tensor_tensor(out=dst, in0=src, scalar=bias, in1=hi, op0=ALU.add,
                                                             op1=ALU.subtract)
                    ins.then_inc(xp_done, 1)

                def blocks(n):
                    return xp(n)[:].rearrange("p (k c) -> p k c", k=K)

                def norm2(b, t):
                    dve.wait_ge(rstd2_ready, b * C + t + 1)
                    nc.vector.tensor_scalar(x2n[:, t, :], x2n[:, t, :], mv2[:, t, 0:1], rstd2[:, t:t + 1],
                                            ALU.subtract, ALU.mult).then_inc(x2_ready, 1)

                def x_stage(b, st):
                    if st[0] == "ctx":
                        for k in range(KC):
                            low(b, CT + k, ct_lo[:, k, :], f32v(ct_hi[:, k, :]), xp(CT + k)[:])
                    elif st[0] == "qk":
                        for i in range(2):
                            low(b, QK + i, qk_lo[:, i, :], f32v(qk_hi[:, i, :]), xp(QK + i)[:], bias=xb[:, i:i + 1])
                    elif st[0] == "x1t":
                        for t in st[1:]:
                            sl = (slice(None), slice(None), slice(t * P, (t + 1) * P))
                            low(b, X1T + t, x1t_lo[sl], f32v(x1t_hi[sl]), blocks(X1T + t))
                    elif st[0] == "en":
                        for m in st[1:]:
                            dve.wait_ge(xp_ps, xp_result(b, EN + m))
                            nc.vector.tensor_reduce(nmax[:, m:m + 1], xp(EN + m)[:], AX_X, ALU.min
                                                    ).then_inc(nmax_ready, 1)
                        for m in st[1:]:
                            dve.wait_ge(exp_done, b * C + m + 1)
                            nc.vector.reciprocal(einv[:, m:m + 1], esum[:, m:m + 1]).then_inc(einv_ready, 1)
                            dve.wait_ge(einv_ready, b * C + m + 1)
                            nc.vector.tensor_scalar(att[:, m, :], att[:, m, :], einv[:, m:m + 1], None, ALU.mult
                                                    ).then_inc(xp_done, 1)
                    elif st[0] == "at":
                        for m in st[1:]:
                            sl = (slice(None), slice(None), slice(m * P, (m + 1) * P))
                            low(b, AT + m, att_lo[sl], f32v(att_hi[sl]), blocks(AT + m))
                    elif st[0] == "xm":
                        t = st[1]
                        n = b * C + t + 1
                        dve.wait_ge(xp_ps, xp_result(b, XM + t))
                        if not isinstance(b, int):
                            dve.wait_ge(x2k_ready, n - C)
                        nc.vector.tensor_tensor(x2n[:, t, :], xp(XM + t)[:], x1n[:, t, :], ALU.add
                                                ).then_inc(xp_done, 1)
                        dve.wait_ge(xp_done, xp_read(b, XM + t))
                        nc.vector.bn_stats(bst2[:], x2n[:, t, :])
                        dve.drain()
                        nc.vector.bn_aggr(mv2[:, t, :], bst2[:]).then_inc(mv2_ready, 1)
                        if t >= 1:
                            norm2(b, t - 1)
                        if t == C - 1:
                            norm2(b, t)
                        if isinstance(b, int) and t == C - 1:
                            finish_scales()
                    elif st[0] == "x2t":
                        for t in st[1:]:
                            sl = (slice(None), slice(None), slice(t * P, (t + 1) * P))
                            low(b, X2T + t, x2t_lo[sl], x2t_hi[sl], blocks(X2T + t), scale=X2_SCALE)

                def inner_tile(i, f):
                    n = i * FT + f + 1
                    dve.wait_ge(th_done, n)
                    nc.vector.scalar_tensor_tensor(out=tu[:, f % 2, :], in0=th[:, f % 2, :], scalar=1.0,
                                                   in1=bank[f % 2][:], op0=ALU.add, op1=ALU.mult).then_inc(tu_done, 1)
                    dve.wait_ge(tu_done, n)
                    dve.wait_ge(u_ps, n)
                    dve.wait_ge(flo_done, n)
                    nc.vector.scalar_tensor_tensor(out=fu[:, f % 2, :], in0=bank[2 + f % 2][:],
                                                   scalar=fuse_scale[:, f:f + 1], in1=tu[:, f % 2, :],
                                                   op0=ALU.mult, op1=ALU.mult).then_inc(gu_done, 1)

                def norm3(i, t):
                    dve.wait_ge(rstd3_ready, i * C + t + 1)
                    nc.vector.tensor_scalar(y3[:, t, :], y3[:, t, :], mv3[:, t, 0:1], rstd3[:, t:t + 1],
                                            ALU.subtract, ALU.mult).then_inc(out_ready, 1)

                def stats3(i, t):
                    n = i * C + t + 1
                    dve.wait_ge(y3_ready, n)
                    nc.vector.bn_stats(bst3[:], y3[:, t, :])
                    dve.drain()
                    nc.vector.bn_aggr(mv3[:, t, :], bst3[:]).then_inc(mv3_ready, 1)

                def down_tile(i, t):
                    n = i * C + t + 1
                    dve.wait_ge(dn_ps, n)
                    dve.wait_ge(out_stored[t], 16 * (i + 1))
                    nc.vector.tensor_tensor(y3[:, t, :], bank[4 + t % 2][:], down_b[:], ALU.mult
                                            ).then_inc(dn_done, 1)
                    if t >= 1:
                        stats3(i, t - 1)
                    if t >= 2:
                        norm3(i, t - 2)
                    if t == C - 1:
                        stats3(i, t)
                        norm3(i, t - 1)
                        norm3(i, t)

                pipeline(dve, x_stage, inner_tile, down_tile)


_INS = ['x', 'ctx_1024', 'L0_attn_log_decay', 'L0_attn_Wq', 'L0_attn_Wk', 'L0_attn_Wv', 'L0_attn_Wo',
        'L0_attn_Wg1', 'L0_attn_Wg2', 'L0_attn_norm_w', 'L0_xattn_Wq', 'L0_xattn_bq', 'L0_xattn_Wk',
        'L0_xattn_bk', 'L0_ffn_gate_w', 'L0_ffn_up_w', 'L0_ffn_down_w', 'L0_ffn_gate_scale',
        'L0_ffn_up_scale', 'L0_ffn_down_scale']


def kernel(**inputs):
    import numpy as _np
    import concourse.bacc as _bacc
    from concourse import mybir as _mybir
    from concourse.bass_utils import run_bass_kernel_spmd as _run

    nc = _bacc.Bacc("TRN2", target_bir_lowering=False, num_devices=1)
    arrays, args = {}, []
    for name in _INS:
        a = _np.ascontiguousarray(inputs[name])
        arrays[f"in_{name}_dram"] = a
        args.append(nc.dram_tensor(f"in_{name}_dram", a.shape, _mybir.dt.from_np(a.dtype), kind="ExternalInput").ap())
    args.append(nc.dram_tensor("out_0_dram", (B, N, D), _mybir.dt.float32, kind="ExternalOutput").ap())
    build(nc, *args)
    r = _run(nc, [arrays], core_ids=[0])
    return r.results[0]["out_0_dram"]
```

```python
from contextlib import ExitStack

import concourse.bass as bass
from concourse import mybir

F32 = mybir.dt.float32
F32R = mybir.dt.float32r
F16 = mybir.dt.float16
BF16 = mybir.dt.bfloat16
U32 = mybir.dt.uint32
I32 = mybir.dt.int32
ALU = mybir.AluOpType
ACT = mybir.ActivationFunctionType
AX_X = mybir.AxisListType.X

P = 128
B, N, D = 4, 512, 512
H, HD = 16, 32
C = N // P
K = D // P
G = K
J = P // HD
CTX = 256
KC = CTX // P
FF = 1536
FT = FF // P
EPS = 1e-5

X2_SCALE = 1024.0
FUSE_TOP = 2.0 ** 15

GROUP_SCALE = HD * 256.0

PA_USES = 20
B5_USES = 7
XP_USES = 24
PREP = 9


def f32v(ap):
    return ap.bitcast(F32)


def build(nc, x, ctx_in, ld, wq, wk, wv, wo, wg1, wg2, nw, xwq, xbq, xwk, xbk,
          gate_w, up_w, down_w, gate_s, up_s, down_s, out):
    x_t = x.rearrange("b (t p) d -> (b t) p d", p=P)
    out_t = out.rearrange("b (t p) d -> (b t) p d", p=P)
    x1_dram = nc.dram_tensor("x1_scratch", (B * C, P, D), F32, kind="Internal").ap()
    ctx_t = ctx_in.rearrange("b (t p) d -> b p t d", p=P)
    gate_t = gate_w.rearrange("(k p) f -> k p f", p=P)
    up_t = up_w.rearrange("(k p) f -> k p f", p=P)
    down_t = down_w.rearrange("(k p) f -> k p f", p=P)

    with ExitStack() as top:
        def sem(name):
            return top.enter_context(nc.semaphore(name))

        def sb(name, shape, dt=F32, stack=top):
            return stack.enter_context(nc.sbuf_tensor(name, shape, dt))

        bank = [top.enter_context(nc.psum_tensor(f"bank{i}", [P, 512], F32)) for i in range(8)]

        ident = sb("ident", [P, P])
        wgu = sb("wgu", [P, 2, K, FF], F16)
        wdn = sb("wdn", [P, FT, D], BF16)
        neg_half = sb("neg_half", [P, H])
        eps_tile = sb("eps_tile", [P, 1])
        xin = sb("xin", [P, 2, D])
        raw = sb("raw", [P, 512])
        phase1_done = sem("phase1_done")
        xw_loaded, cn_loaded = sem("xw_loaded"), sem("cn_loaded")

        with ExitStack() as ph:
            def s1(name, shape, dt=F32):
                return sb(name, shape, dt, ph)

            w_hi = {w: s1(f"{w}_hi", [P, K, D], F32R) for w in ("wq", "wk", "wv", "wo")}
            w_lo = {w: s1(f"{w}_lo", [P, K, D], F32R) for w in ("wq", "wk", "wv", "wo")}
            wg1_hi = s1("wg1_hi", [P, K, P], F32R)
            wg1_lo = s1("wg1_lo", [P, K, P], F32R)
            wg2_st = s1("wg2_st", [P, D], F32R)
            decay = s1("decay", [P, J, G, P])
            qdec = s1("qdec", [P, G, P])
            kdec = s1("kdec", [P, G, P])
            cdec = s1("cdec", [P, G, HD])
            xres = s1("xres", [P, 2, D])
            xt_hi = s1("xt_hi", [P, K, N], F32R)
            xt_lo = s1("xt_lo", [P, K, N], F32R)
            qt = s1("qt", [P, G, N])
            kt = s1("kt", [P, G, N])
            v = s1("v", [P, C, D])
            g1_st = s1("g1_st", [P, N], F32R)
            qtd = s1("qtd", [P, G, P])
            ktd = s1("ktd", [P, G, P])
            kn = s1("kn", [P, D])
            probs = s1("probs", [P, J, G * P])
            gt = s1("gt", [P, D])
            og = s1("og", [P, 2, D])
            osq = s1("osq", [P, D])
            ot_hi = s1("ot_hi", [P, K, P], F32R)
            ot_lo = s1("ot_lo", [P, K, P], F32R)
            y = s1("y", [P, 2, D])
            state = s1("state", [P, G * HD])
            state_d = s1("state_d", [P, G * HD])
            state_bd = s1("state_bd", [P, G, P])
            blocks_of_4 = s1("blocks_of_4", [P, J, HD])
            ss = s1("ss", [P, H])
            ss_e = s1("ss_e", [P, H])
            eps_group = s1("eps_group", [P, H])
            rs = s1("rs", [P, H])
            bst = s1("bst", [P, 6])
            mv = s1("mv", [P, 2])
            var_e = s1("var_e", [P, 1])
            rstd = s1("rstd", [P, 1])
            magic = s1("magic", [P, 512])
            ldb = s1("ldb", [P, H])
            ldp = s1("ldp", [P, G])
            ldn = s1("ldn", [P, G])
            ld127 = s1("ld127", [P, G])
            nw_p = s1("nw_p", [P, K])
            wraw = [[t[:, k, :] for k in range(K)] for t in (qt, kt, v)]
            wraw.append([t[:].rearrange("p g c -> p (g c)") for t in (ktd, qtd)] + [kn[:], osq[:]])
            g1raw = og[:, 0, :].rearrange("p (k m) -> p k m", k=K)
            g2raw = y[:, 0, :]
            diff_i = gt[:, 0 * P:1 * P].bitcast(I32)
            diff = gt[:, 1 * P:2 * P]
            ramp_i = gt[:, 2 * P:3 * P].bitcast(I32)
            ramp = gt[:, 3 * P:4 * P]

            w_loaded = [sem(f"w{i}_loaded") for i in range(4)]
            small_loaded = sem("small_loaded")
            g1raw_loaded, g2raw_loaded, ld_loaded = sem("g1raw_loaded"), sem("g2raw_loaded"), sem("ld_loaded")
            const_done, iota_done, tables_done, masks_exp = (
                sem("const_done"), sem("iota_done"), sem("tables_done"), sem("masks_exp"))
            masks_done, ramps_done, wo_scaled = sem("masks_done"), sem("ramps_done"), sem("wo_scaled")
            wqk_hi_done, wqk_lo_done, wvo_hi_done, wg_hi_done, wlo_done = (
                sem("wqk_hi_done"), sem("wqk_lo_done"), sem("wvo_hi_done"), sem("wg_hi_done"), sem("wlo_done"))
            ident_zero, blocks_step = sem("ident_zero"), sem("blocks_step")
            ldn_done = sem("ldn_done")

            xin_loaded = [sem(f"xin{i}_loaded") for i in range(2)]
            xres_loaded = [sem(f"xres{i}_loaded") for i in range(2)]
            x1_stored = [sem(f"x1_{i}_stored") for i in range(2)]
            raw_loaded, magic_exp, magic_ready, raw_added, prep_done = (
                sem("raw_loaded"), sem("magic_exp"), sem("magic_ready"), sem("raw_added"), sem("prep_done"))
            pa_ps, pa_done, xth_done, tanh_done, g1h_done = (
                sem("pa_ps"), sem("pa_done"), sem("xth_done"), sem("tanh_done"), sem("g1h_done"))
            ktd_ready, qtd_ready = sem("ktd_ready"), sem("qtd_ready")
            b5_ps, b5_done = sem("b5_ps"), sem("b5_done")
            sc_ps, probs_done, pv_done, og_done = sem("sc_ps"), sem("probs_done"), sem("pv_done"), sem("og_done")
            state_new = sem("state_new")
            state_decayed, sq_ready, ss_ready = sem("state_decayed"), sem("sq_ready"), sem("ss_ready")
            ss_scaled, rs_ready, ogn_ready = sem("ss_scaled"), sem("rs_ready"), sem("ogn_ready")
            ot_ps, oth_done, ot_done, wo_ps, y_done = (
                sem("ot_ps"), sem("oth_done"), sem("ot_done"), sem("wo_ps"), sem("y_done"))
            mv_ready, var_ready, rstd_ready, x1_ready = (
                sem("mv_ready"), sem("var_ready"), sem("rstd_ready"), sem("x1_ready"))

            def pa_result(b, n):
                return PA_USES * (b + 1) + n + 1

            def pa_read(b, n):
                return 2 + PA_USES * b + n + 1

            def prob_slot(g):
                return probs[:, g, :]

            def b5_use(c):
                return 2 * c + 1 if c < 3 else 6

            def interleaved(project, step, b, nb):
                project(nb, "x", 0, C)
                if b is not None:
                    step(b, 5)
                project(nb, "qk", 4, 7)
                if b is not None:
                    step(b, 6)
                project(nb, "qk", 7, 10)
                if b is not None:
                    step(b, 7)
                project(nb, "qk", 10, 12)
                project(nb, "v", 12, 16)
                project(nb, "g1", 16, 17)

            def chunk_pipeline(eng, project, step):
                interleaved(project, step, None, 0)
                with eng.Fori(0, B - 1) as i:
                    for s in range(5):
                        step(i, s)
                    interleaved(project, step, i, i + 1)
                for s in range(8):
                    step(B - 1, s)

            with nc.Block() as block:

                @block.sync
                def _(sp):
                    sp.dma_start(ldb[:], ld.rearrange("(a h) -> a h", a=1).to_broadcast([P, H])
                                 ).then_inc(ld_loaded, 16)
                    for j in range(J):
                        sp.dma_start(ldp[j * HD:(j + 1) * HD, :],
                                     ld.rearrange("(g j) -> j g", j=J)[j:j + 1, :].to_broadcast([HD, G]),
                                     allow_slow_non_contiguous=True).then_inc(ld_loaded, 16)
                    sp.dma_start(qt[:], wk.rearrange("(k p) n -> p k n", p=P)).then_inc(w_loaded[1], 16)

                    def load_x(b, t):
                        sp.dma_start(xin[:, t % 2, :], x_t[b * C + t]).then_inc(xin_loaded[t % 2], 16)

                    def load_raw(b, r):
                        sp.wait_ge(prep_done, b * PREP + r + 1)
                        if r < 6:
                            src = (gate_t, up_t)[r // 3][b, :, (r % 3) * 512:(r % 3 + 1) * 512]
                        else:
                            src = down_t[b * 3 + (r - 6)]
                        sp.dma_start(raw[:], src).then_inc(raw_loaded, 16)

                    def load_xres(b, c):
                        sp.wait_ge(y_done, b * C + c + 1)
                        sp.dma_start(xres[:, c % 2, :], x_t[b * C + c]).then_inc(xres_loaded[c % 2], 16)

                    def store_x1(b, c):
                        sp.wait_ge(x1_ready, b * C + c + 1)
                        sp.dma_start(x1_dram[b * C + c], y[:, c % 2, :]).then_inc(x1_stored[c % 2], 16)

                    def project(b, part, first, last):
                        if part == "x":
                            if isinstance(b, int):
                                load_x(b, 0)
                                load_x(b, 1)
                                sp.dma_start(kt[:], wq.rearrange("(k p) n -> p k n", p=P)).then_inc(w_loaded[0], 16)
                            for t in range(2, C):
                                sp.wait_ge(pa_ps, pa_result(b, t - 2))
                                load_x(b, t)
                            load_raw(b, 0)
                        elif part == "qk":
                            for n in range(first, last):
                                if n % 2 == 1:
                                    load_raw(b, (n - 5) // 2 + 1)
                        elif part == "v":
                            load_raw(b, 5)
                            load_raw(b, 6)

                    def step(b, s):
                        if s == 0:
                            if not isinstance(b, int):
                                for t in range(2):
                                    sp.wait_ge(pa_ps, pa_result(b, t + 2))
                                    load_x(b + 1, t)
                            else:
                                sp.wait_ge(pa_ps, pa_result(b, C - 1))
                                sp.dma_start(xin[:].rearrange("p a d -> p (a d)").rearrange("p (t c) -> p t c", t=C),
                                             ctx_t[0]).then_inc(cn_loaded, 16)
                            load_xres(b, 0)
                            load_xres(b, 1)
                        if 1 <= s <= 2:
                            load_raw(b, 6 + s)
                        if s == 3 and isinstance(b, int):
                            sp.wait_ge(prep_done, 1 + B * PREP)
                            sp.dma_start(raw[:, 0:CTX], xwq).then_inc(xw_loaded, 16)
                            sp.dma_start(raw[:, CTX:2 * CTX], xwk).then_inc(xw_loaded, 16)
                        if 4 <= s <= 5:
                            load_xres(b, s - 2)
                        if s >= 4:
                            store_x1(b, s - 4)

                    chunk_pipeline(sp, project, step)
                    for s in x1_stored:
                        sp.wait_ge(s, 16 + 16 * B * C // 2)
                    sp.sem_inc(phase1_done, 1)

                @block.gpsimd
                def _(pool):
                    nc.gpsimd.memset(ident[:], 0.0).then_inc(ident_zero, 1)
                    nc.gpsimd.iota(diff_i, pattern=[[1, P]], base=0, channel_multiplier=-1).then_inc(iota_done, 1)
                    nc.gpsimd.iota(ramp_i, pattern=[[1, P]], base=0, channel_multiplier=0).then_inc(iota_done, 1)
                    pool.wait_ge(ident_zero, 1)
                    nc.gpsimd.affine_select(out=ident[:], in_=ident[:], compare_op=ALU.not_equal, fill=1.0,
                                            base=0, pattern=[[-1, P]], channel_multiplier=1).then_inc(const_done, 1)
                    pool.sem_inc(prep_done, 1)
                    nc.gpsimd.memset(neg_half[:], -0.5)
                    nc.gpsimd.memset(eps_tile[:], EPS)
                    nc.gpsimd.memset(eps_group[:], EPS * GROUP_SCALE)
                    nc.gpsimd.memset(blocks_of_4[:], 1.0).then_inc(blocks_step, 1)
                    pool.wait_ge(blocks_step, 1)
                    nc.gpsimd.affine_select(out=blocks_of_4[:], in_=blocks_of_4[:], compare_op=ALU.is_ge, fill=0.0,
                                            base=0, pattern=[[-HD, J], [0, HD]], channel_multiplier=1
                                            ).then_inc(blocks_step, 1)
                    pool.wait_ge(blocks_step, 2)
                    nc.gpsimd.affine_select(out=blocks_of_4[:], in_=blocks_of_4[:], compare_op=ALU.is_ge, fill=0.0,
                                            base=HD - 1, pattern=[[HD, J], [0, HD]], channel_multiplier=-1
                                            ).then_inc(blocks_step, 1)
                    for h in range(H):
                        pool.wait_ge(masks_exp, h + 1)
                        dh = decay[:, h % J, h // J, :]
                        nc.gpsimd.affine_select(out=dh, in_=dh, compare_op=ALU.is_ge,
                                                fill=0.0, base=0, pattern=[[1, P]], channel_multiplier=-1
                                                ).then_inc(masks_done, 1)
                    for k in range(K):
                        pool.wait_ge(wvo_hi_done, k + 1)
                        nc.gpsimd.tensor_tensor(w_lo["wv"][:, k, :], wraw[2][k], f32v(w_hi["wv"][:, k, :]),
                                                ALU.subtract).then_inc(wlo_done, 1)
                    pool.wait_ge(wg_hi_done, 2)
                    nc.gpsimd.tensor_tensor(wg1_lo[:], g1raw, f32v(wg1_hi[:]), ALU.subtract).then_inc(wlo_done, 1)
                    for r in (2, 3):
                        pool.wait_ge(wlo_done, K + r - 1)
                        q = slice(r * HD, (r + 1) * HD)
                        nc.gpsimd.tensor_tensor(wg2_st[q, :], g2raw[q, :], f32v(wg2_st[q, :]), ALU.subtract
                                                ).then_inc(wlo_done, 1)
                    pool.wait_ge(wlo_done, K + 3)
                    for k in range(K):
                        pool.wait_ge(wvo_hi_done, K + k + 1)
                        nc.gpsimd.tensor_tensor(w_lo["wo"][:, k, :], wraw[3][k], f32v(w_hi["wo"][:, k, :]),
                                                ALU.subtract).then_inc(wlo_done, 1)
                    pool.wait_ge(wlo_done, 2 * K + 3)
                    pool.wait_ge(tables_done, 1)

                    def prep(b, r):
                        pool.wait_ge(magic_ready, b * PREP + r + 1)
                        nc.gpsimd.tensor_tensor(raw[:], raw[:], magic[:], ALU.add).then_inc(raw_added, 1)
                        pool.wait_ge(raw_added, b * PREP + r + 1)
                        if r < 6:
                            dst = wgu[:, r // 3, b, (r % 3) * 512:(r % 3 + 1) * 512]
                        else:
                            dst = wdn[:, b * 3 + (r - 6), :]
                        nc.gpsimd.tensor_tensor(dst, raw[:], magic[:], ALU.subtract).then_inc(prep_done, 1)

                    def project(b, part, first, last):
                        for n in range(first, last):
                            if n >= 5 and n % 2 == 1:
                                prep(b, (n - 5) // 2)

                    def step(b, s):
                        c = s
                        if s == 0:
                            pool.wait_ge(pa_done, pa_read(b, 11))
                        if c <= 2:
                            if c >= 1:
                                pool.wait_ge(b5_ps, b * B5_USES + 2 * (c - 1) + 1)
                            nc.gpsimd.tensor_tensor(ktd[:], kt[:, :, c * P:(c + 1) * P], kdec[:], ALU.mult
                                                    ).then_inc(ktd_ready, 1)
                        if 1 <= c <= 3:
                            if c >= 2:
                                pool.wait_ge(pv_done, b * 16 + 4 * c)
                            nc.gpsimd.tensor_tensor(qtd[:], qt[:, :, c * P:(c + 1) * P], qdec[:], ALU.mult
                                                    ).then_inc(qtd_ready, 1)
                        c = s - 1
                        if 0 <= c < C:
                            n = b * C + c + 1
                            pool.wait_ge(og_done, 1 + n)
                            nc.gpsimd.tensor_tensor(osq[:], og[:, c % 2, :], og[:, c % 2, :], ALU.mult
                                                    ).then_inc(sq_ready, 1)
                            pool.wait_ge(ss_ready, n)
                            nc.gpsimd.tensor_tensor(ss_e[:], ss[:], eps_group[:], ALU.add).then_inc(ss_scaled, 1)
                            pool.wait_ge(ss_scaled, n)
                            nc.gpsimd.tensor_tensor(rs[:], ss_e[:], neg_half[:], ALU.pow).then_inc(rs_ready, 1)
                            pool.wait_ge(rs_ready, n)
                            o3 = og[:, c % 2, :].rearrange("p (h d) -> p h d", d=HD)
                            nc.gpsimd.tensor_tensor(o3, o3, rs[:].unsqueeze(2).to_broadcast([P, H, HD]),
                                                    ALU.mult).then_inc(ogn_ready, 1)
                        c = s - 3
                        if 0 <= c < C:
                            n = b * C + c + 1
                            pool.wait_ge(mv_ready, n)
                            nc.gpsimd.tensor_tensor(var_e[:], mv[:, 1:2], eps_tile[:], ALU.add
                                                    ).then_inc(var_ready, 1)
                            pool.wait_ge(var_ready, n)
                            nc.gpsimd.tensor_tensor(rstd[:], var_e[:], neg_half[:, 0:1], ALU.pow
                                                    ).then_inc(rstd_ready, 1)
                        if 1 <= s <= 3:
                            prep(b, 5 + s)

                    chunk_pipeline(pool, project, step)
                    pool.wait_ge(prep_done, 1 + B * PREP)
                    pool.wait_ge(rstd_ready, B * C)
                    pool.sem_inc(phase1_done, 1)

                @block.scalar
                def _(act):
                    act.sem_inc(b5_done, 1)
                    act.dma_start(v[:], wv.rearrange("(k p) n -> p k n", p=P)).then_inc(w_loaded[2], 16)
                    act.dma_start(nw_p[:], nw.rearrange("(k p) -> p k", p=P), allow_slow_non_contiguous=True
                                  ).then_inc(small_loaded, 16)
                    for r in range(4):
                        act.dma_start(g1raw[:, :, r * HD:(r + 1) * HD], wg1.rearrange("(k p) c -> p k c", p=P)
                                      ).then_inc(g1raw_loaded, 16)
                        act.dma_start(g2raw[r * HD:(r + 1) * HD, :], wg2).then_inc(g2raw_loaded, 16)
                    for k in range(K):
                        act.dma_start(wraw[3][k], wo[k * P:(k + 1) * P, :]).then_inc(w_loaded[3], 16)
                    act.wait_ge(ramps_done, 2)
                    act.wait_ge(ld_loaded, 16 * (1 + J))
                    for h in range(H):
                        nc.scalar.activation(decay[:, h % J, h // J, :], diff, ACT.Exp, scale=ldb[:, h:h + 1]
                                             ).then_inc(masks_exp, 1)
                    act.wait_ge(ldn_done, 2)
                    for g in range(G):
                        nc.scalar.activation(qdec[:, g, :], ramp, ACT.Exp, scale=ldp[:, g:g + 1],
                                             bias=ldp[:, g:g + 1])
                        mm = nc.scalar.activation(kdec[:, g, :], ramp, ACT.Exp, scale=ldn[:, g:g + 1],
                                                  bias=ld127[:, g:g + 1])
                    mm.then_inc(tables_done, 1)
                    for i, w in ((2, "wv"), (3, "wo")):
                        if w == "wo":
                            act.wait_ge(wo_scaled, K)
                        else:
                            act.wait_ge(w_loaded[i], 16)
                        for k in range(K):
                            nc.scalar.activation(w_hi[w][:, k, :], wraw[i][k], ACT.Copy).then_inc(wvo_hi_done, 1)

                    def project(b, part, first, last):
                        if part == "x":
                            for t in range(C):
                                act.wait_ge(pa_ps, pa_result(b, t))
                                nc.scalar.activation(xt_hi[:, :, t * P:(t + 1) * P],
                                                     bank[t % 2][:].rearrange("p (k c) -> p k c", k=K), ACT.Copy
                                                     ).then_inc(xth_done, 1)
                        elif part == "g1":
                            act.wait_ge(pa_ps, pa_result(b, 16))
                            nc.scalar.activation(g1_st[:], bank[0][:], ACT.Copy).then_inc(g1h_done, 1)
                        else:
                            for n in range(first, last):
                                act.wait_ge(pa_ps, pa_result(b, n))
                                if n >= 6:
                                    act.wait_ge(pa_done, pa_read(b, n - 2))
                                nc.scalar.activation(prob_slot(n % 2), bank[n % 2][:], ACT.Tanh, scale=0.5
                                                     ).then_inc(tanh_done, 1)

                    def step(b, s):
                        c = s - 1
                        if 0 <= c < C:
                            act.wait_ge(b5_ps, b * B5_USES + b5_use(c) + 1)
                            act.wait_ge(og_done, b * C + c + 1)
                            nc.scalar.activation(gt[:], bank[5][:], ACT.Tanh, scale=0.5).then_inc(b5_done, 1)
                        c = s
                        if c <= 2:
                            act.wait_ge(b5_ps, b * B5_USES + 2 * c + 1)
                            nc.scalar.activation(kn[:], bank[5][:], ACT.Copy).then_inc(b5_done, 1)
                        c = s - 2
                        if 0 <= c < C:
                            act.wait_ge(ot_ps, b * C + c + 1)
                            nc.scalar.activation(ot_hi[:], bank[6][:].rearrange("p (k c) -> p k c", k=K), ACT.Copy
                                                 ).then_inc(oth_done, 1)

                    chunk_pipeline(act, project, step)
                    act.wait_ge(oth_done, B * C)
                    act.sem_inc(phase1_done, 1)

                @block.tensor
                def _(pe):
                    pe.sem_inc(pa_ps, PA_USES)

                    def project(b, part, first, last):
                        first_batch = isinstance(b, int)
                        if part == "x":
                            if first_batch:
                                pe.wait_ge(const_done, 1)
                            for t in range(C):
                                pe.wait_ge(xin_loaded[t % 2], 32 * b + 16 * (t // 2 + 1))
                                pe.wait_ge(pa_done, PA_USES * b + t + 1)
                                for k in range(K):
                                    mm = nc.tensor.transpose(bank[t % 2][:, k * P:(k + 1) * P],
                                                             xin[:, t % 2, k * P:(k + 1) * P], ident[:])
                                mm.then_inc(pa_ps, 1)
                        elif part == "qk":
                            if first == 4:
                                pe.wait_ge(pa_done, pa_read(b, 3))
                                if first_batch:
                                    pe.wait_ge(wqk_lo_done, 2 * K)
                            for n in range(first, last):
                                w, g = ("wq", "wk")[n % 2], (n - 4) // 2
                                pe.wait_ge(pa_done, PA_USES * b + n + 1)
                                for k in range(K):
                                    for q, (wt, xt) in enumerate(((w_hi, xt_hi), (w_hi, xt_lo), (w_lo, xt_hi))):
                                        mm = nc.tensor.matmul(bank[n % 2][:], wt[w][:, k, g * P:(g + 1) * P],
                                                              xt[:, k, :], start=(k + q == 0), stop=(k == K - 1 and q == 2))
                                mm.then_inc(pa_ps, 1)
                        elif part == "v":
                            if first_batch:
                                pe.wait_ge(wlo_done, K)
                            for n in range(first, last):
                                t = n - 12
                                pe.wait_ge(pa_done, PA_USES * b + n + 1)
                                for k in range(K):
                                    for q, (xt, wt) in enumerate(((xt_hi, w_hi), (xt_hi, w_lo), (xt_lo, w_hi))):
                                        mm = nc.tensor.matmul(bank[n % 2][:], xt[:, k, t * P:(t + 1) * P], wt["wv"][:, k, :],
                                                              start=(k + q == 0), stop=(k == K - 1 and q == 2))
                                mm.then_inc(pa_ps, 1)
                        else:
                            if first_batch:
                                pe.wait_ge(wlo_done, K + 3)
                            pe.wait_ge(pa_done, PA_USES * b + 16 + 1)
                            for k in range(K):
                                for q, (wt, xt) in enumerate(((wg1_hi, xt_hi), (wg1_hi, xt_lo), (wg1_lo, xt_hi))):
                                    mm = nc.tensor.matmul(bank[0][:], wt[:, k, :], xt[:, k, :],
                                                          start=(k + q == 0), stop=(k == K - 1 and q == 2))
                            mm.then_inc(pa_ps, 1)

                    def scores(b, c, j):
                        pe.wait_ge(probs_done, b * 16 + c * 4 + j + 1)
                        r = slice(j * HD, (j + 1) * HD)
                        for g in range(G):
                            mm = nc.tensor.matmul(bank[2 + j % 2][:, g * P:(g + 1) * P],
                                                  kt[r, g, c * P:(c + 1) * P], qt[r, g, c * P:(c + 1) * P],
                                                  start=True, stop=True)
                        mm.then_inc(sc_ps, 1)

                    def values(b, c, j):
                        if j == 0:
                            pe.wait_ge(og_done, b * C + c + 1)
                            if c >= 1:
                                pe.wait_ge(qtd_ready, b * 3 + c)
                                pe.wait_ge(pa_done, pa_read(b, 17 + c - 1))
                                for g in range(G):
                                    nc.tensor.matmul(bank[4][:, g * P:(g + 1) * P], qtd[:, g, :], state_bd[:, g, :],
                                                     start=(g == 0), stop=False, skip_group_check=True)
                        pe.wait_ge(probs_done, 2 + b * 16 + c * 4 + j + 1)
                        for g in range(G):
                            cols = slice((g * J + j) * HD, (g * J + j + 1) * HD)
                            mm = nc.tensor.matmul(bank[4][:, cols], probs[:, j, g * P:(g + 1) * P], v[:, c, cols],
                                                  start=(c == 0 and j + g == 0), stop=(j == J - 1 and g == G - 1),
                                                  skip_group_check=True)
                        mm.then_inc(pv_done, 1)

                    def step(b, s):
                        c = s - 1
                        if 0 <= c < C:
                            if c == 0:
                                pe.wait_ge(pa_done, pa_read(b, 16))
                            pe.wait_ge(b5_done, b * B5_USES + b5_use(c) + 1)
                            nc.tensor.matmul(bank[5][:], g1_st[:, c * P:(c + 1) * P], wg2_st[:],
                                             start=True, stop=True).then_inc(b5_ps, 1)
                        if s == 0:
                            pe.wait_ge(pa_done, pa_read(b, 15))
                        for j in range(J):
                            if s < C:
                                scores(b, s, j)
                            if 0 <= s - 1 < C:
                                values(b, s - 1, j)
                        c = s - 1
                        if 0 <= c <= 2:
                            n = 17 + c
                            pe.wait_ge(b5_done, 1 + b * B5_USES + 2 * c + 1)
                            pe.wait_ge(pa_done, PA_USES * b + n + 1)
                            for h in range(H):
                                g, j = h // J, h % J
                                cols = slice(h * HD, (h + 1) * HD)
                                mm = nc.tensor.matmul(bank[n % 2][j * HD:(j + 1) * HD, g * HD:(g + 1) * HD],
                                                      kn[:, cols], v[:, c, cols], start=True, stop=True)
                            mm.then_inc(pa_ps, 1)
                        c = s
                        if c <= 2:
                            pe.wait_ge(ktd_ready, b * 3 + c + 1)
                            pe.wait_ge(b5_done, b * B5_USES + 2 * c + 1)
                            for g in range(G):
                                mm = nc.tensor.transpose(bank[5][:, g * P:(g + 1) * P], ktd[:, g, :], ident[:])
                            mm.then_inc(b5_ps, 1)
                        c = s - 3
                        if 0 <= c < C:
                            pe.wait_ge(ot_done, 1 + b * C + c + 1)
                            pe.wait_ge(y_done, b * C + c + 2)
                            for k in range(K):
                                for q, (ot, wt) in enumerate(((ot_hi, w_hi), (ot_hi, w_lo), (ot_lo, w_hi))):
                                    mm = nc.tensor.matmul(bank[7][:], ot[:, k, :], wt["wo"][:, k, :],
                                                          start=(k + q == 0), stop=(k == K - 1 and q == 2))
                            mm.then_inc(wo_ps, 1)
                        c = s - 2
                        if 0 <= c < C:
                            pe.wait_ge(ogn_ready, b * C + c + 1)
                            pe.wait_ge(ot_done, b * C + c + 1)
                            for k in range(K):
                                mm = nc.tensor.transpose(bank[6][:, k * P:(k + 1) * P],
                                                         og[:, c % 2, k * P:(k + 1) * P], ident[:])
                            mm.then_inc(ot_ps, 1)

                    chunk_pipeline(pe, project, step)
                    pe.wait_ge(wo_ps, B * C)
                    pe.sem_inc(phase1_done, 1)

                @block.vector
                def _(dve):
                    dve.sem_inc(pa_done, 2)
                    dve.sem_inc(probs_done, 2)
                    dve.sem_inc(og_done, 1)
                    dve.sem_inc(ot_done, 1)
                    dve.sem_inc(y_done, 2)
                    dve.sem_inc(x1_stored[0], 16)
                    dve.sem_inc(x1_stored[1], 16)
                    dve.wait_ge(iota_done, 2)
                    nc.vector.tensor_scalar(diff, diff_i, 0.0, None, ALU.max).then_inc(ramps_done, 1)
                    nc.vector.tensor_copy(ramp, ramp_i).then_inc(ramps_done, 1)
                    dve.wait_ge(ld_loaded, 16 * (1 + J))
                    nc.vector.tensor_scalar(ldn[:], ldp[:], -1.0, None, ALU.mult).then_inc(ldn_done, 1)
                    nc.vector.tensor_scalar(ld127[:], ldp[:], float(P - 1), None, ALU.mult).then_inc(ldn_done, 1)
                    for i, w in enumerate(("wk", "wq")):
                        dve.wait_ge(w_loaded[1 - i], 16)
                        for k in range(K):
                            nc.vector.tensor_copy(w_hi[w][:, k, :], wraw[i][k]).then_inc(wqk_hi_done, 1)
                        for k in range(K):
                            dve.wait_ge(wqk_hi_done, i * K + k + 1)
                            nc.vector.tensor_tensor(w_lo[w][:, k, :], wraw[i][k], f32v(w_hi[w][:, k, :]),
                                                    ALU.subtract).then_inc(wqk_lo_done, 1)
                    dve.wait_ge(small_loaded, 16)
                    dve.wait_ge(w_loaded[3], 16 * K)
                    for k in range(K):
                        nc.vector.tensor_scalar(wraw[3][k], wraw[3][k], nw_p[:, k:k + 1], GROUP_SCALE ** 0.5 / 16,
                                                ALU.mult, ALU.mult).then_inc(wo_scaled, 1)
                    dve.wait_ge(g1raw_loaded, 64)
                    nc.vector.tensor_copy(wg1_hi[:], g1raw).then_inc(wg_hi_done, 1)
                    dve.wait_ge(g2raw_loaded, 64)
                    nc.vector.tensor_copy(wg2_st[:], g2raw).then_inc(wg_hi_done, 1)
                    dve.wait_ge(tables_done, 1)
                    nc.vector.tensor_copy(cdec[:], qdec[:, :, P - 1:P].to_broadcast([P, G, HD])).then_inc(tables_done, 1)

                    def prep(b, r):
                        dve.wait_ge(raw_loaded, 16 * (b * PREP + r + 1))
                        nc.vector.tensor_scalar(magic[:].bitcast(U32), raw[:].bitcast(U32), 0x7F800000, None,
                                                ALU.bitwise_and).then_inc(magic_exp, 1)
                        dve.wait_ge(magic_exp, b * PREP + r + 1)
                        nc.vector.tensor_scalar(magic[:], magic[:], 2.0 ** -6, 1.5 * 2.0 ** 20, ALU.max, ALU.mult
                                                ).then_inc(magic_ready, 1)

                    def project(b, part, first, last):
                        if part == "x":
                            for t in range(C):
                                dve.wait_ge(xth_done, b * C + t + 1)
                                sl = (slice(None), slice(None), slice(t * P, (t + 1) * P))
                                nc.vector.tensor_tensor(xt_lo[sl], bank[t % 2][:].rearrange("p (k c) -> p k c", k=K),
                                                        f32v(xt_hi[sl]), ALU.subtract).then_inc(pa_done, 1)
                        elif part == "g1":
                            dve.wait_ge(g1h_done, b + 1)
                            q = slice(HD, 2 * HD)
                            nc.vector.tensor_tensor(g1_st[q, :], bank[0][q, :], f32v(g1_st[q, :]), ALU.subtract)
                            q = slice(3 * HD, 4 * HD)
                            nc.vector.tensor_tensor(g1_st[q, :], bank[0][q, :], f32v(g1_st[q, :]), ALU.subtract
                                                    ).then_inc(pa_done, 1)
                        else:
                            for n in range(first, last):
                                dve.wait_ge(tanh_done, b * 12 + n - 4 + 1)
                                if n < 12:
                                    dst = (qt, kt)[n % 2][:, (n - 4) // 2, :]
                                else:
                                    dst = v[:, n - 12, :]
                                nc.vector.scalar_tensor_tensor(out=dst, in0=prob_slot(n % 2), scalar=1.0,
                                                               in1=bank[n % 2][:], op0=ALU.add, op1=ALU.mult
                                                               ).then_inc(pa_done, 1)
                                if n % 2 == 1:
                                    prep(b, (n - 5) // 2)

                    def step(b, s):
                        if s == 0 and not isinstance(b, int):
                            dve.wait_ge(masks_done, H)
                            dve.wait_ge(blocks_step, 3)
                            dve.wait_ge(tables_done, 2)
                        for j in range(J):
                            if s < C:
                                dve.wait_ge(sc_ps, b * 16 + s * 4 + j + 1)
                                if s >= 1:
                                    dve.wait_ge(pv_done, b * 16 + (s - 1) * 4 + j + 1)
                                nc.vector.tensor_tensor(prob_slot(j), bank[2 + j % 2][:],
                                                        decay[:, j, :, :].rearrange("p g c -> p (g c)"),
                                                        ALU.mult).then_inc(probs_done, 1)
                        c = s - 1
                        if 0 <= c <= 2:
                            n = 17 + c
                            dve.wait_ge(pa_ps, pa_result(b, n))
                            if c == 0:
                                nc.vector.tensor_copy(state[:], bank[n % 2][:, 0:G * HD]).then_inc(state_new, 1)
                            else:
                                nc.vector.tensor_tensor(state_d[:], state[:], cdec[:].rearrange("p g e -> p (g e)"),
                                                        ALU.mult).then_inc(state_decayed, 1)
                                dve.wait_ge(state_decayed, b * 2 + c)
                                nc.vector.tensor_tensor(state[:], bank[n % 2][:, 0:G * HD], state_d[:], ALU.add
                                                        ).then_inc(state_new, 1)
                            dve.wait_ge(state_new, b * 3 + c + 1)
                            nc.vector.tensor_tensor(
                                state_bd[:].rearrange("p g (j e) -> p g j e", j=J),
                                state[:].rearrange("p (g e) -> p g e", g=G).unsqueeze(2).to_broadcast([P, G, J, HD]),
                                blocks_of_4[:].unsqueeze(1).to_broadcast([P, G, J, HD]), ALU.mult
                                ).then_inc(pa_done, 1)
                        if 0 <= c < C:
                            dve.wait_ge(b5_done, 1 + b * B5_USES + b5_use(c) + 1)
                            dve.wait_ge(pv_done, b * 16 + 4 * c + 4)
                            if c >= 2:
                                dve.wait_ge(ot_ps, b * C + c - 1)
                            nc.vector.scalar_tensor_tensor(out=og[:, c % 2, :], in0=gt[:], scalar=1.0,
                                                           in1=bank[4][:], op0=ALU.add, op1=ALU.mult
                                                           ).then_inc(og_done, 1)
                            dve.wait_ge(sq_ready, b * C + c + 1)
                            nc.vector.tensor_reduce(ss[:], osq[:].rearrange("p (h d) -> p h d", d=HD), AX_X,
                                                    ALU.add).then_inc(ss_ready, 1)
                        c = s - 2
                        if 0 <= c < C:
                            dve.wait_ge(oth_done, b * C + c + 1)
                            nc.vector.tensor_tensor(ot_lo[:], bank[6][:].rearrange("p (k c) -> p k c", k=K),
                                                    f32v(ot_hi[:]), ALU.subtract).then_inc(ot_done, 1)
                        c = s - 4
                        if 0 <= c < C:
                            dve.wait_ge(rstd_ready, b * C + c + 1)
                            nc.vector.tensor_scalar(y[:, c % 2, :], y[:, c % 2, :], mv[:, 0:1], rstd[:],
                                                    ALU.subtract, ALU.mult).then_inc(x1_ready, 1)
                        c = s - 3
                        if 0 <= c < C:
                            n = b * C + c + 1
                            dve.wait_ge(wo_ps, n)
                            dve.wait_ge(xres_loaded[c % 2], 32 * b + 16 * (c // 2 + 1))
                            dve.wait_ge(x1_stored[c % 2], 32 * b + 16 * (c // 2 + 1))
                            nc.vector.tensor_tensor(y[:, c % 2, :], bank[7][:], xres[:, c % 2, :], ALU.add
                                                    ).then_inc(y_done, 1)
                            dve.wait_ge(y_done, 2 + n)
                            nc.vector.bn_stats(bst[:], y[:, c % 2, :])
                            dve.drain()
                            nc.vector.bn_aggr(mv[:], bst[:]).then_inc(mv_ready, 1)
                        if 1 <= s <= 3:
                            prep(b, 5 + s)

                    chunk_pipeline(dve, project, step)
                    dve.wait_ge(x1_ready, B * C)
                    dve.sem_inc(phase1_done, 1)

        phase2(nc, sem, sb, bank, ident, wgu, wdn, neg_half, eps_tile, xin, raw, phase1_done, xw_loaded, cn_loaded,
               x1_dram, ctx_t, out_t, xbq, xbk, gate_s, up_s, down_s)


def phase2(nc, sem, sb, bank, ident, wgu, wdn, neg_half, eps_tile, xin, raw, phase1_done, xw_loaded, cn_loaded,
           x1_dram, ctx_t, out_t, xbq, xbk, gate_s, up_s, down_s):
    with ExitStack() as ph:
        def s2(name, shape, dt=F32):
            return sb(name, shape, dt, ph)

        xw_raw = raw[:].rearrange("p (i c) -> p i c", i=2)
        xw_hi = s2("xw_hi", [P, 2, KC, P], F32R)
        xw_lo = s2("xw_lo", [P, 2, KC, P], F32R)
        xb = s2("xb", [P, 2])
        gs, us = s2("gs", [P, FT]), s2("us", [P, FT])
        tanh_scale, fuse_scale, back = s2("tanh_scale", [P, FT]), s2("fuse_scale", [P, FT]), s2("back", [P, FT])
        sc = s2("sc", [P, 6, FT])
        norms = s2("norms", [P, 2 * FT])
        half = s2("half", [P, FT])
        ones = s2("ones", [P, 1], BF16)
        one = s2("one", [P, 1])
        down_b = s2("down_b", [P, D])

        cn = xin[:].rearrange("p a d -> p (a d)").rearrange("p (t c) -> p t c", t=C)
        ct_hi, ct_lo = s2("ct_hi", [P, KC, N], F32R), s2("ct_lo", [P, KC, N], F32R)
        qk_hi, qk_lo = s2("qk_hi", [P, 2, N], F32R), s2("qk_lo", [P, 2, N], F32R)
        x1n = s2("x1n", [P, C, D])
        x1t_hi, x1t_lo = s2("x1t_hi", [P, K, N], F32R), s2("x1t_lo", [P, K, N], F32R)
        att = s2("att", [P, C, N])
        att_hi, att_lo = s2("att_hi", [P, K, N], F32R), s2("att_lo", [P, K, N], F32R)
        nmax, esum, einv = s2("nmax", [P, C]), s2("esum", [P, C]), s2("einv", [P, C])
        x2n, x2k = s2("x2n", [P, C, D]), s2("x2k", [P, C, D])
        x2t_hi, x2t_lo = s2("x2t_hi", [P, K, N], F16), s2("x2t_lo", [P, K, N], F16)
        th, tu, fu = s2("th", [P, 2, N]), s2("tu", [P, 2, N]), s2("fu", [P, 2, N])
        fu_hi, fu_lo = s2("fu_hi", [P, FT, N], F16), s2("fu_lo", [P, FT, N], F16)
        y3 = s2("y3", [P, C, D])
        bst2, bst3 = s2("bst2", [P, 6]), s2("bst3", [P, 6])
        mv2, mv3 = s2("mv2", [P, C, 2]), s2("mv3", [P, C, 2])
        ve2, ve3 = s2("ve2", [P, C]), s2("ve3", [P, C])
        rstd2, rstd3 = s2("rstd2", [P, C]), s2("rstd3", [P, C])

        sc_loaded, xb_loaded = sem("sc_loaded"), sem("xb_loaded")
        x1_loaded = [sem(f"x1n{t}_loaded") for t in range(C)]
        out_stored = [sem(f"out{t}_stored") for t in range(C)]
        xw_ps, xwh_done, xw_done = sem("xw_ps"), sem("xwh_done"), sem("xw_done")
        const2, norms_done = sem("const2"), sem("norms_done")
        sq_pool, sq_act, sq_dve = sem("sq_pool"), sem("sq_act"), sem("sq_dve")
        sc_step, sqrt_done, scales_done, wdn_done = sem("sc_step"), sem("sqrt_done"), sem("scales_done"), sem("wdn_done")
        xp_ps, xp_done, xhi_done, exp_done = sem("xp_ps"), sem("xp_done"), sem("xhi_done"), sem("exp_done")
        nmax_ready, einv_ready = sem("nmax_ready"), sem("einv_ready")
        mv2_ready, ve2_ready, rstd2_ready = sem("mv2_ready"), sem("ve2_ready"), sem("rstd2_ready")
        x2_ready, x2k_ready = sem("x2_ready"), sem("x2k_ready")
        g_ps, u_ps, th_done, tu_done, gu_done = sem("g_ps"), sem("u_ps"), sem("th_done"), sem("tu_done"), sem("gu_done")
        fhi_done, flo_done, dn_ps, dn_done = sem("fhi_done"), sem("flo_done"), sem("dn_ps"), sem("dn_done")
        y3_ready, mv3_ready, ve3_ready = sem("y3_ready"), sem("mv3_ready"), sem("ve3_ready")
        rstd3_ready, out_ready = sem("rstd3_ready"), sem("out_ready")

        SQ = 2 * 3 * K

        def sq_piece(n):
            i, f4, k = n // (3 * K), n // K % 3, n % K
            dst = (fu_hi, fu_lo)[n // FT][:, n % FT, :].bitcast(BF16)
            return dst, wgu[:, i, k, f4 * 512:(f4 + 1) * 512]

        CT, QK, X1T, EN, AT, XM, X2T = 0, KC, KC + 2, KC + 6, KC + 10, KC + 14, KC + 18
        XHI = 2 + 2 + 3 * 4

        def xp(n):
            return bank[6 + n % 2]

        def xp_result(b, n):
            return XP_USES * b + n + 1

        def xp_free(b, n):
            return XP_USES * b + n + 1

        def xp_read(b, n):
            return 2 + XP_USES * b + n + 1

        def hi_index(n):
            if n < EN:
                return n
            return n - 4 if n < XM else n - 8

        def xhi(b, n):
            return XHI * b + hi_index(n) + 1

        X_STAGES = [("ctx",), ("qk",), ("x1t", 0, 1), ("x1t", 2, 3), ("en", 0, 1), ("en", 2, 3),
                    ("at", 0, 1), ("at", 2, 3), ("xm", 0), ("xm", 1), ("xm", 2), ("xm", 3),
                    ("x2t", 0, 1), ("x2t", 2, 3)]

        def schedule(x_stage, inner_tile, down_tile, fi, xb_):
            for f in range(FT + C):
                if fi is not None:
                    if f < FT:
                        inner_tile(fi, f)
                    else:
                        down_tile(fi, f - FT)
                if xb_ is not None and f < len(X_STAGES):
                    x_stage(xb_, X_STAGES[f])

        def pipeline(eng, x_stage, inner_tile, down_tile):
            schedule(x_stage, inner_tile, down_tile, None, 0)
            with eng.Fori(0, B - 1) as i:
                schedule(x_stage, inner_tile, down_tile, i, i + 1)
            schedule(x_stage, inner_tile, down_tile, B - 1, None)

        with nc.Block() as block:

            @block.sync
            def _(sp):
                sp.wait_ge(phase1_done, 5)
                for t in range(C):
                    sp.dma_start(x1n[:, t, :], x1_dram[t]).then_inc(x1_loaded[t], 16)
                sp.dma_start(xb[:, 0:1], xbq.rearrange("(p a) -> p a", a=1)).then_inc(xb_loaded, 16)
                sp.dma_start(xb[:, 1:2], xbk.rearrange("(p a) -> p a", a=1)).then_inc(xb_loaded, 16)
                sp.dma_start(gs[:], gate_s.rearrange("(f p) -> p f", p=P), allow_slow_non_contiguous=True).then_inc(sc_loaded, 16)
                sp.dma_start(us[:], up_s.rearrange("(f p) -> p f", p=P), allow_slow_non_contiguous=True).then_inc(sc_loaded, 16)
                sp.dma_start(down_b[:], down_s.rearrange("(a n) -> a n", a=1).to_broadcast([P, D])
                             ).then_inc(sc_loaded, 16)

                def store(i, t):
                    sp.wait_ge(out_ready, i * C + t + 1)
                    sp.dma_start(out_t[i * C + t], y3[:, t, :]).then_inc(out_stored[t], 16)

                with sp.Fori(0, B - 1) as i:
                    sp.wait_ge(xp_ps, xp_result(i, CT + KC - 1))
                    sp.dma_start(cn[:], ctx_t[i + 1]).then_inc(cn_loaded, 16)
                    for t in range(C):
                        sp.wait_ge(xp_done, xp_read(i, XM + t))
                        sp.dma_start(x1n[:, t, :], x1_dram[(i + 1) * C + t]).then_inc(x1_loaded[t], 16)
                    for t in range(C):
                        store(i, t)
                for t in range(C):
                    store(B - 1, t)
                for t in range(C):
                    sp.wait_ge(out_stored[t], 16 * (B + 1))

            @block.gpsimd
            def _(pool):
                pool.wait_ge(phase1_done, 5)
                pool.sem_inc(flo_done, 2)
                nc.gpsimd.memset(ones[:], 1.0).then_inc(const2, 1)
                nc.gpsimd.memset(half[:], 0.5).then_inc(const2, 1)
                nc.gpsimd.memset(one[:], 1.0).then_inc(const2, 1)
                pool.wait_ge(const2, 3)
                for n in range(0, SQ // 3):
                    dst, w = sq_piece(n)
                    nc.gpsimd.tensor_tensor(dst, w, w, ALU.mult).then_inc(sq_pool, 1)

                def rstd_op(mv, ve, rstd, t, mv_sem, ve_sem, rstd_sem, n):
                    pool.wait_ge(mv_sem, n)
                    nc.gpsimd.tensor_tensor(ve[:, t:t + 1], mv[:, t, 1:2], eps_tile[:], ALU.add
                                            ).then_inc(ve_sem, 1)
                    pool.wait_ge(ve_sem, n)
                    nc.gpsimd.tensor_tensor(rstd[:, t:t + 1], ve[:, t:t + 1], neg_half[:, 0:1], ALU.pow
                                            ).then_inc(rstd_sem, 1)

                def x_stage(b, st):
                    if st[0] == "xm":
                        rstd_op(mv2, ve2, rstd2, st[1], mv2_ready, ve2_ready, rstd2_ready, b * C + st[1] + 1)
                        if isinstance(b, int) and st[1] == C - 1:
                            pool.wait_ge(sc_step, 6)
                            nc.gpsimd.tensor_tensor(sc[:, 2, :], sc[:, 1, :], half[:], ALU.pow).then_inc(sqrt_done, 1)

                def inner_tile(i, f):
                    if f == 0:
                        for t in range(C):
                            pool.wait_ge(x2_ready, i * C + t + 1)
                            nc.gpsimd.tensor_tensor(x2k[:, t, :], x2n[:, t, :], one[:].to_broadcast([P, D]), ALU.mult
                                                    ).then_inc(x2k_ready, 1)
                    pool.wait_ge(fhi_done, i * FT + f + 1)
                    nc.gpsimd.tensor_tensor(fu_lo[:, f, :], fu[:, f % 2, :], fu_hi[:, f, :], ALU.subtract
                                            ).then_inc(flo_done, 1)

                def down_tile(i, t):
                    n = i * C + t + 1
                    pool.wait_ge(dn_done, 2 + n)
                    nc.gpsimd.tensor_tensor(y3[:, t, :], y3[:, t, :], x2k[:, t, :], ALU.add).then_inc(y3_ready, 1)
                    rstd_op(mv3, ve3, rstd3, t, mv3_ready, ve3_ready, rstd3_ready, n)

                pipeline(pool, x_stage, inner_tile, down_tile)

            @block.scalar
            def _(act):
                act.wait_ge(phase1_done, 5)
                act.wait_ge(xw_ps, 1)
                for i in range(2):
                    nc.scalar.activation(xw_hi[:, i, :, :],
                                         bank[5][:, i * CTX:(i + 1) * CTX].rearrange("p (k c) -> p k c", k=KC),
                                         ACT.Copy, scale=(-1.0, 1.0)[i]).then_inc(xwh_done, 1)

                def squares():
                    for n in range(SQ // 3, 2 * SQ // 3):
                        dst, w = sq_piece(n)
                        nc.scalar.activation(dst, w, ACT.Square).then_inc(sq_act, 1)

                def high(b, n, dst, src, **kw):
                    act.wait_ge(xp_ps, xp_result(b, n))
                    nc.scalar.activation(dst, src, **kw).then_inc(xhi_done, 1)

                def blocks(n):
                    return xp(n)[:].rearrange("p (k c) -> p k c", k=K)

                def x_stage(b, st):
                    if st[0] == "ctx":
                        for k in range(KC):
                            high(b, CT + k, ct_hi[:, k, :], xp(CT + k)[:], func=ACT.Copy)
                        if isinstance(b, int):
                            squares()
                    elif st[0] == "qk":
                        for i in range(2):
                            high(b, QK + i, qk_hi[:, i, :], xp(QK + i)[:], func=ACT.Identity, bias=xb[:, i:i + 1])
                    elif st[0] == "x1t":
                        for t in st[1:]:
                            high(b, X1T + t, x1t_hi[:, :, t * P:(t + 1) * P], blocks(X1T + t), func=ACT.Copy)
                    elif st[0] == "en":
                        for m in st[1:]:
                            act.wait_ge(nmax_ready, b * C + m + 1)
                            nc.scalar.activation(att[:, m, :], xp(EN + m)[:], ACT.Exp, scale=-1.0,
                                                 bias=nmax[:, m:m + 1], accum_out=esum[:, m:m + 1]
                                                 ).then_inc(exp_done, 1)
                    elif st[0] == "at":
                        for m in st[1:]:
                            high(b, AT + m, att_hi[:, :, m * P:(m + 1) * P], blocks(AT + m), func=ACT.Copy)
                    elif st[0] == "x2t":
                        for t in st[1:]:
                            high(b, X2T + t, x2t_hi[:, :, t * P:(t + 1) * P], blocks(X2T + t), func=ACT.Copy,
                                 scale=X2_SCALE)

                def fuse_high(i, f):
                    act.wait_ge(gu_done, 2 + i * FT + f + 1)
                    nc.scalar.activation(fu_hi[:, f, :], fu[:, f % 2, :], ACT.Copy).then_inc(fhi_done, 1)

                def inner_tile(i, f):
                    if f == 0:
                        act.wait_ge(scales_done, 2)
                    act.wait_ge(g_ps, i * FT + f + 1)
                    nc.scalar.activation(th[:, f % 2, :], bank[f % 2][:], ACT.Tanh, scale=tanh_scale[:, f:f + 1]
                                         ).then_inc(th_done, 1)
                    if f >= 1:
                        fuse_high(i, f - 1)
                    if f == FT - 1:
                        fuse_high(i, f)

                def down_tile(i, t):
                    pass

                pipeline(act, x_stage, inner_tile, down_tile)

            @block.tensor
            def _(pe):
                pe.wait_ge(phase1_done, 5)
                pe.wait_ge(xw_loaded, 32)
                for i in range(2):
                    for k in range(KC):
                        mm = nc.tensor.transpose(bank[5][:, (i * KC + k) * P:(i * KC + k + 1) * P],
                                                 xw_raw[:, i, k * P:(k + 1) * P], ident[:])
                mm.then_inc(xw_ps, 1)

                def column_norms():
                    pe.wait_ge(const2, 3)
                    for n in range(SQ):
                        pe.wait_ge((sq_pool, sq_act, sq_dve)[n // (SQ // 3)], n % (SQ // 3) + 1)
                        i, f4, k = n // (3 * K), n // K % 3, n % K
                        for f in range(4):
                            col = (k * 2 + i) * FT + f4 * 4 + f
                            mm = nc.tensor.matmul(bank[4][:, col:col + 1], sq_piece(n)[0][:, f * P:(f + 1) * P],
                                                  ones[:], start=True, stop=True)
                    mm.then_inc(norms_done, 1)

                def three(out_, a_hi, a_lo, b_hi, b_lo, ks):
                    for k in ks:
                        for q, (a, bb) in enumerate(((a_hi, b_hi), (a_hi, b_lo), (a_lo, b_hi))):
                            mm = nc.tensor.matmul(out_, a(k), bb(k), start=(k == 0 and q == 0),
                                                  stop=(k == len(ks) - 1 and q == 2))
                            del bb
                    return mm

                def turn(b, n, src, ks):
                    pe.wait_ge(xp_done, xp_free(b, n))
                    for k in ks:
                        mm = nc.tensor.transpose(xp(n)[:, k * P:(k + 1) * P], src(k), ident[:])
                    mm.then_inc(xp_ps, 1)

                def x_stage(b, st):
                    if st[0] == "ctx":
                        pe.wait_ge(cn_loaded, 16 * (b + 1))
                        for k in range(KC):
                            turn(b, CT + k, lambda t: cn[:, t, k * P:(k + 1) * P], range(C))
                    elif st[0] == "qk":
                        if isinstance(b, int):
                            pe.wait_ge(xw_done, 2)
                        pe.wait_ge(xp_done, xp_read(b, CT + KC - 1))
                        for i in range(2):
                            pe.wait_ge(xp_done, xp_free(b, QK + i))
                            three(xp(QK + i)[:], lambda k: xw_hi[:, i, k, :], lambda k: xw_lo[:, i, k, :],
                                  lambda k: ct_hi[:, k, :], lambda k: ct_lo[:, k, :], range(KC)).then_inc(xp_ps, 1)
                    elif st[0] == "x1t":
                        for t in st[1:]:
                            pe.wait_ge(x1_loaded[t], 16 * (b + 1))
                            turn(b, X1T + t, lambda k: x1n[:, t, k * P:(k + 1) * P], range(K))
                    elif st[0] == "en":
                        if st[1] == 0:
                            pe.wait_ge(xp_done, xp_read(b, QK + 1))
                        elif isinstance(b, int):
                            column_norms()
                        for m in st[1:]:
                            pe.wait_ge(xp_done, xp_free(b, EN + m))
                            mc = slice(m * P, (m + 1) * P)
                            three(xp(EN + m)[:], lambda k: qk_hi[:, 0, mc], lambda k: qk_lo[:, 0, mc],
                                  lambda k: qk_hi[:, 1, :], lambda k: qk_lo[:, 1, :], range(1)).then_inc(xp_ps, 1)
                    elif st[0] == "at":
                        for m in st[1:]:
                            pe.wait_ge(xp_done, xp_read(b, EN + m))
                            turn(b, AT + m, lambda k: att[:, m, k * P:(k + 1) * P], range(K))
                    elif st[0] == "xm":
                        t = st[1]
                        if t == 0:
                            pe.wait_ge(xp_done, xp_read(b, AT + C - 1))
                        pe.wait_ge(xp_done, xp_free(b, XM + t))
                        tc = slice(t * P, (t + 1) * P)
                        three(xp(XM + t)[:], lambda k: x1t_hi[:, k, tc], lambda k: x1t_lo[:, k, tc],
                              lambda k: att_hi[:, k, :], lambda k: att_lo[:, k, :], range(K)).then_inc(xp_ps, 1)
                    elif st[0] == "x2t":
                        for t in st[1:]:
                            pe.wait_ge(x2_ready, b * C + t + 1)
                            turn(b, X2T + t, lambda k: x2n[:, t, k * P:(k + 1) * P], range(K))

                def inner_tile(i, f):
                    if f == 0:
                        pe.wait_ge(xp_done, xp_read(i, X2T + C - 1))
                    pe.wait_ge(gu_done, i * FT + f + 1)
                    for w, (first_bank, ready) in enumerate(((0, g_ps), (2, u_ps))):
                        for k in range(K):
                            for q, xt in enumerate((x2t_hi, x2t_lo)):
                                mm = nc.tensor.matmul(bank[first_bank + f % 2][:], wgu[:, w, k, f * P:(f + 1) * P],
                                                      xt[:, k, :], start=(k + q == 0), stop=(k == K - 1 and q == 1))
                        mm.then_inc(ready, 1)

                def down_tile(i, t):
                    if t == 0:
                        pe.wait_ge(flo_done, 2 + i * FT + FT)
                        pe.wait_ge(wdn_done, FT)
                    pe.wait_ge(dn_done, i * C + t + 1)
                    for f in range(FT):
                        for q, fa in enumerate((fu_hi, fu_lo)):
                            mm = nc.tensor.matmul(bank[4 + t % 2][:], fa[:, f, t * P:(t + 1) * P], wdn[:, f, :],
                                                  start=(f + q == 0), stop=(f == FT - 1 and q == 1))
                    mm.then_inc(dn_ps, 1)

                pipeline(pe, x_stage, inner_tile, down_tile)

            @block.vector
            def _(dve):
                dve.wait_ge(phase1_done, 5)
                dve.sem_inc(xp_done, 2)
                dve.sem_inc(gu_done, 2)
                dve.sem_inc(dn_done, 2)
                for t in range(C):
                    dve.sem_inc(out_stored[t], 16)
                dve.wait_ge(xwh_done, 2)
                for i in range(2):
                    src = bank[5][:, i * CTX:(i + 1) * CTX].rearrange("p (k c) -> p k c", k=KC)
                    nc.vector.scalar_tensor_tensor(out=xw_lo[:, i, :, :], in0=src, scalar=(-1.0, 1.0)[i],
                                                   in1=f32v(xw_hi[:, i, :, :]), op0=ALU.mult, op1=ALU.subtract)
                dve.wait_ge(xb_loaded, 32)
                nc.vector.tensor_scalar(xb[:, 0:1], xb[:, 0:1], -1.0, None, ALU.mult)
                dve.drain().then_inc(xw_done, 2)

                step = [0]

                def small(ins):
                    step[0] += 1
                    ins.then_inc(sc_step, 1)
                    dve.wait_ge(sc_step, step[0])

                def finish_scales():
                    dve.wait_ge(sc_loaded, 48)
                    dve.wait_ge(norms_done, 1)
                    n4 = bank[4][:, 0:K * 2 * FT].rearrange("p (k i) -> p i k", k=K)
                    small(nc.vector.tensor_reduce(norms[:], n4, AX_X, ALU.add))
                    small(nc.vector.tensor_tensor(sc[:, 3, :], gs[:], us[:], ALU.mult))
                    small(nc.vector.tensor_tensor(sc[:, 0, :], norms[:, 0:FT], norms[:, FT:2 * FT], ALU.mult))
                    small(nc.vector.tensor_tensor(sc[:, 5, :], sc[:, 3, :], sc[:, 3, :], ALU.mult))
                    small(nc.vector.tensor_tensor(sc[:, 0, :], sc[:, 0, :], sc[:, 5, :], ALU.mult))
                    small(nc.vector.tensor_scalar(sc[:, 1, :], sc[:, 0, :], 2.0 ** -100, None, ALU.max))
                    dve.wait_ge(sqrt_done, 1)
                    small(nc.vector.tensor_scalar(sc[:, 4, :], sc[:, 2, :], D * 1.1, None, ALU.mult))
                    small(nc.vector.tensor_scalar(sc[:, 5, :].bitcast(U32), sc[:, 4, :].bitcast(U32), 0x7F800000, None,
                                                  ALU.bitwise_and))
                    small(nc.vector.tensor_scalar(back[:], sc[:, 5, :], 2.0 / FUSE_TOP, None, ALU.mult))
                    small(nc.vector.reciprocal(sc[:, 0, :], back[:]))
                    small(nc.vector.tensor_scalar(sc[:, 1, :], sc[:, 3, :], 0.5 / X2_SCALE ** 2, None, ALU.mult))
                    nc.vector.tensor_scalar(tanh_scale[:], gs[:], 0.5 / X2_SCALE, None, ALU.mult
                                            ).then_inc(scales_done, 1)
                    nc.vector.tensor_tensor(fuse_scale[:], sc[:, 0, :], sc[:, 1, :], ALU.mult).then_inc(scales_done, 1)
                    dve.wait_ge(scales_done, 2)
                    for f in range(FT):
                        nc.vector.tensor_scalar(wdn[:, f, :], wdn[:, f, :], back[:, f:f + 1], None, ALU.mult
                                                ).then_inc(wdn_done, 1)

                def low(b, n, dst, hi, src, scale=None, bias=None):
                    dve.wait_ge(xhi_done, xhi(b, n))
                    if scale is None and bias is None:
                        ins = nc.vector.tensor_tensor(dst, src, hi, ALU.subtract)
                    elif bias is None:
                        ins = nc.vector.scalar_tensor_tensor(out=dst, in0=src, scalar=scale, in1=hi, op0=ALU.mult,
                                                             op1=ALU.subtract)
                    else:
                        ins = nc.vector.scalar_tensor_tensor(out=dst, in0=src, scalar=bias, in1=hi, op0=ALU.add,
                                                             op1=ALU.subtract)
                    ins.then_inc(xp_done, 1)

                def blocks(n):
                    return xp(n)[:].rearrange("p (k c) -> p k c", k=K)

                def norm2(b, t):
                    dve.wait_ge(rstd2_ready, b * C + t + 1)
                    nc.vector.tensor_scalar(x2n[:, t, :], x2n[:, t, :], mv2[:, t, 0:1], rstd2[:, t:t + 1],
                                            ALU.subtract, ALU.mult).then_inc(x2_ready, 1)

                def x_stage(b, st):
                    if st[0] == "ctx":
                        for k in range(KC):
                            low(b, CT + k, ct_lo[:, k, :], f32v(ct_hi[:, k, :]), xp(CT + k)[:])
                        if isinstance(b, int):
                            for n in range(2 * SQ // 3, SQ):
                                dst, w = sq_piece(n)
                                nc.vector.tensor_tensor(dst, w, w, ALU.mult).then_inc(sq_dve, 1)
                    elif st[0] == "qk":
                        for i in range(2):
                            low(b, QK + i, qk_lo[:, i, :], f32v(qk_hi[:, i, :]), xp(QK + i)[:], bias=xb[:, i:i + 1])
                    elif st[0] == "x1t":
                        for t in st[1:]:
                            sl = (slice(None), slice(None), slice(t * P, (t + 1) * P))
                            low(b, X1T + t, x1t_lo[sl], f32v(x1t_hi[sl]), blocks(X1T + t))
                    elif st[0] == "en":
                        for m in st[1:]:
                            dve.wait_ge(xp_ps, xp_result(b, EN + m))
                            nc.vector.tensor_reduce(nmax[:, m:m + 1], xp(EN + m)[:], AX_X, ALU.min
                                                    ).then_inc(nmax_ready, 1)
                        for m in st[1:]:
                            dve.wait_ge(exp_done, b * C + m + 1)
                            nc.vector.reciprocal(einv[:, m:m + 1], esum[:, m:m + 1]).then_inc(einv_ready, 1)
                            dve.wait_ge(einv_ready, b * C + m + 1)
                            nc.vector.tensor_scalar(att[:, m, :], att[:, m, :], einv[:, m:m + 1], None, ALU.mult
                                                    ).then_inc(xp_done, 1)
                    elif st[0] == "at":
                        for m in st[1:]:
                            sl = (slice(None), slice(None), slice(m * P, (m + 1) * P))
                            low(b, AT + m, att_lo[sl], f32v(att_hi[sl]), blocks(AT + m))
                    elif st[0] == "xm":
                        t = st[1]
                        n = b * C + t + 1
                        dve.wait_ge(xp_ps, xp_result(b, XM + t))
                        if not isinstance(b, int):
                            dve.wait_ge(x2k_ready, n - C)
                        nc.vector.tensor_tensor(x2n[:, t, :], xp(XM + t)[:], x1n[:, t, :], ALU.add
                                                ).then_inc(xp_done, 1)
                        dve.wait_ge(xp_done, xp_read(b, XM + t))
                        nc.vector.bn_stats(bst2[:], x2n[:, t, :])
                        dve.drain()
                        nc.vector.bn_aggr(mv2[:, t, :], bst2[:]).then_inc(mv2_ready, 1)
                        if t >= 1:
                            norm2(b, t - 1)
                        if t == C - 1:
                            norm2(b, t)
                        if isinstance(b, int) and t == C - 1:
                            finish_scales()
                    elif st[0] == "x2t":
                        for t in st[1:]:
                            sl = (slice(None), slice(None), slice(t * P, (t + 1) * P))
                            low(b, X2T + t, x2t_lo[sl], x2t_hi[sl], blocks(X2T + t), scale=X2_SCALE)

                def inner_tile(i, f):
                    n = i * FT + f + 1
                    dve.wait_ge(th_done, n)
                    nc.vector.scalar_tensor_tensor(out=tu[:, f % 2, :], in0=th[:, f % 2, :], scalar=1.0,
                                                   in1=bank[f % 2][:], op0=ALU.add, op1=ALU.mult).then_inc(tu_done, 1)
                    dve.wait_ge(tu_done, n)
                    dve.wait_ge(u_ps, n)
                    dve.wait_ge(flo_done, n)
                    nc.vector.scalar_tensor_tensor(out=fu[:, f % 2, :], in0=bank[2 + f % 2][:],
                                                   scalar=fuse_scale[:, f:f + 1], in1=tu[:, f % 2, :],
                                                   op0=ALU.mult, op1=ALU.mult).then_inc(gu_done, 1)

                def norm3(i, t):
                    dve.wait_ge(rstd3_ready, i * C + t + 1)
                    nc.vector.tensor_scalar(y3[:, t, :], y3[:, t, :], mv3[:, t, 0:1], rstd3[:, t:t + 1],
                                            ALU.subtract, ALU.mult).then_inc(out_ready, 1)

                def stats3(i, t):
                    n = i * C + t + 1
                    dve.wait_ge(y3_ready, n)
                    nc.vector.bn_stats(bst3[:], y3[:, t, :])
                    dve.drain()
                    nc.vector.bn_aggr(mv3[:, t, :], bst3[:]).then_inc(mv3_ready, 1)

                def down_tile(i, t):
                    n = i * C + t + 1
                    dve.wait_ge(dn_ps, n)
                    dve.wait_ge(out_stored[t], 16 * (i + 1))
                    nc.vector.tensor_tensor(y3[:, t, :], bank[4 + t % 2][:], down_b[:], ALU.mult
                                            ).then_inc(dn_done, 1)
                    if t >= 1:
                        stats3(i, t - 1)
                    if t >= 2:
                        norm3(i, t - 2)
                    if t == C - 1:
                        stats3(i, t)
                        norm3(i, t - 1)
                        norm3(i, t)

                pipeline(dve, x_stage, inner_tile, down_tile)


_INS = ['x', 'ctx_1024', 'L0_attn_log_decay', 'L0_attn_Wq', 'L0_attn_Wk', 'L0_attn_Wv', 'L0_attn_Wo',
        'L0_attn_Wg1', 'L0_attn_Wg2', 'L0_attn_norm_w', 'L0_xattn_Wq', 'L0_xattn_bq', 'L0_xattn_Wk',
        'L0_xattn_bk', 'L0_ffn_gate_w', 'L0_ffn_up_w', 'L0_ffn_down_w', 'L0_ffn_gate_scale',
        'L0_ffn_up_scale', 'L0_ffn_down_scale']


def kernel(**inputs):
    import numpy as _np
    import concourse.bacc as _bacc
    from concourse import mybir as _mybir
    from concourse.bass_utils import run_bass_kernel_spmd as _run

    nc = _bacc.Bacc("TRN2", target_bir_lowering=False, num_devices=1)
    arrays, args = {}, []
    for name in _INS:
        a = _np.ascontiguousarray(inputs[name])
        arrays[f"in_{name}_dram"] = a
        args.append(nc.dram_tensor(f"in_{name}_dram", a.shape, _mybir.dt.from_np(a.dtype), kind="ExternalInput").ap())
    args.append(nc.dram_tensor("out_0_dram", (B, N, D), _mybir.dt.float32, kind="ExternalOutput").ap())
    build(nc, *args)
    r = _run(nc, [arrays], core_ids=[0])
    return r.results[0]["out_0_dram"]
```

```python
from contextlib import ExitStack

import concourse.bass as bass
from concourse import mybir

F32 = mybir.dt.float32
F32R = mybir.dt.float32r
F16 = mybir.dt.float16
BF16 = mybir.dt.bfloat16
U32 = mybir.dt.uint32
I32 = mybir.dt.int32
ALU = mybir.AluOpType
ACT = mybir.ActivationFunctionType
AX_X = mybir.AxisListType.X

P = 128
B, N, D = 4, 512, 512
H, HD = 16, 32
C = N // P
K = D // P
G = K
J = P // HD
CTX = 256
KC = CTX // P
FF = 1536
FT = FF // P
EPS = 1e-5

X2_SCALE = 1024.0
FUSE_TOP = 2.0 ** 15

GROUP_SCALE = HD * 256.0

PA_USES = C + C + 2 * G
B5_USES = 1 + 3 * G
XP_USES = 24
PREP = 9


def f32v(ap):
    return ap.bitcast(F32)


def build(nc, x, ctx_in, ld, wq, wk, wv, wo, wg1, wg2, nw, xwq, xbq, xwk, xbk,
          gate_w, up_w, down_w, gate_s, up_s, down_s, out):
    x_t = x.rearrange("b (t p) d -> (b t) p d", p=P)
    out_t = out.rearrange("b (t p) d -> (b t) p d", p=P)
    x1_dram = nc.dram_tensor("x1_scratch", (B * C, P, D), F32, kind="Internal").ap()
    ctx_t = ctx_in.rearrange("b (t p) d -> b p t d", p=P)
    gate_t = gate_w.rearrange("(k p) f -> k p f", p=P)
    up_t = up_w.rearrange("(k p) f -> k p f", p=P)
    down_t = down_w.rearrange("(k p) f -> k p f", p=P)

    with ExitStack() as top:
        def sem(name):
            return top.enter_context(nc.semaphore(name))

        def sb(name, shape, dt=F32, stack=top):
            return stack.enter_context(nc.sbuf_tensor(name, shape, dt))

        bank = [top.enter_context(nc.psum_tensor(f"bank{i}", [P, 512], F32)) for i in range(8)]

        ident = sb("ident", [P, P])
        wgu = sb("wgu", [P, 2, K, FF], F16)
        wdn = sb("wdn", [P, FT, D], BF16)
        neg_half = sb("neg_half", [P, H])
        eps_tile = sb("eps_tile", [P, 1])
        ones = sb("ones", [P, 1], BF16)
        one = sb("one", [P, 1])
        half = sb("half", [P, FT])

        with ExitStack() as ph:
            def s1(name, shape, dt=F32):
                return sb(name, shape, dt, ph)

            w_hi, w_lo = {}, {}
            for w in ("wq", "wk", "wv"):
                w_hi[w] = s1(f"{w}_hi", [P, K, D], F32R)
                w_lo[w] = s1(f"{w}_lo", [P, K, D], F32R)
            xt_hi = s1("xt_hi", [P, K, N], F32R)
            xt_lo = s1("xt_lo", [P, K, N], F32R)
            qb_hi = s1("qb_hi", [P, C, 2, P], F32R)
            qb_lo = s1("qb_lo", [P, C, 2, P], F32R)
            kt_hi = s1("kt_hi", [P, N], F32R)
            kt_lo = s1("kt_lo", [P, N], F32R)
            v = s1("v", [P, C, D])
            probs = s1("probs", [P, C, J, P])
            qf = s1("qf", [P, N])
            kf = s1("kf", [P, N])
            kd = s1("kd", [P, C - 1, P])
            qd = s1("qd", [P, C - 1, P])
            kn = s1("kn", [P, C - 1, P])
            g1_st = s1("g1_st", [P, N], F32R)
            gt = s1("gt", [P, C, P])
            wg1_hi = s1("wg1_hi", [P, K, P], F32R)
            wg1_lo = s1("wg1_lo", [P, K, P], F32R)
            wg2_st = s1("wg2_st", [P, D], F32R)
            state = s1("state", [P, C - 1, HD])
            state_d = s1("state_d", [P, HD])
            state_bd = s1("state_bd", [P, C - 1, J, HD])
            decay = s1("decay", [P, G, J, P])
            qdec = s1("qdec", [P, G, P])
            kdec = s1("kdec", [P, G, P])
            cdec = s1("cdec", [P, G, HD])
            blocks_of_4 = s1("blocks_of_4", [P, J, HD])
            w_hi["wo"] = s1("wo_hi", [P, K, D], F32R)
            w_lo["wo"] = s1("wo_lo", [P, K, D], F32R)
            og = s1("og", [P, C, D])
            ot_hi = s1("ot_hi", [P, K, P], F32R)
            ot_lo = s1("ot_lo", [P, K, P], F32R)
            y = s1("y", [P, 2, D])
            osq = s1("osq", [P, C, P])
            xin = s1("xin", [P, 2, D])
            raw = s1("raw", [P, 2, 512])
            magic = s1("magic", [P, 512])
            ss = s1("ss", [P, C * J])
            ss_e = s1("ss_e", [P, C * J])
            eps_group = s1("eps_group", [P, C * J])
            rs = s1("rs", [P, C * J])
            bst = s1("bst", [P, 6])
            mv = s1("mv", [P, 2])
            var_e = s1("var_e", [P, 1])
            rstd = s1("rstd", [P, 1])
            ldb = s1("ldb", [P, H])
            ldp = s1("ldp", [P, G])
            ldn = s1("ldn", [P, G])
            ld127 = s1("ld127", [P, G])
            nw_p = s1("nw_p", [P, K])
            wq_raw = wdn[:, 4:12, :].rearrange("p f d -> p (f d)").bitcast(F32).rearrange("p (k d) -> p k d", k=K)
            wk_raw = v[:]
            wv_raw = probs[:].rearrange("p c j n -> p c (j n)")
            wo_raw = og[:]
            g1raw = y[:, 0, :].rearrange("p (k m) -> p k m", k=K)
            g2raw = y[:, 1, :]
            diff_i = osq[:, 0, :].bitcast(I32)
            diff = osq[:, 1, :]
            ramp_i = qd[:, 0, :].bitcast(I32)
            ramp = qd[:, 1, :]

            wq_loaded, wk_loaded, wv_loaded, wo_loaded = (
                sem("wq_loaded"), sem("wk_loaded"), sem("wv_loaded"), sem("wo_loaded"))
            small_loaded = sem("small_loaded")
            g1raw_loaded, g2raw_loaded, ld_loaded = sem("g1raw_loaded"), sem("g2raw_loaded"), sem("ld_loaded")
            const_done, iota_done, tables_done, masks_exp = (
                sem("const_done"), sem("iota_done"), sem("tables_done"), sem("masks_exp"))
            masks_done, ramps_done, wo_scaled = sem("masks_done"), sem("ramps_done"), sem("wo_scaled")
            wqk_hi_done, wqk_lo_done, wvo_hi_done, wg_hi_done, wlo_done = (
                sem("wqk_hi_done"), sem("wqk_lo_done"), sem("wvo_hi_done"), sem("wg_hi_done"), sem("wlo_done"))
            ident_zero, blocks_step, ldn_done, qb_zero = (
                sem("ident_zero"), sem("blocks_step"), sem("ldn_done"), sem("qb_zero"))

            xin_loaded = [sem(f"xin{i}_loaded") for i in range(2)]
            x23_loaded = [sem(f"x{2 + i}_loaded") for i in range(2)]
            y_loaded = [sem(f"y{i}_loaded") for i in range(2)]
            x1_stored = [sem(f"x1_{i}_stored") for i in range(2)]
            raw_loaded = [sem(f"raw{i}_loaded") for i in range(2)]
            magic_exp, magic_ready, raw_added, prep_done = (
                sem("magic_exp"), sem("magic_ready"), sem("raw_added"), sem("prep_done"))
            pa_ps, pa_done, xth_done, tanh_done = sem("pa_ps"), sem("pa_done"), sem("xth_done"), sem("tanh_done")
            b5_ps, b5_done, g1h_done = sem("b5_ps"), sem("b5_done"), sem("g1h_done")
            qhi_done, q_split, khi_done, k_split = sem("qhi_done"), sem("q_split"), sem("khi_done"), sem("k_split")
            kd_ready, qd_ready = sem("kd_ready"), sem("qd_ready")
            sc_ps, probs_done, pv_done, og_done = sem("sc_ps"), sem("probs_done"), sem("pv_done"), sem("og_done")
            state_step, state_ready = sem("state_step"), sem("state_ready")
            sq_ready, ss_ready = sem("sq_ready"), sem("ss_ready")
            ss_scaled, rs_ready, ogn_ready = sem("ss_scaled"), sem("rs_ready"), sem("ogn_ready")
            ot_ps, oth_done, ot_done, wo_ps, y_done = (
                sem("ot_ps"), sem("oth_done"), sem("ot_done"), sem("wo_ps"), sem("y_done"))
            mv_ready, var_ready, rstd_ready, x1_ready = (
                sem("mv_ready"), sem("var_ready"), sem("rstd_ready"), sem("x1_ready"))

            V0 = C + 2

            def pa_use(name, i):
                if name == "v":
                    return V0 + i
                return (C if i == 0 else V0 + C + 2 * (i - 1)) + (name == "k")

            def pa_result(b, n):
                return PA_USES * (b + 1) + n + 1

            def pa_free(b, n):
                return PA_USES * b + n + 1

            def pa_read(b, n):
                return 2 + PA_USES * b + n + 1

            G1, KN, ST, GA = 0, 1, 2, 3

            def b5_result(b, n):
                return B5_USES * b + n + 1

            def b5_free(b, n):
                return B5_USES * b + n + 1

            def b5_read(b, n):
                return 1 + B5_USES * b + n + 1

            def heads(b, nb):
                st = []
                for g in range(G):
                    if g >= 1:
                        st += [("scores", b, g, 0), ("k_turned", b, g), ("prep", b, 2 * g)]
                    st += [("state", b, g), ("scores", b, g, 1)]
                    if g >= 1:
                        st.append(("norm", b, g - 1))
                    if g < G - 1:
                        st += [("q", b, g + 1, (b, g, 0)), ("gate", b, g), ("k", b, g + 1, (b, g, 1)),
                               ("values", b, g, 2), ("values", b, g, 3), ("gated", b, g), ("prep", b, 2 * g + 1)]
                    else:
                        st.append(("prep", b, 2 * g + 1))
                    if g == G - 1 and nb is not None:
                        st += [("x", nb, 0), ("x", nb, 1), ("values", b, g, 0), ("x", nb, 2), ("x", nb, 3),
                               ("gate", b, g), ("q", nb, 0, (b, g, 1)), ("prep", b, 2 * g + 2),
                               ("k", nb, 0, (b, g, 2)), ("values", b, g, 3), ("gated", b, g)]
                return st

            def outputs_and_values(b, nb):
                outs = [[], [("turned", b, 0)], [("out", b, 0), ("turned", b, 1)], [("out", b, 1), ("turned", b, 2)],
                        [("out", b, 2), ("turned", b, 3)], [("out", b, 3), ("end", b)]]
                ins = [[("g1", nb)], [("v", nb, 0), ("prep", nb, 0), ("v", nb, 1)], [("v", nb, 2)], [("v", nb, 3)],
                       [("scores", nb, 0, 0)], [("k_turned", nb, 0)]]
                st = [("norm", b, G - 1)]
                for i in range(6):
                    st += ins[i] + outs[i]
                return st

            def first_batch_start():
                return [("setup", 0, 0), ("x", 0, 0), ("x", 0, 1), ("x", 0, 2), ("x", 0, 3), ("setup", 0, 1),
                        ("q", 0, 0, None), ("k", 0, 0, None), ("setup", 0, 2), ("v", 0, 0), ("masks", 0, 0),
                        ("prep", 0, 0), ("v", 0, 1), ("masks", 0, 1), ("v", 0, 2), ("masks", 0, 2),
                        ("v", 0, 3), ("masks", 0, 3), ("g1", 0), ("scores", 0, 0, 0), ("k_turned", 0, 0)]

            def last_batch():
                b, g = B - 1, G - 1
                st = heads(b, None)
                loads = st.index(("k", b, g, (b, g - 1, 1))) + 1
                return st[:loads] + [("X", "loads")] + st[loads:] + [
                    ("X", "weights"), ("values", b, g, 0), ("X", "ctx"), ("values", b, g, 1), ("gate", b, g),
                    ("X", "qk"), ("values", b, g, 2), ("prep", b, 2 * g + 2), ("values", b, g, 3),
                    ("X", "en", 0, 1), ("gated", b, g), ("norm", b, g), ("X", "x1t", 0, 1), ("X", "en", 2, 3),
                    ("X", "x1t", 2, 3), ("X", "at", 0, 1), ("turned", b, 0), ("X", "at", 2, 3), ("out", b, 0),
                    ("X", "squares", 0),
                    ("turned", b, 1), ("X", "xm", 0), ("out", b, 1), ("X", "squares", 1),
                    ("turned", b, 2), ("X", "xm", 1), ("out", b, 2), ("X", "squares", 2),
                    ("turned", b, 3), ("X", "squares", 3), ("X", "xm", 2), ("out", b, 3), ("end", b),
                    ("X", "xm", 3), ("X", "x2t", 0, 1), ("X", "norms"), ("X", "x2t", 2, 3), ("X", "scales")]

            def run(eng, stage, x_stage, inner_tile, down_tile):
                for st in first_batch_start():
                    stage(*st)
                with eng.Fori(0, B - 1) as i:
                    for st in heads(i, i + 1) + outputs_and_values(i, i + 1):
                        stage(*st)
                for st in last_batch():
                    if st[0] == "X":
                        x_stage(0, st[1:])
                    else:
                        stage(*st)
                pipeline(eng, x_stage, inner_tile, down_tile)

            def run_loads(sp, stage, first_loads, loop):
                for st in first_batch_start():
                    stage(*st)
                with sp.Fori(0, B - 1) as i:
                    for st in heads(i, i + 1) + outputs_and_values(i, i + 1):
                        stage(*st)
                for st in last_batch():
                    if st == ("X", "loads"):
                        first_loads()
                    elif st[0] != "X":
                        stage(*st)
                loop()

        with ExitStack() as ph:
            def s2(name, shape, dt=F32):
                return sb(name, shape, dt, ph)

            xw_raw = s2("xw_raw", [P, 2, CTX])
            cn = s2("cn", [P, C, CTX])
            xw_hi = s2("xw_hi", [P, 2, KC, P], F32R)
            xw_lo = s2("xw_lo", [P, 2, KC, P], F32R)
            xb = s2("xb", [P, 2])
            gs, us = s2("gs", [P, FT]), s2("us", [P, FT])
            tanh_scale, fuse_scale, back = s2("tanh_scale", [P, FT]), s2("fuse_scale", [P, FT]), s2("back", [P, FT])
            sc = s2("sc", [P, 6, FT])
            norms = s2("norms", [P, 2 * FT])
            ct_hi, ct_lo = s2("ct_hi", [P, KC, N], F32R), s2("ct_lo", [P, KC, N], F32R)
            qk_hi, qk_lo = s2("qk_hi", [P, 2, N], F32R), s2("qk_lo", [P, 2, N], F32R)
            x1n = s2("x1n", [P, C, D])
            att = s2("att", [P, C, N])
            att_hi, att_lo = s2("att_hi", [P, K, N], F32R), s2("att_lo", [P, K, N], F32R)
            nmax, esum, einv = s2("nmax", [P, C]), s2("esum", [P, C]), s2("einv", [P, C])
            bst2, bst3 = s2("bst2", [P, 6]), s2("bst3", [P, 6])
            mv2, mv3 = s2("mv2", [P, C, 2]), s2("mv3", [P, C, 2])
            ve2, ve3 = s2("ve2", [P, C]), s2("ve3", [P, C])
            rstd2, rstd3 = s2("rstd2", [P, C]), s2("rstd3", [P, C])
            x1t_hi, x1t_lo = s2("x1t_hi", [P, K, N], F32R), s2("x1t_lo", [P, K, N], F32R)
            x2n = s2("x2n", [P, C, D])
            x2k = s2("x2k", [P, C, D])
            x2t_hi, x2t_lo = s2("x2t_hi", [P, K, N], F16), s2("x2t_lo", [P, K, N], F16)
            fu_hi, fu_lo = s2("fu_hi", [P, FT, N], F16), s2("fu_lo", [P, FT, N], F16)
            th, tu, fu = s2("th", [P, 2, N]), s2("tu", [P, 2, N]), s2("fu", [P, 2, N])
            y3 = s2("y3", [P, C, D])
            down_b = s2("down_b", [P, D])

            xw_loaded, cn_loaded = sem("xw_loaded"), sem("cn_loaded")
            sc_loaded, xb_loaded, down_loaded = sem("sc_loaded"), sem("xb_loaded"), sem("down_loaded")
            x1_loaded = [sem(f"x1n{t}_loaded") for t in range(C)]
            out_stored = [sem(f"out{t}_stored") for t in range(C)]
            xw_ps, xwh_done, xw_done = sem("xw_ps"), sem("xwh_done"), sem("xw_done")
            const2, norms_done = sem("const2"), sem("norms_done")
            sq_pool, sq_act, sq_dve = sem("sq_pool"), sem("sq_act"), sem("sq_dve")
            back_done = sem("back_done")
            sc_step, sqrt_done, scales_done, wdn_done = sem("sc_step"), sem("sqrt_done"), sem("scales_done"), sem("wdn_done")
            xp_ps, xp_done, xhi_done, exp_done = sem("xp_ps"), sem("xp_done"), sem("xhi_done"), sem("exp_done")
            nmax_ready, einv_ready = sem("nmax_ready"), sem("einv_ready")
            mv2_ready, ve2_ready, rstd2_ready = sem("mv2_ready"), sem("ve2_ready"), sem("rstd2_ready")
            x2_ready, x2k_ready = sem("x2_ready"), sem("x2k_ready")
            g_ps, u_ps, th_done, tu_done, gu_done = sem("g_ps"), sem("u_ps"), sem("th_done"), sem("tu_done"), sem("gu_done")
            fhi_done, flo_done, dn_ps, dn_done = sem("fhi_done"), sem("flo_done"), sem("dn_ps"), sem("dn_done")
            y3_ready, mv3_ready, ve3_ready = sem("y3_ready"), sem("mv3_ready"), sem("ve3_ready")
            rstd3_ready, out_ready = sem("rstd3_ready"), sem("out_ready")

            SQ = 2 * 3 * K
            SQ_ACT, SQ_DVE = 4, 14

            def sq_piece(n):
                i, f4, k = n // (3 * K), n // K % 3, n % K
                dst = (fu_hi, fu_lo)[n // FT][:, n % FT, :].bitcast(BF16)
                return dst, wgu[:, i, k, f4 * 512:(f4 + 1) * 512]

            CT, QK, AT, XM, X2T = 0, KC, KC + 10, KC + 14, KC + 18

            def en_use(m):
                return KC + 2 + 4 * (m // 2) + m % 2

            def x1t_use(t):
                return KC + 4 + 4 * (t // 2) + t % 2

            HIGHS = ([CT + k for k in range(KC)] + [QK, QK + 1] + [x1t_use(t) for t in range(C)]
                     + [AT + m for m in range(C)] + [X2T + t for t in range(C)])

            def xp(b, n):
                return bank[(0 if isinstance(b, int) else 6) + n % 2]

            def xp_result(b, n):
                return XP_USES * b + n + 1

            def xp_free(b, n):
                return XP_USES * b + n + 1

            def xp_read(b, n):
                return 2 + XP_USES * b + n + 1

            def xhi(b, n):
                return len(HIGHS) * b + HIGHS.index(n) + 1

            X_STAGES = [[], [], [("ctx",)], [("qk",)], [("en", 0, 1), ("x1t", 0, 1)], [("en", 2, 3), ("x1t", 2, 3)],
                        [("at", 0, 1)], [("at", 2, 3)], [("xm", 0)], [("xm", 1)], [("xm", 2)], [("xm", 3)],
                        [("x2t", 0, 1)], [("x2t", 2, 3)], [], []]

            def schedule(x_stage, inner_tile, down_tile, fi, xb_):
                for f in range(FT + C):
                    if fi is not None:
                        if f < FT:
                            inner_tile(fi, f)
                        else:
                            down_tile(fi, f - FT)
                    if xb_ is not None:
                        for st in X_STAGES[f]:
                            x_stage(xb_, st)

            def pipeline(eng, x_stage, inner_tile, down_tile):
                with eng.Fori(0, B - 1) as i:
                    schedule(x_stage, inner_tile, down_tile, i, i + 1)
                schedule(x_stage, inner_tile, down_tile, B - 1, None)

            def sync_phase2(sp):
                def first_loads():
                    sp.wait_ge(pa_ps, PA_USES * (B + 1))
                    sp.dma_start(xw_raw[:, 0, :], xwq).then_inc(xw_loaded, 16)
                    sp.dma_start(xw_raw[:, 1, :], xwk).then_inc(xw_loaded, 16)
                    sp.dma_start(cn[:], ctx_t[0]).then_inc(cn_loaded, 16)
                    for s in x1_stored:
                        sp.wait_ge(s, 16 + 32)
                    for t in range(C):
                        sp.dma_start(x1n[:, t, :], x1_dram[t]).then_inc(x1_loaded[t], 16)
                    sp.dma_start(xb[:, 0:1], xbq.rearrange("(p a) -> p a", a=1)).then_inc(xb_loaded, 16)
                    sp.dma_start(xb[:, 1:2], xbk.rearrange("(p a) -> p a", a=1)).then_inc(xb_loaded, 16)
                    sp.dma_start(gs[:], gate_s.rearrange("(f p) -> p f", p=P), allow_slow_non_contiguous=True).then_inc(sc_loaded, 16)
                    sp.dma_start(us[:], up_s.rearrange("(f p) -> p f", p=P), allow_slow_non_contiguous=True).then_inc(sc_loaded, 16)

                def store(i, t):
                    sp.wait_ge(out_ready, i * C + t + 1)
                    sp.dma_start(out_t[i * C + t], y3[:, t, :]).then_inc(out_stored[t], 16)

                def loop():
                    sp.wait_ge(x1_ready, B * C)
                    sp.dma_start(down_b[:], down_s.rearrange("(a n) -> a n", a=1).to_broadcast([P, D])
                                 ).then_inc(down_loaded, 16)
                    for s in x1_stored:
                        sp.wait_ge(s, 16 + 16 * B * C // 2)
                    with sp.Fori(0, B - 1) as i:
                        sp.wait_ge(xp_ps, xp_result(i, CT + KC - 1))
                        sp.dma_start(cn[:], ctx_t[i + 1]).then_inc(cn_loaded, 16)
                        for t in range(C):
                            sp.wait_ge(xp_done, xp_read(i, XM + t))
                            sp.dma_start(x1n[:, t, :], x1_dram[(i + 1) * C + t]).then_inc(x1_loaded[t], 16)
                        for t in range(C):
                            store(i, t)
                    for t in range(C):
                        store(B - 1, t)
                    for t in range(C):
                        sp.wait_ge(out_stored[t], 16 * (B + 1))

                return first_loads, loop

            def gpsimd_phase2(pool):
                def rstd_op(mv, ve, rstd, t, mv_sem, ve_sem, rstd_sem, n):
                    pool.wait_ge(mv_sem, n)
                    nc.gpsimd.tensor_tensor(ve[:, t:t + 1], mv[:, t, 1:2], eps_tile[:], ALU.add
                                            ).then_inc(ve_sem, 1)
                    pool.wait_ge(ve_sem, n)
                    nc.gpsimd.tensor_tensor(rstd[:, t:t + 1], ve[:, t:t + 1], neg_half[:, 0:1], ALU.pow
                                            ).then_inc(rstd_sem, 1)

                def x_stage(b, st):
                    if st[0] == "weights":
                        pool.sem_inc(flo_done, 2)
                        nc.gpsimd.memset(ones[:], 1.0).then_inc(const2, 1)
                        nc.gpsimd.memset(half[:], 0.5).then_inc(const2, 1)
                        nc.gpsimd.memset(one[:], 1.0).then_inc(const2, 1)
                        pool.wait_ge(const2, 3)
                    elif st[0] == "squares":
                        pool.wait_ge(og_done, 1 + B * G)
                        dst, w = sq_piece(st[1])
                        nc.gpsimd.tensor_tensor(dst, w, w, ALU.mult).then_inc(sq_pool, 1)
                    elif st[0] == "xm":
                        rstd_op(mv2, ve2, rstd2, st[1], mv2_ready, ve2_ready, rstd2_ready, b * C + st[1] + 1)
                    elif st[0] == "norms":
                        pool.wait_ge(sc_step, 6)
                        nc.gpsimd.tensor_tensor(sc[:, 2, :], sc[:, 1, :], half[:], ALU.pow).then_inc(sqrt_done, 1)

                def inner_tile(i, f):
                    if f == 0:
                        for t in range(C):
                            pool.wait_ge(x2_ready, i * C + t + 1)
                            nc.gpsimd.tensor_tensor(x2k[:, t, :], x2n[:, t, :], one[:].to_broadcast([P, D]), ALU.mult
                                                    ).then_inc(x2k_ready, 1)
                    pool.wait_ge(fhi_done, i * FT + f + 1)
                    nc.gpsimd.tensor_tensor(fu_lo[:, f, :], fu[:, f % 2, :], fu_hi[:, f, :], ALU.subtract
                                            ).then_inc(flo_done, 1)

                def down_tile(i, t):
                    n = i * C + t + 1
                    pool.wait_ge(dn_done, 2 + n)
                    nc.gpsimd.tensor_tensor(y3[:, t, :], y3[:, t, :], x2k[:, t, :], ALU.add).then_inc(y3_ready, 1)
                    rstd_op(mv3, ve3, rstd3, t, mv3_ready, ve3_ready, rstd3_ready, n)

                return x_stage, inner_tile, down_tile

            def scalar_phase2(act):
                def high(b, n, dst, src, **kw):
                    act.wait_ge(xp_ps, xp_result(b, n))
                    nc.scalar.activation(dst, src, **kw).then_inc(xhi_done, 1)

                def blocks(b, n):
                    return xp(b, n)[:].rearrange("p (k c) -> p k c", k=K)

                def x_stage(b, st):
                    if st[0] == "weights":
                        act.wait_ge(xw_ps, 1)
                        for i in range(2):
                            nc.scalar.activation(xw_hi[:, i, :, :],
                                                 bank[0][:, i * CTX:(i + 1) * CTX].rearrange("p (k c) -> p k c", k=KC),
                                                 ACT.Copy, scale=(-1.0, 1.0)[i]).then_inc(xwh_done, 1)
                    elif st[0] == "squares":
                        act.wait_ge(og_done, 1 + B * G)
                        for n in range(SQ_ACT + 10 * st[1] // 4, SQ_ACT + 10 * (st[1] + 1) // 4):
                            dst, w = sq_piece(n)
                            nc.scalar.activation(dst, w, ACT.Square).then_inc(sq_act, 1)
                    elif st[0] == "scales":
                        act.wait_ge(back_done, 1)
                        for f in range(0, FT, 2):
                            nc.scalar.activation(wdn[:, f, :], wdn[:, f, :], ACT.Identity, scale=back[:, f:f + 1]
                                                 ).then_inc(wdn_done, 1)
                    elif st[0] == "ctx":
                        for k in range(KC):
                            high(b, CT + k, ct_hi[:, k, :], xp(b, CT + k)[:], func=ACT.Copy)
                    elif st[0] == "qk":
                        for i in range(2):
                            high(b, QK + i, qk_hi[:, i, :], xp(b, QK + i)[:], func=ACT.Identity, bias=xb[:, i:i + 1])
                    elif st[0] == "x1t":
                        for t in st[1:]:
                            high(b, x1t_use(t), x1t_hi[:, :, t * P:(t + 1) * P], blocks(b, x1t_use(t)), func=ACT.Copy)
                    elif st[0] == "en":
                        for m in st[1:]:
                            act.wait_ge(nmax_ready, b * C + m + 1)
                            nc.scalar.activation(att[:, m, :], xp(b, en_use(m))[:], ACT.Exp, scale=-1.0,
                                                 bias=nmax[:, m:m + 1], accum_out=esum[:, m:m + 1]
                                                 ).then_inc(exp_done, 1)
                    elif st[0] == "at":
                        for m in st[1:]:
                            high(b, AT + m, att_hi[:, :, m * P:(m + 1) * P], blocks(b, AT + m), func=ACT.Copy)
                    elif st[0] == "x2t":
                        for t in st[1:]:
                            high(b, X2T + t, x2t_hi[:, :, t * P:(t + 1) * P], blocks(b, X2T + t), func=ACT.Copy,
                                 scale=X2_SCALE)

                def fuse_high(i, f):
                    act.wait_ge(gu_done, 2 + i * FT + f + 1)
                    nc.scalar.activation(fu_hi[:, f, :], fu[:, f % 2, :], ACT.Copy).then_inc(fhi_done, 1)

                def inner_tile(i, f):
                    if f == 0:
                        act.wait_ge(scales_done, 1)
                    act.wait_ge(g_ps, i * FT + f + 1)
                    nc.scalar.activation(th[:, f % 2, :], bank[f % 2][:], ACT.Tanh, scale=tanh_scale[:, f:f + 1]
                                         ).then_inc(th_done, 1)
                    if f >= 1:
                        fuse_high(i, f - 1)
                    if f == FT - 1:
                        fuse_high(i, f)

                def down_tile(i, t):
                    pass

                return x_stage, inner_tile, down_tile

            def tensor_phase2(pe):
                def column_norms():
                    pe.wait_ge(const2, 3)
                    pe.wait_ge(og_done, 1 + B * G)
                    for n in range(SQ):
                        if n < SQ_ACT:
                            pe.wait_ge(sq_pool, n + 1)
                        elif n < SQ_DVE:
                            pe.wait_ge(sq_act, n - SQ_ACT + 1)
                        else:
                            pe.wait_ge(sq_dve, n - SQ_DVE + 1)
                        i, f4, k = n // (3 * K), n // K % 3, n % K
                        for f in range(4):
                            col = (k * 2 + i) * FT + f4 * 4 + f
                            mm = nc.tensor.matmul(bank[4][:, col:col + 1], sq_piece(n)[0][:, f * P:(f + 1) * P],
                                                  ones[:], start=True, stop=True)
                    mm.then_inc(norms_done, 1)

                def three(out_, a_hi, a_lo, b_hi, b_lo, ks):
                    for k in ks:
                        for q, (a, bb) in enumerate(((a_hi, b_hi), (a_hi, b_lo), (a_lo, b_hi))):
                            mm = nc.tensor.matmul(out_, a(k), bb(k), start=(k == 0 and q == 0),
                                                  stop=(k == len(ks) - 1 and q == 2))
                    return mm

                def turn(b, n, src, ks):
                    pe.wait_ge(xp_done, xp_free(b, n))
                    for k in ks:
                        mm = nc.tensor.transpose(xp(b, n)[:, k * P:(k + 1) * P], src(k), ident[:])
                    mm.then_inc(xp_ps, 1)

                def x_stage(b, st):
                    if st[0] == "weights":
                        pe.wait_ge(xw_loaded, 32)
                        pe.wait_ge(pa_done, 2 + PA_USES * B)
                        for i in range(2):
                            for k in range(KC):
                                mm = nc.tensor.transpose(bank[0][:, (i * KC + k) * P:(i * KC + k + 1) * P],
                                                         xw_raw[:, i, k * P:(k + 1) * P], ident[:])
                        mm.then_inc(xw_ps, 1)
                    elif st[0] == "norms":
                        column_norms()
                    elif st[0] == "ctx":
                        if isinstance(b, int):
                            pe.wait_ge(xw_done, 2)
                        pe.wait_ge(cn_loaded, 16 * (b + 1))
                        for k in range(KC):
                            turn(b, CT + k, lambda t: cn[:, t, k * P:(k + 1) * P], range(C))
                    elif st[0] == "qk":
                        pe.wait_ge(xp_done, xp_read(b, CT + KC - 1))
                        for i in range(2):
                            pe.wait_ge(xp_done, xp_free(b, QK + i))
                            three(xp(b, QK + i)[:], lambda k: xw_hi[:, i, k, :], lambda k: xw_lo[:, i, k, :],
                                  lambda k: ct_hi[:, k, :], lambda k: ct_lo[:, k, :], range(KC)).then_inc(xp_ps, 1)
                    elif st[0] == "x1t":
                        for t in st[1:]:
                            pe.wait_ge(x1_loaded[t], 16 * (b + 1))
                            turn(b, x1t_use(t), lambda k: x1n[:, t, k * P:(k + 1) * P], range(K))
                    elif st[0] == "en":
                        if st[1] == 0:
                            pe.wait_ge(xp_done, xp_read(b, QK + 1))
                        for m in st[1:]:
                            pe.wait_ge(xp_done, xp_free(b, en_use(m)))
                            mc = slice(m * P, (m + 1) * P)
                            three(xp(b, en_use(m))[:], lambda k: qk_hi[:, 0, mc], lambda k: qk_lo[:, 0, mc],
                                  lambda k: qk_hi[:, 1, :], lambda k: qk_lo[:, 1, :], range(1)).then_inc(xp_ps, 1)
                    elif st[0] == "at":
                        for m in st[1:]:
                            pe.wait_ge(xp_done, xp_read(b, en_use(m)))
                            turn(b, AT + m, lambda k: att[:, m, k * P:(k + 1) * P], range(K))
                    elif st[0] == "xm":
                        t = st[1]
                        if t == 0:
                            pe.wait_ge(xp_done, xp_read(b, AT + C - 1))
                        pe.wait_ge(xp_done, xp_free(b, XM + t))
                        tc = slice(t * P, (t + 1) * P)
                        three(xp(b, XM + t)[:], lambda k: x1t_hi[:, k, tc], lambda k: x1t_lo[:, k, tc],
                              lambda k: att_hi[:, k, :], lambda k: att_lo[:, k, :], range(K)).then_inc(xp_ps, 1)
                    elif st[0] == "x2t":
                        for t in st[1:]:
                            pe.wait_ge(x2_ready, b * C + t + 1)
                            turn(b, X2T + t, lambda k: x2n[:, t, k * P:(k + 1) * P], range(K))

                def inner_tile(i, f):
                    if f == 0:
                        pe.wait_ge(xp_done, xp_read(i, X2T + C - 1))
                    pe.wait_ge(gu_done, i * FT + f + 1)
                    for w, (first_bank, ready) in enumerate(((0, g_ps), (2, u_ps))):
                        for k in range(K):
                            for q, xt in enumerate((x2t_hi, x2t_lo)):
                                mm = nc.tensor.matmul(bank[first_bank + f % 2][:], wgu[:, w, k, f * P:(f + 1) * P],
                                                      xt[:, k, :], start=(k + q == 0), stop=(k == K - 1 and q == 1))
                        mm.then_inc(ready, 1)

                def down_tile(i, t):
                    if t == 0:
                        pe.wait_ge(flo_done, 2 + i * FT + FT)
                        pe.wait_ge(wdn_done, FT)
                    pe.wait_ge(dn_done, i * C + t + 1)
                    for f in range(FT):
                        for q, fa in enumerate((fu_hi, fu_lo)):
                            mm = nc.tensor.matmul(bank[4 + t % 2][:], fa[:, f, t * P:(t + 1) * P], wdn[:, f, :],
                                                  start=(f + q == 0), stop=(f == FT - 1 and q == 1))
                    mm.then_inc(dn_ps, 1)

                return x_stage, inner_tile, down_tile

            def vector_phase2(dve):
                step = [0]

                def small(ins):
                    step[0] += 1
                    ins.then_inc(sc_step, 1)
                    dve.wait_ge(sc_step, step[0])

                def bound_squared():
                    dve.wait_ge(sc_loaded, 32)
                    dve.wait_ge(norms_done, 1)
                    n4 = bank[4][:, 0:K * 2 * FT].rearrange("p (k i) -> p i k", k=K)
                    small(nc.vector.tensor_reduce(norms[:], n4, AX_X, ALU.add))
                    small(nc.vector.tensor_tensor(sc[:, 3, :], gs[:], us[:], ALU.mult))
                    small(nc.vector.tensor_tensor(sc[:, 0, :], norms[:, 0:FT], norms[:, FT:2 * FT], ALU.mult))
                    small(nc.vector.tensor_tensor(sc[:, 5, :], sc[:, 3, :], sc[:, 3, :], ALU.mult))
                    small(nc.vector.tensor_tensor(sc[:, 0, :], sc[:, 0, :], sc[:, 5, :], ALU.mult))
                    small(nc.vector.tensor_scalar(sc[:, 1, :], sc[:, 0, :], 2.0 ** -100, None, ALU.max))

                def finish_scales():
                    dve.wait_ge(sqrt_done, 1)
                    small(nc.vector.tensor_scalar(sc[:, 4, :], sc[:, 2, :], D * 1.1, None, ALU.mult))
                    small(nc.vector.tensor_scalar(sc[:, 5, :].bitcast(U32), sc[:, 4, :].bitcast(U32), 0x7F800000, None,
                                                  ALU.bitwise_and))
                    small(nc.vector.tensor_scalar(back[:], sc[:, 5, :], 2.0 / FUSE_TOP, None, ALU.mult))
                    dve.sem_inc(back_done, 1)
                    small(nc.vector.reciprocal(sc[:, 0, :], back[:]))
                    small(nc.vector.tensor_scalar(sc[:, 1, :], sc[:, 3, :], 0.5 / X2_SCALE ** 2, None, ALU.mult))
                    nc.vector.tensor_tensor(fuse_scale[:], sc[:, 0, :], sc[:, 1, :], ALU.mult).then_inc(scales_done, 1)
                    for f in range(1, FT, 2):
                        nc.vector.tensor_scalar(wdn[:, f, :], wdn[:, f, :], back[:, f:f + 1], None, ALU.mult
                                                ).then_inc(wdn_done, 1)

                def low(b, n, dst, hi, src, scale=None, bias=None):
                    dve.wait_ge(xhi_done, xhi(b, n))
                    if scale is None and bias is None:
                        ins = nc.vector.tensor_tensor(dst, src, hi, ALU.subtract)
                    elif bias is None:
                        ins = nc.vector.scalar_tensor_tensor(out=dst, in0=src, scalar=scale, in1=hi, op0=ALU.mult,
                                                             op1=ALU.subtract)
                    else:
                        ins = nc.vector.scalar_tensor_tensor(out=dst, in0=src, scalar=bias, in1=hi, op0=ALU.add,
                                                             op1=ALU.subtract)
                    ins.then_inc(xp_done, 1)

                def blocks(b, n):
                    return xp(b, n)[:].rearrange("p (k c) -> p k c", k=K)

                def norm2(b, t):
                    dve.wait_ge(rstd2_ready, b * C + t + 1)
                    nc.vector.tensor_scalar(x2n[:, t, :], x2n[:, t, :], mv2[:, t, 0:1], rstd2[:, t:t + 1],
                                            ALU.subtract, ALU.mult).then_inc(x2_ready, 1)

                def x_stage(b, st):
                    if st[0] == "weights":
                        dve.sem_inc(xp_done, 2)
                        dve.sem_inc(gu_done, 2)
                        dve.sem_inc(dn_done, 2)
                        for t in range(C):
                            dve.sem_inc(out_stored[t], 16)
                        dve.wait_ge(xwh_done, 2)
                        for i in range(2):
                            src = bank[0][:, i * CTX:(i + 1) * CTX].rearrange("p (k c) -> p k c", k=KC)
                            nc.vector.scalar_tensor_tensor(out=xw_lo[:, i, :, :], in0=src, scalar=(-1.0, 1.0)[i],
                                                           in1=f32v(xw_hi[:, i, :, :]), op0=ALU.mult, op1=ALU.subtract)
                        dve.wait_ge(xb_loaded, 32)
                        nc.vector.tensor_scalar(xb[:, 0:1], xb[:, 0:1], -1.0, None, ALU.mult)
                        dve.drain().then_inc(xw_done, 2)
                        dve.wait_ge(sc_loaded, 32)
                        nc.vector.tensor_scalar(tanh_scale[:], gs[:], 0.5 / X2_SCALE, None, ALU.mult
                                                ).then_inc(scales_done, 1)
                    elif st[0] == "norms":
                        bound_squared()
                    elif st[0] == "scales":
                        finish_scales()
                    elif st[0] == "squares":
                        dve.wait_ge(og_done, 1 + B * G)
                        for n in range(SQ_DVE + 10 * st[1] // 4, SQ_DVE + 10 * (st[1] + 1) // 4):
                            dst, w = sq_piece(n)
                            nc.vector.tensor_tensor(dst, w, w, ALU.mult).then_inc(sq_dve, 1)
                    elif st[0] == "ctx":
                        for k in range(KC):
                            low(b, CT + k, ct_lo[:, k, :], f32v(ct_hi[:, k, :]), xp(b, CT + k)[:])
                    elif st[0] == "qk":
                        for i in range(2):
                            low(b, QK + i, qk_lo[:, i, :], f32v(qk_hi[:, i, :]), xp(b, QK + i)[:], bias=xb[:, i:i + 1])
                    elif st[0] == "x1t":
                        for t in st[1:]:
                            sl = (slice(None), slice(None), slice(t * P, (t + 1) * P))
                            low(b, x1t_use(t), x1t_lo[sl], f32v(x1t_hi[sl]), blocks(b, x1t_use(t)))
                    elif st[0] == "en":
                        for m in st[1:]:
                            dve.wait_ge(xp_ps, xp_result(b, en_use(m)))
                            nc.vector.tensor_reduce(nmax[:, m:m + 1], xp(b, en_use(m))[:], AX_X, ALU.min
                                                    ).then_inc(nmax_ready, 1)
                        for m in st[1:]:
                            dve.wait_ge(exp_done, b * C + m + 1)
                            nc.vector.reciprocal(einv[:, m:m + 1], esum[:, m:m + 1]).then_inc(einv_ready, 1)
                            dve.wait_ge(einv_ready, b * C + m + 1)
                            nc.vector.tensor_scalar(att[:, m, :], att[:, m, :], einv[:, m:m + 1], None, ALU.mult
                                                    ).then_inc(xp_done, 1)
                    elif st[0] == "at":
                        for m in st[1:]:
                            sl = (slice(None), slice(None), slice(m * P, (m + 1) * P))
                            low(b, AT + m, att_lo[sl], f32v(att_hi[sl]), blocks(b, AT + m))
                    elif st[0] == "xm":
                        t = st[1]
                        n = b * C + t + 1
                        dve.wait_ge(xp_ps, xp_result(b, XM + t))
                        if not isinstance(b, int):
                            dve.wait_ge(x2k_ready, n - C)
                        nc.vector.tensor_tensor(x2n[:, t, :], xp(b, XM + t)[:], x1n[:, t, :], ALU.add
                                                ).then_inc(xp_done, 1)
                        dve.wait_ge(xp_done, xp_read(b, XM + t))
                        nc.vector.bn_stats(bst2[:], x2n[:, t, :])
                        dve.drain()
                        nc.vector.bn_aggr(mv2[:, t, :], bst2[:]).then_inc(mv2_ready, 1)
                        if t >= 1:
                            norm2(b, t - 1)
                        if t == C - 1:
                            norm2(b, t)
                    elif st[0] == "x2t":
                        for t in st[1:]:
                            sl = (slice(None), slice(None), slice(t * P, (t + 1) * P))
                            low(b, X2T + t, x2t_lo[sl], x2t_hi[sl], blocks(b, X2T + t), scale=X2_SCALE)

                def inner_tile(i, f):
                    n = i * FT + f + 1
                    dve.wait_ge(th_done, n)
                    nc.vector.scalar_tensor_tensor(out=tu[:, f % 2, :], in0=th[:, f % 2, :], scalar=1.0,
                                                   in1=bank[f % 2][:], op0=ALU.add, op1=ALU.mult).then_inc(tu_done, 1)
                    dve.wait_ge(tu_done, n)
                    dve.wait_ge(u_ps, n)
                    dve.wait_ge(flo_done, n)
                    nc.vector.scalar_tensor_tensor(out=fu[:, f % 2, :], in0=bank[2 + f % 2][:],
                                                   scalar=fuse_scale[:, f:f + 1], in1=tu[:, f % 2, :],
                                                   op0=ALU.mult, op1=ALU.mult).then_inc(gu_done, 1)

                def norm3(i, t):
                    dve.wait_ge(rstd3_ready, i * C + t + 1)
                    nc.vector.tensor_scalar(y3[:, t, :], y3[:, t, :], mv3[:, t, 0:1], rstd3[:, t:t + 1],
                                            ALU.subtract, ALU.mult).then_inc(out_ready, 1)

                def stats3(i, t):
                    n = i * C + t + 1
                    dve.wait_ge(y3_ready, n)
                    nc.vector.bn_stats(bst3[:], y3[:, t, :])
                    dve.drain()
                    nc.vector.bn_aggr(mv3[:, t, :], bst3[:]).then_inc(mv3_ready, 1)

                def down_tile(i, t):
                    n = i * C + t + 1
                    dve.wait_ge(down_loaded, 16)
                    dve.wait_ge(dn_ps, n)
                    dve.wait_ge(out_stored[t], 16 * (i + 1))
                    nc.vector.tensor_tensor(y3[:, t, :], bank[4 + t % 2][:], down_b[:], ALU.mult
                                            ).then_inc(dn_done, 1)
                    if t >= 1:
                        stats3(i, t - 1)
                    if t >= 2:
                        norm3(i, t - 2)
                    if t == C - 1:
                        stats3(i, t)
                        norm3(i, t - 1)
                        norm3(i, t)

                return x_stage, inner_tile, down_tile

        with nc.Block() as block:

            @block.sync
            def _(sp):
                sp.dma_start(wq_raw, wq.rearrange("(k p) n -> p k n", p=P)).then_inc(wq_loaded, 16)

                def load_x(b, t):
                    sp.dma_start(xin[:, t % 2, :], x_t[b * C + t]).then_inc(xin_loaded[t % 2], 16)

                for t in range(2):
                    load_x(0, t)
                for t in range(2):
                    sp.dma_start(raw[:, t, :], x_t[2 + t]).then_inc(x23_loaded[t], 16)
                sp.dma_start(wk_raw, wk.rearrange("(k p) n -> p k n", p=P)).then_inc(wk_loaded, 16)
                sp.dma_start(nw_p[:], nw.rearrange("(k p) -> p k", p=P), allow_slow_non_contiguous=True
                              ).then_inc(small_loaded, 16)
                for r in range(4):
                    sp.dma_start(g1raw[:, :, r * HD:(r + 1) * HD], wg1.rearrange("(k p) c -> p k c", p=P)
                                  ).then_inc(g1raw_loaded, 16)
                    sp.dma_start(g2raw[r * HD:(r + 1) * HD, :], wg2).then_inc(g2raw_loaded, 16)
                sp.dma_start(wo_raw, wo.rearrange("(k p) n -> p k n", p=P)).then_inc(wo_loaded, 16)

                def load_raw(b, r):
                    n = b * PREP + r
                    if r < 6:
                        src = (gate_t, up_t)[r // 3][b, :, (r % 3) * 512:(r % 3 + 1) * 512]
                    else:
                        src = down_t[b * 3 + (r - 6)]
                    sp.wait_ge(prep_done, n + 1 if r == 0 else n)
                    sp.dma_start(raw[:, r % 2, :], src).then_inc(raw_loaded[r % 2], 16)

                def load_y(b, c):
                    sp.wait_ge(x1_stored[c % 2], 32 * b + 16 * (c // 2) + 16)
                    sp.dma_start(y[:, c % 2, :], x_t[b * C + c]).then_inc(y_loaded[c % 2], 16)

                def store_x1(b, c):
                    sp.wait_ge(x1_ready, b * C + c + 1)
                    sp.dma_start(x1_dram[b * C + c], y[:, c % 2, :]).then_inc(x1_stored[c % 2], 16)

                def stage(name, b, *a):
                    if name == "x":
                        t = a[0]
                        if isinstance(b, int):
                            if t == 3:
                                sp.wait_ge(pa_ps, pa_result(b, 3))
                                load_raw(b, 0)
                                load_raw(b, 1)
                        elif t >= 2:
                            sp.wait_ge(pa_ps, pa_result(b, t - 2))
                            load_x(b, t)
                    elif name == "prep":
                        if a[0] + 2 < PREP:
                            load_raw(b, a[0] + 2)
                        elif a[0] == PREP - 1 and not isinstance(b, int):
                            load_raw(b + 1, 0)
                            load_raw(b + 1, 1)
                    elif name == "scores" and a == (0, 1):
                        if not isinstance(b, int):
                            for t in range(2):
                                sp.wait_ge(pa_ps, pa_result(b, t + 2))
                                load_x(b + 1, t)
                    elif name == "scores" and a == (G - 1, 0):
                        sp.wait_ge(wlo_done, K + 3)
                        load_y(b, 0)
                        load_y(b, 1)
                    elif name == "out" and a[0] >= 1:
                        store_x1(b, a[0] - 1)
                        if a[0] + 1 < C:
                            load_y(b, a[0] + 1)
                    elif name == "end":
                        store_x1(b, C - 1)

                run_loads(sp, stage, *sync_phase2(sp))

            @block.gpsimd
            def _(pool):
                def set_up(part):
                    if part == 0:
                        nc.gpsimd.memset(ident[:], 0.0).then_inc(ident_zero, 1)
                        nc.gpsimd.iota(diff_i, pattern=[[1, P]], base=0, channel_multiplier=-1).then_inc(iota_done, 1)
                        nc.gpsimd.iota(ramp_i, pattern=[[1, P]], base=0, channel_multiplier=0).then_inc(iota_done, 1)
                        pool.wait_ge(ident_zero, 1)
                        nc.gpsimd.affine_select(out=ident[:], in_=ident[:], compare_op=ALU.not_equal, fill=1.0,
                                                base=0, pattern=[[-1, P]], channel_multiplier=1).then_inc(const_done, 1)
                        for qb in (qb_hi, qb_lo):
                            nc.gpsimd.memset(f32v(qb[:]), 0.0).then_inc(qb_zero, 1)
                        pool.sem_inc(prep_done, 1)
                        pool.sem_inc(ss_scaled, 1)
                        nc.gpsimd.memset(neg_half[:], -0.5)
                        nc.gpsimd.memset(eps_tile[:], EPS)
                        nc.gpsimd.memset(eps_group[:], EPS * GROUP_SCALE)
                        nc.gpsimd.memset(blocks_of_4[:], 1.0).then_inc(blocks_step, 1)
                        pool.wait_ge(blocks_step, 1)
                        nc.gpsimd.affine_select(out=blocks_of_4[:], in_=blocks_of_4[:], compare_op=ALU.is_ge, fill=0.0,
                                                base=0, pattern=[[-HD, J], [0, HD]], channel_multiplier=1
                                                ).then_inc(blocks_step, 1)
                        pool.wait_ge(blocks_step, 2)
                        nc.gpsimd.affine_select(out=blocks_of_4[:], in_=blocks_of_4[:], compare_op=ALU.is_ge, fill=0.0,
                                                base=HD - 1, pattern=[[HD, J], [0, HD]], channel_multiplier=-1
                                                ).then_inc(blocks_step, 1)
                    elif part == 1:
                        for k in range(K):
                            pool.wait_ge(wvo_hi_done, k + 1)
                            nc.gpsimd.tensor_tensor(w_lo["wv"][:, k, :], wv_raw[:, k, :], f32v(w_hi["wv"][:, k, :]),
                                                    ALU.subtract).then_inc(wlo_done, 1)
                        pool.wait_ge(tables_done, 1)
                    elif part == 2:
                        pool.wait_ge(wg_hi_done, 2)
                        nc.gpsimd.tensor_tensor(wg1_lo[:], g1raw, f32v(wg1_hi[:]), ALU.subtract).then_inc(wlo_done, 1)
                        for r in (2, 3):
                            pool.wait_ge(wlo_done, K + r - 1)
                            q = slice(r * HD, (r + 1) * HD)
                            nc.gpsimd.tensor_tensor(wg2_st[q, :], g2raw[q, :], f32v(wg2_st[q, :]), ALU.subtract
                                                    ).then_inc(wlo_done, 1)
                        pool.wait_ge(wlo_done, K + 3)
                        for h in range(H):
                            pool.wait_ge(masks_exp, h + 1)
                            dh = decay[:, h // J, h % J, :]
                            nc.gpsimd.affine_select(out=dh, in_=dh, compare_op=ALU.is_ge,
                                                    fill=0.0, base=0, pattern=[[1, P]], channel_multiplier=-1
                                                    ).then_inc(masks_done, 1)
                        for k in range(K):
                            pool.wait_ge(wvo_hi_done, K + k + 1)
                            nc.gpsimd.tensor_tensor(w_lo["wo"][:, k, :], wo_raw[:, k, :], f32v(w_hi["wo"][:, k, :]),
                                                    ALU.subtract).then_inc(wlo_done, 1)

                def stage(name, b, *a):
                    if name == "setup":
                        set_up(a[0])
                        return
                    if name == "prep":
                        r = a[0]
                        pool.wait_ge(magic_ready, b * PREP + r + 1)
                        piece = raw[:, r % 2, :]
                        nc.gpsimd.tensor_tensor(piece, piece, magic[:], ALU.add).then_inc(raw_added, 1)
                        pool.wait_ge(raw_added, b * PREP + r + 1)
                        if r < 6:
                            dst = wgu[:, r // 3, b, (r % 3) * 512:(r % 3 + 1) * 512]
                        else:
                            dst = wdn[:, b * 3 + (r - 6), :]
                        nc.gpsimd.tensor_tensor(dst, piece, magic[:], ALU.subtract).then_inc(prep_done, 1)
                    elif name == "k":
                        g = a[0]
                        pool.wait_ge(pa_done, pa_read(b, pa_use("k", g)))
                        nc.gpsimd.tensor_tensor(
                            kd[:], kf[:, 0:(C - 1) * P].rearrange("p (c s) -> p c s", c=C - 1),
                            kdec[:, g, :].unsqueeze(1).to_broadcast([P, C - 1, P]), ALU.mult).then_inc(kd_ready, 1)
                    elif name == "state":
                        g = a[0]
                        if g >= 1:
                            pool.wait_ge(pv_done, b * 16 + 4 * g)
                            pool.wait_ge(pa_done, pa_read(b, pa_use("q", g)))
                        else:
                            pool.wait_ge(pa_done, pa_read(b, V0 + C - 1))
                        nc.gpsimd.tensor_tensor(
                            qd[:], qf[:, P:N].rearrange("p (c s) -> p c s", c=C - 1),
                            qdec[:, g, :].unsqueeze(1).to_broadcast([P, C - 1, P]), ALU.mult).then_inc(qd_ready, 1)
                    elif name == "norm":
                        g = a[0]
                        n = b * G + g + 1
                        pool.wait_ge(ss_ready, n)
                        nc.gpsimd.tensor_tensor(ss_e[:], ss[:], eps_group[:], ALU.add).then_inc(ss_scaled, 1)
                        pool.wait_ge(ss_scaled, 1 + n)
                        nc.gpsimd.tensor_tensor(rs[:], ss_e[:], neg_half[:], ALU.pow).then_inc(rs_ready, 1)
                        pool.wait_ge(rs_ready, n)
                        o4 = og[:, :, g * P:(g + 1) * P].rearrange("p c (j e) -> p c j e", j=J)
                        rs4 = rs[:].rearrange("p (c j) -> p c j", c=C).unsqueeze(3).to_broadcast([P, C, J, HD])
                        nc.gpsimd.tensor_tensor(o4, o4, rs4, ALU.mult).then_inc(ogn_ready, 1)
                    elif name == "out":
                        n = b * C + a[0] + 1
                        pool.wait_ge(mv_ready, n)
                        nc.gpsimd.tensor_tensor(var_e[:], mv[:, 1:2], eps_tile[:], ALU.add
                                                ).then_inc(var_ready, 1)
                        pool.wait_ge(var_ready, n)
                        nc.gpsimd.tensor_tensor(rstd[:], var_e[:], neg_half[:, 0:1], ALU.pow
                                                ).then_inc(rstd_ready, 1)

                run(pool, stage, *gpsimd_phase2(pool))

            @block.scalar
            def _(act):
                def set_up(part):
                    if part == 0:
                        act.dma_start(ldb[:], ld.rearrange("(a h) -> a h", a=1).to_broadcast([P, H])
                                      ).then_inc(ld_loaded, 16)
                        for j in range(J):
                            act.dma_start(ldp[j * HD:(j + 1) * HD, :],
                                         ld.rearrange("(g j) -> j g", j=J)[j:j + 1, :].to_broadcast([HD, G]),
                                         allow_slow_non_contiguous=True).then_inc(ld_loaded, 16)
                        act.dma_start(wv_raw, wv.rearrange("(k p) n -> p k n", p=P)).then_inc(wv_loaded, 16)
                    elif part == 1:
                        act.wait_ge(wv_loaded, 16)
                        for k in range(K):
                            nc.scalar.activation(w_hi["wv"][:, k, :], wv_raw[:, k, :], ACT.Copy).then_inc(wvo_hi_done, 1)
                        act.wait_ge(ramps_done, 2)
                        act.wait_ge(ldn_done, 2)
                        for g in range(G):
                            nc.scalar.activation(qdec[:, g, :], ramp, ACT.Exp, scale=ldp[:, g:g + 1],
                                                 bias=ldp[:, g:g + 1])
                            mm = nc.scalar.activation(kdec[:, g, :], ramp, ACT.Exp, scale=ldn[:, g:g + 1],
                                                      bias=ld127[:, g:g + 1])
                        mm.then_inc(tables_done, 1)

                def stage(name, b, *a):
                    if name == "setup":
                        set_up(a[0])
                        return
                    if name == "masks":
                        if a[0] == 0:
                            act.wait_ge(ramps_done, 2)
                            act.wait_ge(ld_loaded, 16 * (1 + J))
                        for j in range(J):
                            h = a[0] * J + j
                            nc.scalar.activation(decay[:, a[0], j, :], diff, ACT.Exp, scale=ldb[:, h:h + 1]
                                                 ).then_inc(masks_exp, 1)
                        if a[0] == G - 1:
                            act.wait_ge(wo_scaled, K)
                            for k in range(K):
                                nc.scalar.activation(w_hi["wo"][:, k, :], wo_raw[:, k, :], ACT.Copy
                                                     ).then_inc(wvo_hi_done, 1)
                    elif name == "x":
                        t = a[0]
                        act.wait_ge(pa_ps, pa_result(b, t))
                        nc.scalar.activation(xt_hi[:, :, t * P:(t + 1) * P],
                                             bank[t % 2][:].rearrange("p (k c) -> p k c", k=K), ACT.Copy
                                             ).then_inc(xth_done, 1)
                    elif name in ("q", "k", "v"):
                        n = pa_use(name, a[0])
                        m = b * G + a[0] + 1
                        dst = {"q": qf[:], "k": kf[:], "v": v[:, a[0], :]}[name]
                        act.wait_ge(pa_ps, pa_result(b, n))
                        if name == "q" and (a[0] > 0 or not isinstance(b, int)):
                            act.wait_ge(q_split, m - 1)
                            act.wait_ge(qd_ready, m - 1)
                        if name == "k" and (a[0] > 0 or not isinstance(b, int)):
                            act.wait_ge(k_split, m - 1)
                            act.wait_ge(kd_ready, m - 1)
                        nc.scalar.activation(dst, bank[n % 2][:], ACT.Tanh, scale=0.5).then_inc(tanh_done, 1)
                        if name == "q":
                            act.wait_ge(pa_done, pa_read(b, n))
                            if a[0] == 0 and isinstance(b, int):
                                act.wait_ge(qb_zero, 2)
                            for j in range(J):
                                r = slice(j * HD, (j + 1) * HD)
                                mm = nc.scalar.activation(qb_hi[r, :, j % 2, :],
                                                          qf[r, :].rearrange("p (c s) -> p c s", c=C), ACT.Copy)
                                mm.then_inc(qhi_done, 1)
                        elif name == "k":
                            act.wait_ge(pa_done, pa_read(b, n))
                            nc.scalar.activation(kt_hi[:], kf[:], ACT.Copy).then_inc(khi_done, 1)
                    elif name == "g1":
                        act.wait_ge(b5_ps, b5_result(b, G1))
                        nc.scalar.activation(g1_st[:], bank[5][:], ACT.Copy).then_inc(g1h_done, 1)
                    elif name == "gated":
                        n = b * G + a[0] + 1
                        act.wait_ge(og_done, 1 + n)
                        nc.scalar.activation(osq[:], og[:, :, a[0] * P:(a[0] + 1) * P], ACT.Square
                                             ).then_inc(sq_ready, 1)
                    elif name == "k_turned":
                        n = 3 * a[0] + KN
                        act.wait_ge(b5_ps, b5_result(b, n))
                        nc.scalar.activation(kn[:], bank[5][:, 0:(C - 1) * P].rearrange("p (c s) -> p c s", c=C - 1),
                                             ACT.Copy).then_inc(b5_done, 1)
                    elif name == "gate":
                        n = 3 * a[0] + GA
                        act.wait_ge(b5_ps, b5_result(b, n))
                        act.wait_ge(og_done, b * G + a[0] + 1)
                        nc.scalar.activation(gt[:], bank[5][:].rearrange("p (c d) -> p c d", c=C), ACT.Tanh, scale=0.5
                                             ).then_inc(b5_done, 1)
                    elif name == "turned":
                        act.wait_ge(ot_ps, b * C + a[0] + 1)
                        nc.scalar.activation(ot_hi[:], bank[6][:].rearrange("p (k c) -> p k c", k=K), ACT.Copy
                                             ).then_inc(oth_done, 1)

                run(act, stage, *scalar_phase2(act))

            @block.tensor
            def _(pe):
                pe.sem_inc(pa_ps, PA_USES)

                def values_wait(b, g, c):
                    if c == 0:
                        pe.wait_ge(og_done, b * G + g + 1)
                    pe.wait_ge(probs_done, 2 + b * 16 + g * 4 + 2 * (c // 2) + 2)
                    if c == 1:
                        pe.wait_ge(qd_ready, b * G + g + 1)
                        pe.wait_ge(state_ready, b * G + g + 1)

                def value(b, g, c, j):
                    if c >= 1 and j == 0:
                        nc.tensor.matmul(bank[4][:, c * P:(c + 1) * P], qd[:, c - 1, :], state_bd[:, c - 1, :, :],
                                         start=False, stop=False, skip_group_check=True)
                    cols = slice((g * J + j) * HD, (g * J + j + 1) * HD)
                    mm = nc.tensor.matmul(bank[4][:, c * P + j * HD:c * P + (j + 1) * HD], probs[:, c, j, :],
                                          v[:, c, cols], start=(c + j == 0), stop=(c == C - 1 and j == J - 1),
                                          skip_group_check=True)
                    if j == J - 1:
                        mm.then_inc(pv_done, 1)

                def stage(name, b, *a):
                    first_batch = isinstance(b, int) and b == 0
                    if name == "x":
                        t = a[0]
                        if first_batch and t == 0:
                            pe.wait_ge(const_done, 1)
                        src = xin
                        if first_batch and t >= 2:
                            src = raw
                            pe.wait_ge(x23_loaded[t % 2], 16)
                            pe.sem_inc(xin_loaded[t % 2], 16)
                        else:
                            pe.wait_ge(xin_loaded[t % 2], 32 * b + 16 * (t // 2 + 1))
                        pe.wait_ge(pa_done, pa_free(b, t))
                        for k in range(K):
                            mm = nc.tensor.transpose(bank[t % 2][:, k * P:(k + 1) * P],
                                                     src[:, t % 2, k * P:(k + 1) * P], ident[:])
                        mm.then_inc(pa_ps, 1)
                    elif name in ("q", "k"):
                        g = a[0]
                        n = pa_use(name, g)
                        if name == "q" and g == 0:
                            pe.wait_ge(pa_done, pa_read(b, C - 1))
                        if first_batch and g == 0:
                            pe.wait_ge(wqk_lo_done, K if name == "q" else 2 * K)
                        pe.wait_ge(pa_done, pa_free(b, n))
                        between = a[1]
                        if between:
                            values_wait(*between)
                        for k in range(K):
                            for i, (wt, xt) in enumerate(((w_hi, xt_hi), (w_hi, xt_lo), (w_lo, xt_hi))):
                                mm = nc.tensor.matmul(bank[n % 2][:], wt["w" + name][:, k, g * P:(g + 1) * P],
                                                      xt[:, k, :], start=(k + i == 0), stop=(k == K - 1 and i == 2))
                            if k == K - 1:
                                mm.then_inc(pa_ps, 1)
                            if between:
                                value(*between, k)
                    elif name == "v":
                        t = a[0]
                        n = V0 + t
                        if first_batch and t == 0:
                            pe.wait_ge(wlo_done, K)
                        pe.wait_ge(pa_done, pa_free(b, n))
                        for k in range(K):
                            for i, (xt, wt) in enumerate(((xt_hi, w_hi), (xt_hi, w_lo), (xt_lo, w_hi))):
                                mm = nc.tensor.matmul(bank[n % 2][:], xt[:, k, t * P:(t + 1) * P], wt["wv"][:, k, :],
                                                      start=(k + i == 0), stop=(k == K - 1 and i == 2))
                        mm.then_inc(pa_ps, 1)
                    elif name == "g1":
                        if first_batch:
                            pe.wait_ge(wlo_done, K + 3)
                        pe.wait_ge(b5_done, b5_free(b, G1))
                        for k in range(K):
                            for i, (wt, xt) in enumerate(((wg1_hi, xt_hi), (wg1_hi, xt_lo), (wg1_lo, xt_hi))):
                                mm = nc.tensor.matmul(bank[5][:], wt[:, k, :], xt[:, k, :],
                                                      start=(k + i == 0), stop=(k == K - 1 and i == 2))
                        mm.then_inc(b5_ps, 1)
                    elif name == "scores":
                        g, w = a
                        if w == 0:
                            pe.wait_ge(q_split, b * G + g + 1)
                            pe.wait_ge(k_split, b * G + g + 1)
                        pe.wait_ge(probs_done, b * 16 + g * 4 + w * 2 + 2)
                        for c2 in range(2):
                            ch = slice((2 * w + c2) * P, (2 * w + c2 + 1) * P)
                            for i, (kt, qb) in enumerate(((kt_hi, qb_hi), (kt_hi, qb_lo), (kt_lo, qb_hi))):
                                for p in range(2):
                                    r = slice(p * 2 * HD, (p + 1) * 2 * HD)
                                    mm = nc.tensor.matmul(bank[2 + p][:, c2 * 2 * P:(c2 + 1) * 2 * P], kt[r, ch],
                                                          qb[r, 2 * w + c2, :, :], start=(i == 0), stop=(i == 2))
                                    if c2 == 1 and i == 2:
                                        mm.then_inc(sc_ps, 1)
                    elif name == "values":
                        g, c = a
                        values_wait(b, g, c)
                        for j in range(J):
                            value(b, g, c, j)
                    elif name == "k_turned":
                        g = a[0]
                        pe.wait_ge(kd_ready, b * G + g + 1)
                        pe.wait_ge(b5_done, b5_free(b, 3 * g + KN))
                        for c in range(C - 1):
                            mm = nc.tensor.transpose(bank[5][:, c * P:(c + 1) * P], kd[:, c, :], ident[:])
                        mm.then_inc(b5_ps, 1)
                    elif name == "state":
                        g = a[0]
                        if g == 0:
                            pe.wait_ge(pa_done, pa_read(b, V0 + C - 1))
                        pe.wait_ge(b5_done, b5_read(b, 3 * g + KN))
                        for c in range(C - 1):
                            for j in range(J):
                                cols = slice((g * J + j) * HD, (g * J + j + 1) * HD)
                                mm = nc.tensor.matmul(bank[5][j * HD:(j + 1) * HD, c * HD:(c + 1) * HD],
                                                      kn[:, c, j * HD:(j + 1) * HD], v[:, c, cols],
                                                      start=True, stop=True)
                        mm.then_inc(b5_ps, 1)
                    elif name == "gate":
                        g = a[0]
                        pe.wait_ge(b5_done, b5_free(b, 3 * g + GA))
                        for c in range(C):
                            mm = nc.tensor.matmul(bank[5][:, c * P:(c + 1) * P], g1_st[:, c * P:(c + 1) * P],
                                                  wg2_st[:, g * P:(g + 1) * P], start=True, stop=True)
                        mm.then_inc(b5_ps, 1)
                    elif name == "turned":
                        c = a[0]
                        pe.wait_ge(ogn_ready, b * G + G)
                        pe.wait_ge(ot_done, b * C + c + 1)
                        for k in range(K):
                            mm = nc.tensor.transpose(bank[6][:, k * P:(k + 1) * P], og[:, c, k * P:(k + 1) * P],
                                                     ident[:])
                        mm.then_inc(ot_ps, 1)
                    elif name == "out":
                        c = a[0]
                        if first_batch or not isinstance(b, int):
                            pe.wait_ge(wlo_done, 2 * K + 3)
                        pe.wait_ge(ot_done, 1 + b * C + c + 1)
                        pe.wait_ge(y_done, b * C + c + 1)
                        for k in range(K):
                            for i, (ot, wt) in enumerate(((ot_hi, w_hi), (ot_hi, w_lo), (ot_lo, w_hi))):
                                mm = nc.tensor.matmul(bank[7][:], ot[:, k, :], wt["wo"][:, k, :],
                                                      start=(k + i == 0), stop=(k == K - 1 and i == 2))
                        mm.then_inc(wo_ps, 1)

                run(pe, stage, *tensor_phase2(pe))

            @block.vector
            def _(dve):
                def in_two_parts(i, w, w_raw):
                    for k in range(K):
                        nc.vector.tensor_copy(w_hi[w][:, k, :], w_raw[:, k, :]).then_inc(wqk_hi_done, 1)
                    for k in range(K):
                        dve.wait_ge(wqk_hi_done, i * K + k + 1)
                        nc.vector.tensor_tensor(w_lo[w][:, k, :], w_raw[:, k, :], f32v(w_hi[w][:, k, :]),
                                                ALU.subtract).then_inc(wqk_lo_done, 1)

                def set_up(part):
                    if part == 0:
                        dve.sem_inc(pa_done, 2)
                        dve.sem_inc(b5_done, 1)
                        dve.sem_inc(probs_done, 2)
                        dve.sem_inc(og_done, 1)
                        dve.sem_inc(ot_done, 1)
                        dve.sem_inc(y_done, 1)
                        dve.sem_inc(x1_stored[0], 16)
                        dve.sem_inc(x1_stored[1], 16)
                        dve.wait_ge(iota_done, 2)
                        nc.vector.tensor_scalar(diff, diff_i, 0.0, None, ALU.max).then_inc(ramps_done, 1)
                        nc.vector.tensor_copy(ramp, ramp_i).then_inc(ramps_done, 1)
                        dve.wait_ge(wq_loaded, 16)
                        in_two_parts(0, "wq", wq_raw)
                        dve.wait_ge(ld_loaded, 16 * (1 + J))
                        nc.vector.tensor_scalar(ldn[:], ldp[:], -1.0, None, ALU.mult).then_inc(ldn_done, 1)
                        nc.vector.tensor_scalar(ld127[:], ldp[:], float(P - 1), None, ALU.mult).then_inc(ldn_done, 1)
                    elif part == 1:
                        dve.wait_ge(wk_loaded, 16)
                        in_two_parts(1, "wk", wk_raw)
                    elif part == 2:
                        dve.wait_ge(g1raw_loaded, 64)
                        nc.vector.tensor_copy(wg1_hi[:], g1raw).then_inc(wg_hi_done, 1)
                        dve.wait_ge(g2raw_loaded, 64)
                        nc.vector.tensor_copy(wg2_st[:], g2raw).then_inc(wg_hi_done, 1)
                        dve.wait_ge(small_loaded, 16)
                        dve.wait_ge(wo_loaded, 16)
                        for k in range(K):
                            nc.vector.tensor_scalar(wo_raw[:, k, :], wo_raw[:, k, :], nw_p[:, k:k + 1],
                                                    GROUP_SCALE ** 0.5 / 16, ALU.mult, ALU.mult).then_inc(wo_scaled, 1)
                        dve.wait_ge(tables_done, 1)
                        nc.vector.tensor_copy(cdec[:], qdec[:, :, P - 1:P].to_broadcast([P, G, HD])).then_inc(tables_done, 1)

                def x1(b, c):
                    dve.wait_ge(rstd_ready, b * C + c + 1)
                    nc.vector.tensor_scalar(y[:, c % 2, :], y[:, c % 2, :], mv[:, 0:1], rstd[:],
                                            ALU.subtract, ALU.mult).then_inc(x1_ready, 1)

                def stage(name, b, *a):
                    if name == "setup":
                        set_up(a[0])
                        return
                    if name == "prep":
                        r = a[0]
                        n = b * PREP + r + 1
                        dve.wait_ge(prep_done, n)
                        dve.wait_ge(raw_loaded[r % 2], 16 * (b * (PREP // 2 + (r + 1) % 2) + r // 2 + 1))
                        nc.vector.tensor_scalar(magic[:].bitcast(U32), raw[:, r % 2, :].bitcast(U32), 0x7F800000, None,
                                                ALU.bitwise_and).then_inc(magic_exp, 1)
                        dve.wait_ge(magic_exp, n)
                        nc.vector.tensor_scalar(magic[:], magic[:], 2.0 ** -6, 1.5 * 2.0 ** 20, ALU.max, ALU.mult
                                                ).then_inc(magic_ready, 1)
                    elif name == "x":
                        t = a[0]
                        dve.wait_ge(xth_done, b * C + t + 1)
                        sl = (slice(None), slice(None), slice(t * P, (t + 1) * P))
                        nc.vector.tensor_tensor(xt_lo[sl], bank[t % 2][:].rearrange("p (k c) -> p k c", k=K),
                                                f32v(xt_hi[sl]), ALU.subtract).then_inc(pa_done, 1)
                    elif name in ("q", "k", "v"):
                        n = pa_use(name, a[0])
                        m = b * G + a[0] + 1
                        dst = {"q": qf[:], "k": kf[:], "v": v[:, a[0], :]}[name]
                        dve.wait_ge(tanh_done, b * 12 + n - C + 1)
                        nc.vector.scalar_tensor_tensor(out=dst, in0=dst, scalar=1.0, in1=bank[n % 2][:],
                                                       op0=ALU.add, op1=ALU.mult).then_inc(pa_done, 1)
                        if name == "q":
                            for j in range(J):
                                r = slice(j * HD, (j + 1) * HD)
                                dve.wait_ge(qhi_done, (m - 1) * J + j + 1)
                                mm = nc.vector.tensor_tensor(qb_lo[r, :, j % 2, :],
                                                             qf[r, :].rearrange("p (c s) -> p c s", c=C),
                                                             f32v(qb_hi[r, :, j % 2, :]), ALU.subtract)
                            mm.then_inc(q_split, 1)
                        elif name == "k":
                            dve.wait_ge(khi_done, m)
                            nc.vector.tensor_tensor(kt_lo[:], kf[:], f32v(kt_hi[:]), ALU.subtract
                                                    ).then_inc(k_split, 1)
                    elif name == "g1":
                        dve.wait_ge(g1h_done, b + 1)
                        q = slice(HD, 2 * HD)
                        nc.vector.tensor_tensor(g1_st[q, :], bank[5][q, :], f32v(g1_st[q, :]), ALU.subtract)
                        q = slice(3 * HD, 4 * HD)
                        nc.vector.tensor_tensor(g1_st[q, :], bank[5][q, :], f32v(g1_st[q, :]), ALU.subtract
                                                ).then_inc(b5_done, 1)
                    elif name == "scores":
                        g, w = a
                        if g == 0 and w == 0:
                            dve.wait_ge(wlo_done, K)
                            dve.wait_ge(masks_done, H)
                            dve.wait_ge(blocks_step, 3)
                            dve.wait_ge(tables_done, 2)
                        for p in range(2):
                            dve.wait_ge(sc_ps, b * 16 + g * 4 + w * 2 + p + 1)
                            dst = probs[:, 2 * w:2 * w + 2, 2 * p:2 * p + 2, :]
                            nc.vector.tensor_tensor(
                                dst, bank[2 + p][:].rearrange("p (c j s) -> p c j s", c=2, j=2),
                                decay[:, g, 2 * p:2 * p + 2, :].unsqueeze(1).to_broadcast([P, 2, 2, P]),
                                ALU.mult).then_inc(probs_done, 1)
                    elif name == "state":
                        g = a[0]
                        n = (b * G + g) * 5
                        dve.wait_ge(b5_ps, b5_result(b, 3 * g + ST))
                        nc.vector.tensor_copy(state[:, 0, :], bank[5][:, 0:HD]).then_inc(state_step, 1)
                        for c in range(1, C - 1):
                            dve.wait_ge(state_step, n + 2 * c - 1)
                            nc.vector.tensor_tensor(state_d[:], state[:, c - 1, :], cdec[:, g, :], ALU.mult
                                                    ).then_inc(state_step, 1)
                            dve.wait_ge(state_step, n + 2 * c)
                            mm = nc.vector.tensor_tensor(state[:, c, :], bank[5][:, c * HD:(c + 1) * HD],
                                                         state_d[:], ALU.add)
                            mm.then_inc(state_step, 1)
                        dve.wait_ge(state_step, n + 5)
                        dve.sem_inc(b5_done, 1)
                        nc.vector.tensor_tensor(
                            state_bd[:], state[:].unsqueeze(2).to_broadcast([P, C - 1, J, HD]),
                            blocks_of_4[:].unsqueeze(1).to_broadcast([P, C - 1, J, HD]), ALU.mult
                            ).then_inc(state_ready, 1)
                    elif name == "gated":
                        g = a[0]
                        if g == 0:
                            dve.wait_ge(wlo_done, 2 * K + 3)
                        dve.wait_ge(b5_done, b5_read(b, 3 * g + GA))
                        dve.wait_ge(pv_done, b * 16 + 4 * g + 4)
                        nc.vector.scalar_tensor_tensor(out=og[:, :, g * P:(g + 1) * P], in0=gt[:], scalar=1.0,
                                                       in1=bank[4][:].rearrange("p (c d) -> p c d", c=C),
                                                       op0=ALU.add, op1=ALU.mult).then_inc(og_done, 1)
                    elif name == "norm":
                        g = a[0]
                        dve.wait_ge(sq_ready, b * G + g + 1)
                        dve.wait_ge(ss_scaled, b * G + g + 1)
                        nc.vector.tensor_reduce(ss[:], osq[:].rearrange("p c (j e) -> p (c j) e", j=J), AX_X,
                                                ALU.add).then_inc(ss_ready, 1)
                    elif name == "turned":
                        c = a[0]
                        dve.wait_ge(oth_done, b * C + c + 1)
                        nc.vector.tensor_tensor(ot_lo[:], bank[6][:].rearrange("p (k c) -> p k c", k=K),
                                                f32v(ot_hi[:]), ALU.subtract).then_inc(ot_done, 1)
                    elif name == "out":
                        c = a[0]
                        n = b * C + c + 1
                        if c >= 1:
                            x1(b, c - 1)
                        dve.wait_ge(wo_ps, n)
                        dve.wait_ge(y_loaded[c % 2], 32 * b + 16 * (c // 2 + 1))
                        nc.vector.tensor_tensor(y[:, c % 2, :], bank[7][:], y[:, c % 2, :], ALU.add
                                                ).then_inc(y_done, 1)
                        dve.wait_ge(y_done, 1 + n)
                        nc.vector.bn_stats(bst[:], y[:, c % 2, :])
                        dve.drain()
                        nc.vector.bn_aggr(mv[:], bst[:]).then_inc(mv_ready, 1)
                    elif name == "end":
                        x1(b, C - 1)

                run(dve, stage, *vector_phase2(dve))


_INS = ['x', 'ctx_1024', 'L0_attn_log_decay', 'L0_attn_Wq', 'L0_attn_Wk', 'L0_attn_Wv', 'L0_attn_Wo',
        'L0_attn_Wg1', 'L0_attn_Wg2', 'L0_attn_norm_w', 'L0_xattn_Wq', 'L0_xattn_bq', 'L0_xattn_Wk',
        'L0_xattn_bk', 'L0_ffn_gate_w', 'L0_ffn_up_w', 'L0_ffn_down_w', 'L0_ffn_gate_scale',
        'L0_ffn_up_scale', 'L0_ffn_down_scale']


def kernel(**inputs):
    import numpy as _np
    import concourse.bacc as _bacc
    from concourse import mybir as _mybir
    from concourse.bass_utils import run_bass_kernel_spmd as _run

    nc = _bacc.Bacc("TRN2", target_bir_lowering=False, num_devices=1)
    arrays, args = {}, []
    for name in _INS:
        a = _np.ascontiguousarray(inputs[name])
        arrays[f"in_{name}_dram"] = a
        args.append(nc.dram_tensor(f"in_{name}_dram", a.shape, _mybir.dt.from_np(a.dtype), kind="ExternalInput").ap())
    args.append(nc.dram_tensor("out_0_dram", (B, N, D), _mybir.dt.float32, kind="ExternalOutput").ap())
    build(nc, *args)
    r = _run(nc, [arrays], core_ids=[0])
    return r.results[0]["out_0_dram"]
```
